# Optimizing a Trainium2 kernel written in Bass

```python
import numpy as np
import jax
import jax.numpy as jnp

def _softmax(x, axis=-1):
    return jax.nn.softmax(x, axis=axis)

def _gelu(x):
    return jax.nn.gelu(x, approximate=True)

def _silu(x):
    return jax.nn.silu(x)

def _sigmoid(x):
    return jax.nn.sigmoid(x)

def _layernorm(x, axis=-1, eps=1e-05):
    m = jnp.mean(x, axis=axis, keepdims=True)
    v = jnp.var(x, axis=axis, keepdims=True)
    return (x - m) / jnp.sqrt(v + eps)

def _scatter_add(tgt, idx, src, axis=0):
    return tgt.at[idx].add(src)

def _segment_sum(src, seg, n):
    return jax.ops.segment_sum(src, seg, n)
kernel_name = 'mk_macaron_d4_jaxref_r8_46a4c3'

def setup_inputs(seed: int=0):
    np.random.seed(seed)
    _w = jnp.asarray

    def _L0_attn_setup():
        import jax, jax.numpy as jnp
        import numpy as np
        D_MODEL = 128
        N_STATE = 128

        def _ssm_scan(A, B_x):
            a = jnp.broadcast_to(A, B_x.shape)

            def combine(c1, c2):
                a1, b1 = c1
                a2, b2 = c2
                return (a1 * a2, a2 * b1 + b2)
            _, h = jax.lax.associative_scan(combine, (a, B_x), axis=1)
            return h
        key = jax.random.key(seed)
        k_x, k_A, k_Bw, k_Bb, k_Cw, k_Cb = jax.random.split(key, 6)
        x = jax.random.normal(k_x, (8, 256, D_MODEL), dtype=jnp.float32)
        log_A = jax.random.normal(k_A, (N_STATE,), dtype=jnp.float32) * 0.1 - 1.0
        bnd_B = 1.0 / np.sqrt(D_MODEL)
        B_w = jax.random.uniform(k_Bw, (N_STATE, D_MODEL), minval=-bnd_B, maxval=bnd_B, dtype=jnp.float32)
        B_b = jax.random.uniform(k_Bb, (N_STATE,), minval=-bnd_B, maxval=bnd_B, dtype=jnp.float32)
        bnd_C = 1.0 / np.sqrt(N_STATE)
        C_w = jax.random.uniform(k_Cw, (D_MODEL, N_STATE), minval=-bnd_C, maxval=bnd_C, dtype=jnp.float32)
        C_b = jax.random.uniform(k_Cb, (D_MODEL,), minval=-bnd_C, maxval=bnd_C, dtype=jnp.float32)
        return {'x': x, 'log_A': log_A, 'B_w': B_w, 'B_b': B_b, 'C_w': C_w, 'C_b': C_b}
    _L0_attn_in = _L0_attn_setup()

    def _L0_ffn_setup():
        import jax, jax.numpy as jnp
        import numpy as np
        B, S, DIM = (4, 512, 128)
        BASE_COUPLING = 0.1
        NUM_CYCLES = 3

        def _gelu(x):
            return jax.nn.gelu(x, approximate=False)

        def _coupling_net(h, w1, b1, w2, b2, w3, b3, w4, b4):
            h = _gelu(h @ w1 + b1)
            h = _gelu(h @ w2 + b2)
            h = _gelu(h @ w3 + b3)
            return jax.nn.sigmoid(h @ w4 + b4)

        def _global_net(h, w1, b1, w2, b2, w3, b3):
            h = _gelu(h @ w1 + b1)
            h = _gelu(h @ w2 + b2)
            return jax.nn.sigmoid(h @ w3 + b3)

        def _twist(x):
            o_r, o_i, p_r, p_i = jnp.split(x, 4, axis=-1)
            return jnp.concatenate([p_r, -p_i, -o_r, o_i], axis=-1)
        key = jax.random.key(seed)
        ks = jax.random.split(key, 9)
        d = DIM

        def w(k, fan_in, fan_out):
            return jax.random.normal(k, (fan_in, fan_out), dtype=jnp.float32) / np.sqrt(fan_in).astype(np.float32)
        inp = {'x': jax.random.normal(ks[0], (B, S, d), dtype=jnp.float32)}
        cn_dims = [(d, d), (d, d // 2), (d // 2, d // 4), (d // 4, 1)]
        for i, (a, b) in enumerate(cn_dims):
            inp[f'cn_w{i + 1}'] = w(ks[1 + i], a, b)
            inp[f'cn_b{i + 1}'] = jnp.zeros((b,), dtype=jnp.float32)
        gc_dims = [(d, d // 2), (d // 2, d // 4), (d // 4, 1)]
        for i, (a, b) in enumerate(gc_dims):
            inp[f'gc_w{i + 1}'] = w(ks[5 + i], a, b)
            inp[f'gc_b{i + 1}'] = jnp.zeros((b,), dtype=jnp.float32)
        inp['adaptive_range'] = jnp.full((1,), 0.2, dtype=jnp.float32)
        return inp
    _L0_ffn_in = _L0_ffn_setup()

    def _L1_attn_setup():
        import jax, jax.numpy as jnp
        import numpy as np
        B, T, C = (2, 256, 128)
        H = 16
        D = C // H
        ROPE_BASE = 10000.0

        def _rope_tables(seq_len, dim, dtype=jnp.float32):
            inv_freq = 1.0 / ROPE_BASE ** (jnp.arange(0, dim, 2, dtype=jnp.float32) / dim)
            t = jnp.arange(seq_len, dtype=jnp.float32)
            freqs = jnp.einsum('i,j->ij', t, inv_freq)
            emb = jnp.concatenate([freqs, freqs], axis=-1)
            return (jnp.cos(emb).astype(dtype), jnp.sin(emb).astype(dtype))

        def _rotate_half(x):
            x1, x2 = jnp.split(x, 2, axis=-1)
            return jnp.concatenate([-x2, x1], axis=-1)
        key = jax.random.key(seed)
        ks = jax.random.split(key, 9)
        s = 0.02
        return {'x': jax.random.normal(ks[0], (B, T, C), jnp.float32), 'Wq': jax.random.normal(ks[1], (C, C), jnp.float32) * s, 'bq': jax.random.normal(ks[2], (C,), jnp.float32) * s, 'Wk': jax.random.normal(ks[3], (C, C), jnp.float32) * s, 'bk': jax.random.normal(ks[4], (C,), jnp.float32) * s, 'Wv': jax.random.normal(ks[5], (C, C), jnp.float32) * s, 'bv': jax.random.normal(ks[6], (C,), jnp.float32) * s, 'Wo': jax.random.normal(ks[7], (C, C), jnp.float32) * s, 'bo': jax.random.normal(ks[8], (C,), jnp.float32) * s}
    _L1_attn_in = _L1_attn_setup()

    def _L1_ffn_setup():
        import jax, jax.numpy as jnp
        import numpy as np
        ALPHA = 2.0
        TOP_K = 2
        key = jax.random.key(seed)
        ks = jax.random.split(key, 8)
        B, S, D, H, E = (2, 256, 128, 512, 8)
        Er = E - 1
        s_in = 1.0 / np.sqrt(D)
        s_hid = 1.0 / np.sqrt(H)
        return {'x': jax.random.normal(ks[0], (B, S, D), dtype=jnp.float32), 'router_w': jax.random.normal(ks[1], (D, E), dtype=jnp.float32) * s_in, 'up_w': jax.random.normal(ks[2], (Er, D, H), dtype=jnp.float32) * s_in, 'gate_w': jax.random.normal(ks[3], (Er, D, H), dtype=jnp.float32) * s_in, 'down_w': jax.random.normal(ks[4], (Er, H, D), dtype=jnp.float32) * s_hid * 0.1, 'shared_up_w': jax.random.normal(ks[5], (D, H), dtype=jnp.float32) * s_in, 'shared_gate_w': jax.random.normal(ks[6], (D, H), dtype=jnp.float32) * s_in, 'shared_down_w': jax.random.normal(ks[7], (H, D), dtype=jnp.float32) * s_hid * 0.1}
    _L1_ffn_in = _L1_ffn_setup()

    def _L2_attn_setup():
        import jax, jax.numpy as jnp
        import numpy as np
        NUM_HEADS = 1
        LN_EPS = 1e-05
        key = jax.random.key(seed)
        ks = jax.random.split(key, 4)
        B, L, D = (8, 512, 128)
        x = jax.random.normal(ks[0], (B, L, D), dtype=jnp.float32)
        qkv_w = jax.random.normal(ks[1], (3 * D, D), dtype=jnp.float32) * np.float32(np.sqrt(1.0 / D))
        qkv_b = jnp.zeros((3 * D,), dtype=jnp.float32)
        proj_w = jax.random.normal(ks[2], (D, D), dtype=jnp.float32) * np.float32(np.sqrt(1.0 / D))
        proj_b = jnp.zeros((D,), dtype=jnp.float32)
        return {'x': x, 'norm_w': jnp.ones((D,), dtype=jnp.float32), 'norm_b': jnp.zeros((D,), dtype=jnp.float32), 'qkv_w': qkv_w, 'qkv_b': qkv_b, 'proj_w': proj_w, 'proj_b': proj_b}
    _L2_attn_in = _L2_attn_setup()

    def _L2_ffn_setup():
        import jax, jax.numpy as jnp
        import numpy as np
        D_IN, D_HID = (128, 512)

        def _ternary(key, shape):
            return jax.random.randint(key, shape, -1, 2).astype(jnp.float32)

        def _tlin(x, w, s):
            return jnp.einsum('bsi,oi->bso', x, w) * s
        key = jax.random.key(seed)
        ks = jax.random.split(key, 12)
        inv = lambda fan: 1.0 / np.sqrt(fan).astype(np.float32)
        return {'x': jax.random.normal(ks[0], (4, 256, D_IN), dtype=jnp.float32), 'w1_w': _ternary(ks[1], (D_HID, D_IN)), 'w1_s': jax.random.uniform(ks[2], (D_HID,), dtype=jnp.float32) * inv(D_IN), 'w2_w': _ternary(ks[3], (D_HID, D_IN)), 'w2_s': jax.random.uniform(ks[4], (D_HID,), dtype=jnp.float32) * inv(D_IN), 'h1_w': _ternary(ks[5], (D_HID, D_HID)), 'h1_s': jax.random.uniform(ks[6], (D_HID,), dtype=jnp.float32) * inv(D_HID), 'h2_w': _ternary(ks[7], (D_HID, D_HID)), 'h2_s': jax.random.uniform(ks[8], (D_HID,), dtype=jnp.float32) * inv(D_HID), 'w3_w': _ternary(ks[9], (D_IN, D_HID)), 'w3_s': jax.random.uniform(ks[10], (D_IN,), dtype=jnp.float32) * inv(D_HID)}
    _L2_ffn_in = _L2_ffn_setup()

    def _L3_attn_setup():
        import jax, jax.numpy as jnp
        import numpy as np
        D = 128
        H = 16
        KVH = 4
        HD = D // H
        LAT = 32
        WIN = 32
        B, S = (1, 256)
        BASE_G, BASE_L = (1000000.0, 10000.0)
        EPS = 1e-06

        def rmsnorm(x, w):
            return x * jax.lax.rsqrt(jnp.mean(x * x, axis=-1, keepdims=True) + EPS) * w

        def qk_norm(x):
            return x * jax.lax.rsqrt(jnp.mean(x * x, axis=-1, keepdims=True) + EPS)

        def rope(x, base):
            s, hd = (x.shape[-2], x.shape[-1])
            inv_freq = 1.0 / base ** (jnp.arange(0, hd, 2, dtype=jnp.float32) / hd)
            freqs = jnp.arange(s, dtype=jnp.float32)[:, None] * inv_freq[None, :]
            cos, sin = (jnp.cos(freqs), jnp.sin(freqs))
            xe, xo = (x[..., ::2], x[..., 1::2])
            out = jnp.stack([xe * cos - xo * sin, xe * sin + xo * cos], axis=-1)
            return out.reshape(x.shape)

        def split_heads(x, n_heads):
            b, s, _ = x.shape
            return x.reshape(b, s, n_heads, HD).transpose(0, 2, 1, 3)

        def repeat_kv(x):
            return jnp.repeat(x, H // KVH, axis=1)

        def sdpa(q, k, v, mask):
            scores = jnp.einsum('bhqd,bhkd->bhqk', q, k) / np.sqrt(HD).astype(np.float32)
            scores = jnp.where(mask, scores, jnp.float32(-1e+30))
            probs = jax.nn.softmax(scores, axis=-1)
            return jnp.einsum('bhqk,bhkd->bhqd', probs, v)

        def merge_heads(x):
            b, h, s, hd = x.shape
            return x.transpose(0, 2, 1, 3).reshape(b, s, h * hd)

        def global_latent_attn(x, wq, w_kv_down, w_k_up, w_v_up, wo):
            q = split_heads(x @ wq, H)
            latent = x @ w_kv_down
            k = split_heads(latent @ w_k_up, KVH)
            v = split_heads(latent @ w_v_up, KVH)
            q, k = (rope(q, BASE_G), rope(k, BASE_G))
            q, k = (qk_norm(q), qk_norm(k))
            k, v = (repeat_kv(k), repeat_kv(v))
            i = jnp.arange(x.shape[1])
            causal = i[:, None] >= i[None, :]
            return merge_heads(sdpa(q, k, v, causal)) @ wo

        def local_gqa_attn(x, wq, wk, wv, wo):
            q = split_heads(x @ wq, H)
            k = split_heads(x @ wk, KVH)
            v = split_heads(x @ wv, KVH)
            q, k = (rope(q, BASE_L), rope(k, BASE_L))
            q, k = (qk_norm(q), qk_norm(k))
            k, v = (repeat_kv(k), repeat_kv(v))
            i = jnp.arange(x.shape[1])
            diff = i[:, None] - i[None, :]
            mask = (diff >= 0) & (diff < WIN)
            return merge_heads(sdpa(q, k, v, mask)) @ wo
        key = jax.random.key(seed)
        ks = jax.random.split(key, 12)
        std = 0.02
        return {'hidden': jax.random.normal(ks[0], (B, S, D), dtype=jnp.float32), 'norm1_w': jnp.ones((D,), jnp.float32), 'norm2_w': jnp.ones((D,), jnp.float32), 'g_wq': jax.random.normal(ks[1], (D, H * HD), jnp.float32) * std, 'g_kv_down': jax.random.normal(ks[2], (D, LAT), jnp.float32) * std, 'g_k_up': jax.random.normal(ks[3], (LAT, KVH * HD), jnp.float32) * std, 'g_v_up': jax.random.normal(ks[4], (LAT, KVH * HD), jnp.float32) * std, 'g_wo': jax.random.normal(ks[5], (D, D), jnp.float32) * std, 'l_wq': jax.random.normal(ks[6], (D, H * HD), jnp.float32) * std, 'l_wk': jax.random.normal(ks[7], (D, KVH * HD), jnp.float32) * std, 'l_wv': jax.random.normal(ks[8], (D, KVH * HD), jnp.float32) * std, 'l_wo': jax.random.normal(ks[9], (D, D), jnp.float32) * std}
    _L3_attn_in = _L3_attn_setup()

    def _L3_ffn_setup():
        import jax, jax.numpy as jnp
        import numpy as np
        TOP_K = 4
        CAP_FACTOR = 4

        def swiglu(x, w1, w2, w3):
            return jax.nn.silu(x @ w1) * (x @ w3) @ w2
        key = jax.random.key(seed)
        ks = jax.random.split(key, 8)
        B, S, D, H, E = (2, 256, 128, 64, 32)
        Hs = 2 * H
        sd = lambda *sh: 1.0 / np.sqrt(sh[-2])
        x = jax.random.normal(ks[0], (B, S, D), dtype=jnp.float32)
        Wg = jax.random.normal(ks[1], (D, E), dtype=jnp.float32) * (1.0 / np.sqrt(D))
        W1 = jax.random.normal(ks[2], (E, D, H), dtype=jnp.float32) * (1.0 / np.sqrt(D))
        W3 = jax.random.normal(ks[3], (E, D, H), dtype=jnp.float32) * (1.0 / np.sqrt(D))
        W2 = jax.random.normal(ks[4], (E, H, D), dtype=jnp.float32) * (1.0 / np.sqrt(H))
        Ws1 = jax.random.normal(ks[5], (D, Hs), dtype=jnp.float32) * (1.0 / np.sqrt(D))
        Ws3 = jax.random.normal(ks[6], (D, Hs), dtype=jnp.float32) * (1.0 / np.sqrt(D))
        Ws2 = jax.random.normal(ks[7], (Hs, D), dtype=jnp.float32) * (1.0 / np.sqrt(Hs))
        return {'x': x, 'Wg': Wg, 'W1': W1, 'W2': W2, 'W3': W3, 'Ws1': Ws1, 'Ws2': Ws2, 'Ws3': Ws3}
    _L3_ffn_in = _L3_ffn_setup()
    _d = {'L0_attn_x': _L0_attn_in['x'], 'L0_attn_log_A': _L0_attn_in['log_A'], 'L0_attn_B_w': _L0_attn_in['B_w'], 'L0_attn_B_b': _L0_attn_in['B_b'], 'L0_attn_C_w': _L0_attn_in['C_w'], 'L0_attn_C_b': _L0_attn_in['C_b'], 'L0_ffn_cn_w1': _L0_ffn_in['cn_w1'], 'L0_ffn_cn_b1': _L0_ffn_in['cn_b1'], 'L0_ffn_cn_w2': _L0_ffn_in['cn_w2'], 'L0_ffn_cn_b2': _L0_ffn_in['cn_b2'], 'L0_ffn_cn_w3': _L0_ffn_in['cn_w3'], 'L0_ffn_cn_b3': _L0_ffn_in['cn_b3'], 'L0_ffn_cn_w4': _L0_ffn_in['cn_w4'], 'L0_ffn_cn_b4': _L0_ffn_in['cn_b4'], 'L0_ffn_gc_w1': _L0_ffn_in['gc_w1'], 'L0_ffn_gc_b1': _L0_ffn_in['gc_b1'], 'L0_ffn_gc_w2': _L0_ffn_in['gc_w2'], 'L0_ffn_gc_b2': _L0_ffn_in['gc_b2'], 'L0_ffn_gc_w3': _L0_ffn_in['gc_w3'], 'L0_ffn_gc_b3': _L0_ffn_in['gc_b3'], 'L0_ffn_adaptive_range': _L0_ffn_in['adaptive_range'], 'L1_attn_Wq': _L1_attn_in['Wq'], 'L1_attn_bq': _L1_attn_in['bq'], 'L1_attn_Wk': _L1_attn_in['Wk'], 'L1_attn_bk': _L1_attn_in['bk'], 'L1_attn_Wv': _L1_attn_in['Wv'], 'L1_attn_bv': _L1_attn_in['bv'], 'L1_attn_Wo': _L1_attn_in['Wo'], 'L1_attn_bo': _L1_attn_in['bo'], 'L1_ffn_router_w': _L1_ffn_in['router_w'], 'L1_ffn_up_w': _L1_ffn_in['up_w'], 'L1_ffn_gate_w': _L1_ffn_in['gate_w'], 'L1_ffn_down_w': _L1_ffn_in['down_w'], 'L1_ffn_shared_up_w': _L1_ffn_in['shared_up_w'], 'L1_ffn_shared_gate_w': _L1_ffn_in['shared_gate_w'], 'L1_ffn_shared_down_w': _L1_ffn_in['shared_down_w'], 'L2_attn_norm_w': _L2_attn_in['norm_w'], 'L2_attn_norm_b': _L2_attn_in['norm_b'], 'L2_attn_qkv_w': _L2_attn_in['qkv_w'], 'L2_attn_qkv_b': _L2_attn_in['qkv_b'], 'L2_attn_proj_w': _L2_attn_in['proj_w'], 'L2_attn_proj_b': _L2_attn_in['proj_b'], 'L2_ffn_w1_w': _L2_ffn_in['w1_w'], 'L2_ffn_w1_s': _L2_ffn_in['w1_s'], 'L2_ffn_w2_w': _L2_ffn_in['w2_w'], 'L2_ffn_w2_s': _L2_ffn_in['w2_s'], 'L2_ffn_h1_w': _L2_ffn_in['h1_w'], 'L2_ffn_h1_s': _L2_ffn_in['h1_s'], 'L2_ffn_h2_w': _L2_ffn_in['h2_w'], 'L2_ffn_h2_s': _L2_ffn_in['h2_s'], 'L2_ffn_w3_w': _L2_ffn_in['w3_w'], 'L2_ffn_w3_s': _L2_ffn_in['w3_s'], 'L3_attn_norm1_w': _L3_attn_in['norm1_w'], 'L3_attn_norm2_w': _L3_attn_in['norm2_w'], 'L3_attn_g_wq': _L3_attn_in['g_wq'], 'L3_attn_g_kv_down': _L3_attn_in['g_kv_down'], 'L3_attn_g_k_up': _L3_attn_in['g_k_up'], 'L3_attn_g_v_up': _L3_attn_in['g_v_up'], 'L3_attn_g_wo': _L3_attn_in['g_wo'], 'L3_attn_l_wq': _L3_attn_in['l_wq'], 'L3_attn_l_wk': _L3_attn_in['l_wk'], 'L3_attn_l_wv': _L3_attn_in['l_wv'], 'L3_attn_l_wo': _L3_attn_in['l_wo'], 'L3_ffn_Wg': _L3_ffn_in['Wg'], 'L3_ffn_W1': _L3_ffn_in['W1'], 'L3_ffn_W2': _L3_ffn_in['W2'], 'L3_ffn_W3': _L3_ffn_in['W3'], 'L3_ffn_Ws1': _L3_ffn_in['Ws1'], 'L3_ffn_Ws2': _L3_ffn_in['Ws2'], 'L3_ffn_Ws3': _L3_ffn_in['Ws3']}
    _x0 = _d['L0_attn_x']
    _d['L0_attn_x'] = jax.random.normal(jax.random.fold_in(jax.random.key(seed), 1), (2, 1024, 128), dtype=_x0.dtype)
    del _x0
    return _d

def reference(L0_attn_x, L0_attn_log_A, L0_attn_B_w, L0_attn_B_b, L0_attn_C_w, L0_attn_C_b, L0_ffn_cn_w1, L0_ffn_cn_b1, L0_ffn_cn_w2, L0_ffn_cn_b2, L0_ffn_cn_w3, L0_ffn_cn_b3, L0_ffn_cn_w4, L0_ffn_cn_b4, L0_ffn_gc_w1, L0_ffn_gc_b1, L0_ffn_gc_w2, L0_ffn_gc_b2, L0_ffn_gc_w3, L0_ffn_gc_b3, L0_ffn_adaptive_range, L1_attn_Wq, L1_attn_bq, L1_attn_Wk, L1_attn_bk, L1_attn_Wv, L1_attn_bv, L1_attn_Wo, L1_attn_bo, L1_ffn_router_w, L1_ffn_up_w, L1_ffn_gate_w, L1_ffn_down_w, L1_ffn_shared_up_w, L1_ffn_shared_gate_w, L1_ffn_shared_down_w, L2_attn_norm_w, L2_attn_norm_b, L2_attn_qkv_w, L2_attn_qkv_b, L2_attn_proj_w, L2_attn_proj_b, L2_ffn_w1_w, L2_ffn_w1_s, L2_ffn_w2_w, L2_ffn_w2_s, L2_ffn_h1_w, L2_ffn_h1_s, L2_ffn_h2_w, L2_ffn_h2_s, L2_ffn_w3_w, L2_ffn_w3_s, L3_attn_norm1_w, L3_attn_norm2_w, L3_attn_g_wq, L3_attn_g_kv_down, L3_attn_g_k_up, L3_attn_g_v_up, L3_attn_g_wo, L3_attn_l_wq, L3_attn_l_wk, L3_attn_l_wv, L3_attn_l_wo, L3_ffn_Wg, L3_ffn_W1, L3_ffn_W2, L3_ffn_W3, L3_ffn_Ws1, L3_ffn_Ws2, L3_ffn_Ws3):

    def _L0_attn_ref(x, log_A, B_w, B_b, C_w, C_b):
        import jax, jax.numpy as jnp
        import numpy as np
        D_MODEL = 128
        N_STATE = 128

        def _ssm_scan(A, B_x):
            a = jnp.broadcast_to(A, B_x.shape)

            def combine(c1, c2):
                a1, b1 = c1
                a2, b2 = c2
                return (a1 * a2, a2 * b1 + b2)
            _, h = jax.lax.associative_scan(combine, (a, B_x), axis=1)
            return h
        A = jax.nn.sigmoid(log_A)
        B_x = jnp.einsum('btd,nd->btn', x, B_w) + B_b
        h = _ssm_scan(A, B_x)
        y = jnp.einsum('btn,dn->btd', h, C_w) + C_b
        return y

    def _L0_ffn_ref(x, cn_w1, cn_b1, cn_w2, cn_b2, cn_w3, cn_b3, cn_w4, cn_b4, gc_w1, gc_b1, gc_w2, gc_b2, gc_w3, gc_b3, adaptive_range):
        import jax, jax.numpy as jnp
        import numpy as np
        B, S, DIM = (4, 512, 128)
        BASE_COUPLING = 0.1
        NUM_CYCLES = 3

        def _gelu(x):
            return jax.nn.gelu(x, approximate=False)

        def _coupling_net(h, w1, b1, w2, b2, w3, b3, w4, b4):
            h = _gelu(h @ w1 + b1)
            h = _gelu(h @ w2 + b2)
            h = _gelu(h @ w3 + b3)
            return jax.nn.sigmoid(h @ w4 + b4)

        def _global_net(h, w1, b1, w2, b2, w3, b3):
            h = _gelu(h @ w1 + b1)
            h = _gelu(h @ w2 + b2)
            return jax.nn.sigmoid(h @ w3 + b3)

        def _twist(x):
            o_r, o_i, p_r, p_i = jnp.split(x, 4, axis=-1)
            return jnp.concatenate([p_r, -p_i, -o_r, o_i], axis=-1)
        global_context = x.mean(axis=1, keepdims=True)
        gf = _global_net(global_context, gc_w1, gc_b1, gc_w2, gc_b2, gc_w3, gc_b3)
        out = x
        for _ in range(NUM_CYCLES):
            tf = _coupling_net(out, cn_w1, cn_b1, cn_w2, cn_b2, cn_w3, cn_b3, cn_w4, cn_b4)
            combined = 0.7 * gf + 0.3 * tf
            coupling = BASE_COUPLING + adaptive_range * (combined - 0.5) * 2.0
            out = out + coupling * _twist(out)
        return out

    def _L1_attn_ref(x, Wq, bq, Wk, bk, Wv, bv, Wo, bo):
        import jax, jax.numpy as jnp
        import numpy as np
        B, T, C = (2, 256, 128)
        H = 16
        D = C // H
        ROPE_BASE = 10000.0

        def _rope_tables(seq_len, dim, dtype=jnp.float32):
            inv_freq = 1.0 / ROPE_BASE ** (jnp.arange(0, dim, 2, dtype=jnp.float32) / dim)
            t = jnp.arange(seq_len, dtype=jnp.float32)
            freqs = jnp.einsum('i,j->ij', t, inv_freq)
            emb = jnp.concatenate([freqs, freqs], axis=-1)
            return (jnp.cos(emb).astype(dtype), jnp.sin(emb).astype(dtype))

        def _rotate_half(x):
            x1, x2 = jnp.split(x, 2, axis=-1)
            return jnp.concatenate([-x2, x1], axis=-1)
        b, t, c = x.shape
        q = x @ Wq.T + bq
        k = x @ Wk.T + bk
        v = x @ Wv.T + bv
        q = q.reshape(b, t, H, D).transpose(0, 2, 1, 3)
        k = k.reshape(b, t, H, D).transpose(0, 2, 1, 3)
        v = v.reshape(b, t, H, D).transpose(0, 2, 1, 3)
        cos, sin = _rope_tables(t, D, x.dtype)
        q = q * cos + _rotate_half(q) * sin
        k = k * cos + _rotate_half(k) * sin
        scale = 1.0 / jnp.sqrt(jnp.array(D, x.dtype))
        scores = jnp.einsum('bhqd,bhkd->bhqk', q, k) * scale
        causal = jnp.triu(jnp.full((t, t), -jnp.inf, dtype=x.dtype), k=1)
        scores = scores + causal
        attn = jax.nn.softmax(scores, axis=-1)
        out = jnp.einsum('bhqk,bhkd->bhqd', attn, v)
        out = out.transpose(0, 2, 1, 3).reshape(b, t, c)
        return out @ Wo.T + bo

    def _L1_ffn_ref(x, router_w, up_w, gate_w, down_w, shared_up_w, shared_gate_w, shared_down_w):
        import jax, jax.numpy as jnp
        import numpy as np
        ALPHA = 2.0
        TOP_K = 2
        logits = jnp.einsum('bsd,de->bse', x, router_w)
        probs = jax.nn.softmax(logits, axis=-1)
        topk_vals, topk_idx = jax.lax.top_k(probs, TOP_K)
        top1_val = topk_vals[..., 0]
        top1_idx = topk_idx[..., 0]
        hid = jnp.einsum('bsd,edh->ebsh', x, up_w) * jax.nn.silu(jnp.einsum('bsd,edh->ebsh', x, gate_w))
        Er = up_w.shape[0]
        mask = (top1_idx[None, :, :] == jnp.arange(Er)[:, None, None]).astype(x.dtype)
        routed = jnp.einsum('ebsh,ehd,ebs->bsd', hid, down_w, mask)
        shid = jnp.einsum('bsd,dh->bsh', x, shared_up_w) * jax.nn.silu(jnp.einsum('bsd,dh->bsh', x, shared_gate_w))
        shared = jnp.einsum('bsh,hd->bsd', shid, shared_down_w)
        return ALPHA * top1_val[..., None] * routed + shared

    def _L2_attn_ref(x, norm_w, norm_b, qkv_w, qkv_b, proj_w, proj_b):
        import jax, jax.numpy as jnp
        import numpy as np
        NUM_HEADS = 1
        LN_EPS = 1e-05
        B, L, D = x.shape
        H = NUM_HEADS
        mu = jnp.mean(x, axis=-1, keepdims=True)
        var = jnp.mean(jnp.square(x - mu), axis=-1, keepdims=True)
        h = (x - mu) / jnp.sqrt(var + LN_EPS) * norm_w + norm_b
        qkv = h @ qkv_w.T + qkv_b
        qkv = qkv.reshape(B * H, L // H, 3, D)
        q, k, v = (qkv[..., 0, :], qkv[..., 1, :], qkv[..., 2, :])
        scale = np.float32(1.0 / np.sqrt(L // H))
        w = jax.nn.softmax(jnp.einsum('ncq,nck->nqk', q, k * scale), axis=2)
        a = jnp.einsum('nqk,nck->ncq', w, v)
        a = a.reshape(B, L, D)
        return a @ proj_w.T + proj_b + x

    def _L2_ffn_ref(x, w1_w, w1_s, w2_w, w2_s, h1_w, h1_s, h2_w, h2_s, w3_w, w3_s):
        import jax, jax.numpy as jnp
        import numpy as np
        D_IN, D_HID = (128, 512)

        def _ternary(key, shape):
            return jax.random.randint(key, shape, -1, 2).astype(jnp.float32)

        def _tlin(x, w, s):
            return jnp.einsum('bsi,oi->bso', x, w) * s
        h = jax.nn.silu(_tlin(x, w1_w, w1_s)) * _tlin(x, w2_w, w2_s)
        h = jax.nn.gelu(_tlin(h, h1_w, h1_s), approximate=False)
        h = jax.nn.gelu(_tlin(h, h2_w, h2_s), approximate=False)
        return _tlin(h, w3_w, w3_s)

    def _L3_attn_ref(hidden, norm1_w, norm2_w, g_wq, g_kv_down, g_k_up, g_v_up, g_wo, l_wq, l_wk, l_wv, l_wo):
        import jax, jax.numpy as jnp
        import numpy as np
        D = 128
        H = 16
        KVH = 4
        HD = D // H
        LAT = 32
        WIN = 32
        B, S = (1, 256)
        BASE_G, BASE_L = (1000000.0, 10000.0)
        EPS = 1e-06

        def rmsnorm(x, w):
            return x * jax.lax.rsqrt(jnp.mean(x * x, axis=-1, keepdims=True) + EPS) * w

        def qk_norm(x):
            return x * jax.lax.rsqrt(jnp.mean(x * x, axis=-1, keepdims=True) + EPS)

        def rope(x, base):
            s, hd = (x.shape[-2], x.shape[-1])
            inv_freq = 1.0 / base ** (jnp.arange(0, hd, 2, dtype=jnp.float32) / hd)
            freqs = jnp.arange(s, dtype=jnp.float32)[:, None] * inv_freq[None, :]
            cos, sin = (jnp.cos(freqs), jnp.sin(freqs))
            xe, xo = (x[..., ::2], x[..., 1::2])
            out = jnp.stack([xe * cos - xo * sin, xe * sin + xo * cos], axis=-1)
            return out.reshape(x.shape)

        def split_heads(x, n_heads):
            b, s, _ = x.shape
            return x.reshape(b, s, n_heads, HD).transpose(0, 2, 1, 3)

        def repeat_kv(x):
            return jnp.repeat(x, H // KVH, axis=1)

        def sdpa(q, k, v, mask):
            scores = jnp.einsum('bhqd,bhkd->bhqk', q, k) / np.sqrt(HD).astype(np.float32)
            scores = jnp.where(mask, scores, jnp.float32(-1e+30))
            probs = jax.nn.softmax(scores, axis=-1)
            return jnp.einsum('bhqk,bhkd->bhqd', probs, v)

        def merge_heads(x):
            b, h, s, hd = x.shape
            return x.transpose(0, 2, 1, 3).reshape(b, s, h * hd)

        def global_latent_attn(x, wq, w_kv_down, w_k_up, w_v_up, wo):
            q = split_heads(x @ wq, H)
            latent = x @ w_kv_down
            k = split_heads(latent @ w_k_up, KVH)
            v = split_heads(latent @ w_v_up, KVH)
            q, k = (rope(q, BASE_G), rope(k, BASE_G))
            q, k = (qk_norm(q), qk_norm(k))
            k, v = (repeat_kv(k), repeat_kv(v))
            i = jnp.arange(x.shape[1])
            causal = i[:, None] >= i[None, :]
            return merge_heads(sdpa(q, k, v, causal)) @ wo

        def local_gqa_attn(x, wq, wk, wv, wo):
            q = split_heads(x @ wq, H)
            k = split_heads(x @ wk, KVH)
            v = split_heads(x @ wv, KVH)
            q, k = (rope(q, BASE_L), rope(k, BASE_L))
            q, k = (qk_norm(q), qk_norm(k))
            k, v = (repeat_kv(k), repeat_kv(v))
            i = jnp.arange(x.shape[1])
            diff = i[:, None] - i[None, :]
            mask = (diff >= 0) & (diff < WIN)
            return merge_heads(sdpa(q, k, v, mask)) @ wo
        x = hidden
        x = x + global_latent_attn(rmsnorm(x, norm1_w), g_wq, g_kv_down, g_k_up, g_v_up, g_wo)
        x = x + local_gqa_attn(rmsnorm(x, norm2_w), l_wq, l_wk, l_wv, l_wo)
        return x

    def _L3_ffn_ref(x, Wg, W1, W2, W3, Ws1, Ws2, Ws3):
        import jax, jax.numpy as jnp
        import numpy as np
        TOP_K = 4
        CAP_FACTOR = 4

        def swiglu(x, w1, w2, w3):
            return jax.nn.silu(x @ w1) * (x @ w3) @ w2
        B, S, D = x.shape
        E = Wg.shape[1]
        T = B * S
        xf = x.reshape(T, D)
        scores = jax.nn.softmax(xf @ Wg, axis=-1)
        weights, indices = jax.lax.top_k(scores, TOP_K)
        P = T * TOP_K
        pair_expert = indices.reshape(-1)
        pair_token = jnp.repeat(jnp.arange(T), TOP_K)
        pair_weight = weights.reshape(-1).astype(xf.dtype)
        C = CAP_FACTOR * P // E
        y = jnp.zeros_like(xf)
        for e in range(E):
            pos = jnp.nonzero(pair_expert == e, size=C, fill_value=P)[0]
            valid = pos < P
            safe = jnp.minimum(pos, P - 1)
            tok = jnp.where(valid, pair_token[safe], 0)
            w = jnp.where(valid, pair_weight[safe], 0.0)
            xg = xf[tok]
            out = swiglu(xg, W1[e], W2[e], W3[e]) * w[:, None]
            y = y.at[tok].add(out)
        z = swiglu(xf, Ws1, Ws2, Ws3)
        return (y + z).reshape(B, S, D)
    x = L0_attn_x
    x = x + 0.5 * _L0_ffn_ref(_layernorm(x, axis=-1), L0_ffn_cn_w1, L0_ffn_cn_b1, L0_ffn_cn_w2, L0_ffn_cn_b2, L0_ffn_cn_w3, L0_ffn_cn_b3, L0_ffn_cn_w4, L0_ffn_cn_b4, L0_ffn_gc_w1, L0_ffn_gc_b1, L0_ffn_gc_w2, L0_ffn_gc_b2, L0_ffn_gc_w3, L0_ffn_gc_b3, L0_ffn_adaptive_range)
    x = x + _L0_attn_ref(_layernorm(x, axis=-1), L0_attn_log_A, L0_attn_B_w, L0_attn_B_b, L0_attn_C_w, L0_attn_C_b)
    x = x + 0.5 * _L0_ffn_ref(_layernorm(x, axis=-1), L0_ffn_cn_w1, L0_ffn_cn_b1, L0_ffn_cn_w2, L0_ffn_cn_b2, L0_ffn_cn_w3, L0_ffn_cn_b3, L0_ffn_cn_w4, L0_ffn_cn_b4, L0_ffn_gc_w1, L0_ffn_gc_b1, L0_ffn_gc_w2, L0_ffn_gc_b2, L0_ffn_gc_w3, L0_ffn_gc_b3, L0_ffn_adaptive_range)
    x = x + 0.5 * _L1_ffn_ref(_layernorm(x, axis=-1), L1_ffn_router_w, L1_ffn_up_w, L1_ffn_gate_w, L1_ffn_down_w, L1_ffn_shared_up_w, L1_ffn_shared_gate_w, L1_ffn_shared_down_w)
    x = x + _L1_attn_ref(_layernorm(x, axis=-1), L1_attn_Wq, L1_attn_bq, L1_attn_Wk, L1_attn_bk, L1_attn_Wv, L1_attn_bv, L1_attn_Wo, L1_attn_bo)
    x = x + 0.5 * _L1_ffn_ref(_layernorm(x, axis=-1), L1_ffn_router_w, L1_ffn_up_w, L1_ffn_gate_w, L1_ffn_down_w, L1_ffn_shared_up_w, L1_ffn_shared_gate_w, L1_ffn_shared_down_w)
    x = x + 0.5 * _L2_ffn_ref(_layernorm(x, axis=-1), L2_ffn_w1_w, L2_ffn_w1_s, L2_ffn_w2_w, L2_ffn_w2_s, L2_ffn_h1_w, L2_ffn_h1_s, L2_ffn_h2_w, L2_ffn_h2_s, L2_ffn_w3_w, L2_ffn_w3_s)
    x = x + _L2_attn_ref(_layernorm(x, axis=-1), L2_attn_norm_w, L2_attn_norm_b, L2_attn_qkv_w, L2_attn_qkv_b, L2_attn_proj_w, L2_attn_proj_b)
    x = x + 0.5 * _L2_ffn_ref(_layernorm(x, axis=-1), L2_ffn_w1_w, L2_ffn_w1_s, L2_ffn_w2_w, L2_ffn_w2_s, L2_ffn_h1_w, L2_ffn_h1_s, L2_ffn_h2_w, L2_ffn_h2_s, L2_ffn_w3_w, L2_ffn_w3_s)
    x = x + 0.5 * _L3_ffn_ref(_layernorm(x, axis=-1), L3_ffn_Wg, L3_ffn_W1, L3_ffn_W2, L3_ffn_W3, L3_ffn_Ws1, L3_ffn_Ws2, L3_ffn_Ws3)
    x = x + _L3_attn_ref(_layernorm(x, axis=-1), L3_attn_norm1_w, L3_attn_norm2_w, L3_attn_g_wq, L3_attn_g_kv_down, L3_attn_g_k_up, L3_attn_g_v_up, L3_attn_g_wo, L3_attn_l_wq, L3_attn_l_wk, L3_attn_l_wv, L3_attn_l_wo)
    x = x + 0.5 * _L3_ffn_ref(_layernorm(x, axis=-1), L3_ffn_Wg, L3_ffn_W1, L3_ffn_W2, L3_ffn_W3, L3_ffn_Ws1, L3_ffn_Ws2, L3_ffn_Ws3)
    return x

_drawn_inputs = setup_inputs


def setup_inputs(seed=0):
    import zlib

    import numpy as np

    out = dict(_drawn_inputs(seed))
    spreads = {'L0_ffn_cn_b1': (0.0, 0.1),
     'L0_ffn_cn_b2': (0.0, 0.1),
     'L0_ffn_cn_b3': (0.0, 0.1),
     'L0_ffn_gc_b1': (0.0, 0.1),
     'L0_ffn_gc_b2': (0.0, 0.1),
     'L2_attn_norm_w': (1.0, 0.2),
     'L2_attn_norm_b': (0.0, 0.1),
     'L2_attn_qkv_b': (0.0, 0.1),
     'L2_attn_proj_b': (0.0, 0.1),
     'L3_attn_norm1_w': (1.0, 0.2),
     'L3_attn_norm2_w': (1.0, 0.2)}
    factors = {}
    for name, (base, spread) in spreads.items():
        noise = np.random.default_rng([zlib.crc32(name.encode()), seed]).standard_normal(out[name].shape)
        drawn = base * np.exp(spread * noise) if base else spread * noise
        out[name] = jnp.asarray(drawn.astype(out[name].dtype))
    for name, factor in factors.items():
        out[name] = (out[name] * factor).astype(out[name].dtype)
    return out
```

```python
from contextlib import ExitStack

import numpy as np

import concourse.bass as bass
from concourse import mybir

ALU = mybir.AluOpType
ACT = mybir.ActivationFunctionType
AX = mybir.AxisListType
F32 = mybir.dt.float32
BF16 = mybir.dt.bfloat16
U16 = mybir.dt.uint16
I32 = mybir.dt.int32

P = 128
D = 128
NB, T = 2, 1024
N = NB * T
NT = N // P
CH = 512
NC = N // CH
TPC = CH // P
LN_EPS = 1e-5


def columns(widths):
    at, out = 0, {}
    for name, w in widths:
        out[name] = (at, w)
        at += w
    return out, at


L0_COLS, L0_W = columns([
    ("cn_w1", 128), ("cn_w2", 64), ("cn_w3", 128), ("cn_w4", 128), ("gc_w1", 64), ("gc_w2", 32), ("gc_w3", 128),
    ("cn_b1", 1), ("cn_b2", 1), ("cn_b3", 1), ("cn_b4", 1), ("gc_b1", 1), ("gc_b2", 1), ("gc_b3", 1),
    ("range", 1), ("B_wT", 128), ("C_wT", 128), ("C_b", 128), ("log_A", 1), ("B_b", 1)])
L1_COLS, L1_W = columns([
    ("qk", 512), ("v", 128), ("qk_b", 512), ("v_b", 128), ("o", 128), ("o_b", 128), ("ones", 128), ("cos", 64), ("sin", 64)])
MASK_COLS, MASK_W = columns([("ident", 128), ("future_key", 128), ("past_query", 128), ("band", 160)])
L2A_COLS, L2A_W = columns([
    ("qkT", 256), ("vT", 128), ("projT", 128), ("qk_b", 256), ("proj_b", 128), ("ones", 128), ("v_b", 1), ("norm_w", 1), ("norm_b", 1)])
L3_COLS, L3_W = columns([
    ("router", 32), ("g_q", 128), ("g_qr", 128), ("g_down", 32), ("g_k", 32), ("g_krv", 64), ("g_o", 128), ("l_qkv", 352), ("l_o", 128),
    ("gcos", 64), ("gsin", 64), ("lcos", 64), ("lsin", 64), ("norm1", 1), ("norm2", 1)])
L2_COLS, L2_W = columns([
    ("w1T", 512), ("w2T", 512), ("h1T", 2048), ("h2T", 2048), ("w3T", 512), ("s3", 128), ("s1", 4), ("s2", 4), ("sh1", 4), ("sh2", 4)])
CONST_COLS, CONST_W = columns([("ident", 128), ("twist", 128), ("first8", 8), ("earlier", 128), ("ones", 128), ("block_start", NT + 8)])


class Steps:

    def __init__(self, eng, sem):
        self.eng, self.sem, self.n = eng, sem, 0

    def did(self, ins):
        ins.then_inc(self.sem, 1)
        self.n += 1
        return self.n

    def after(self, n):
        self.eng.wait_ge(self.sem, n)

    def chain(self, ins):
        self.after(self.did(ins))


class Core:

    def __init__(self, nc, ctx):
        self.nc, self.ctx = nc, ctx
        self.stage_sems = []
        self.x = self.sb(ctx, "x", [P, NT, D])
        self.xn = self.sb(ctx, "xn", [P, NT, D])
        self.xnT = self.sb(ctx, "xnT", [P, N])
        self.stats = self.sb(ctx, "stats", [P, NT, 6])
        self.meanvar = self.sb(ctx, "meanvar", [P, NT, 2])
        self.rstd = self.sb(ctx, "rstd", [P, NT])
        self.mhalf = self.sb(ctx, "mhalf", [P, NT])
        self.const = self.sb(ctx, "const", [P, CONST_W])
        self.psum = ctx.enter_context(nc.psum_tensor("psum", [P, 8, CH], F32))

    def sb(self, ctx, name, shape, dt=F32):
        return ctx.enter_context(self.nc.sbuf_tensor(name, shape, dt))

    def weight_sem(self, ctx, name):
        s = ctx.enter_context(self.nc.semaphore(name))
        self.first_stage_sem = s.num + 1
        return s

    def sem(self, ctx, name):
        s = self.nc.alloc_semaphore(name, num=self.first_stage_sem + len(self.stage_sems))
        self.stage_sems.append(s)
        return s

    def block(self, ctx):
        sems, self.stage_sems = self.stage_sems, []

        def close():
            self.nc.all_engine_barrier(sems_to_clear=range(sems[0].num, sems[-1].num + 1))
            for s in sems:
                self.nc.release_semaphore(s)

        ctx.callback(close)
        return ctx.enter_context(self.nc.Block())

    def c(self, name):
        a, w = CONST_COLS[name]
        return self.const[:, a:a + w]


class LayerNorm:

    BANKS = (6, 7)

    def __init__(self, core, ctx, tag):
        self.k = core
        self.var_ready = core.sem(ctx, tag + "var_ready")
        self.eps_added = core.sem(ctx, tag + "eps_added")
        self.rstd_ready = core.sem(ctx, tag + "rstd_ready")
        self.stat_step = core.sem(ctx, tag + "stat_step")
        self.xn_ready = core.sem(ctx, tag + "xn_ready")
        self.turned = core.sem(ctx, tag + "turned")
        self.xnT_ready = core.sem(ctx, tag + "xnT_ready")

    def vector(self, v):
        k = self.k

        def statistics(c):
            tiles = range(TPC * c, TPC * (c + 1))
            for t in tiles:
                v.bn_stats(k.stats[:, t, :], k.x[:, t, :]).then_inc(self.stat_step, 1)
            for t in tiles:
                v.wait_ge(self.stat_step, t + 1)
                ins = v.bn_aggr(k.meanvar[:, t, :], k.stats[:, t, :])
                ins.then_inc(self.var_ready, 1)

        def normalise(c):
            v.wait_ge(self.var_ready, TPC * (c + 1))
            v.wait_ge(self.rstd_ready, c + 1)
            for t in range(TPC * c, TPC * (c + 1)):
                v.tensor_scalar(k.xn[:, t, :], k.x[:, t, :], k.meanvar[:, t, 0:1], k.rstd[:, t:t + 1],
                                ALU.subtract, ALU.mult).then_inc(self.xn_ready, 1)

        statistics(0)
        for c in range(NC):
            if c + 1 < NC:
                statistics(c + 1)
            normalise(c)

    def pool(self, g):
        k = self.k
        for c in range(NC):
            a, b = TPC * c, TPC * (c + 1)
            g.wait_ge(self.var_ready, b)
            g.tensor_scalar(k.rstd[:, a:b], k.meanvar[:, a:b, 1], LN_EPS, None, ALU.add).then_inc(self.eps_added, 1)
            g.wait_ge(self.eps_added, c + 1)
            g.tensor_tensor(k.rstd[:, a:b], k.rstd[:, a:b], k.mhalf[:, a:b], ALU.pow).then_inc(self.rstd_ready, 1)

    def tensor(self, pe, c):
        k = self.k
        if c >= 2:
            pe.wait_ge(self.xnT_ready, c - 1)
        for t in range(TPC):
            pe.wait_ge(self.xn_ready, TPC * c + t + 1)
            ins = pe.transpose(k.psum[:, self.BANKS[c % 2], t * P:(t + 1) * P], k.xn[:, TPC * c + t, :], k.c("ident"))
        ins.then_inc(self.turned, 1)

    def scalar(self, act, c):
        k = self.k
        act.wait_ge(self.turned, c + 1)
        act.activation(k.xnT[:, c * CH:(c + 1) * CH], k.psum[:, self.BANKS[c % 2], :], ACT.Copy).then_inc(self.xnT_ready, 1)


def load_stage(core, dram, loads, sorted_x):
    nc = core.nc
    with ExitStack() as ctx:
        K = sorted_x.shape[0] // P
        zero = core.sb(ctx, "zero", [P, K, D])
        x_in = core.sem(ctx, "x_in")
        mhalf_set = core.sem(ctx, "mhalf_set")
        zero_set = core.sem(ctx, "zero_set")
        cleared = core.sem(ctx, "cleared")
        block = core.block(ctx)

        @block.sync
        def _(sp):
            sp.dma_start(core.x[:, :, :], dram["x"].rearrange("(t p) d -> p t d", p=P)).then_inc(x_in, 16)
            sp.dma_start(core.const[:, :], dram["const"]).then_inc(x_in, 16)
            sp.wait_ge(zero_set, 1)
            sp.dma_start(sorted_x.rearrange("(k p) d -> p k d", p=P), zero[:, :, :]).then_inc(cleared, 16)
            sp.wait_ge(x_in, 32)
            sp.wait_ge(cleared, 16)

        @block.scalar
        def _(act):
            for tile, name, sem in loads:
                act.dma_start(tile, dram[name]).then_inc(sem, 16)

        @block.vector
        def _(v):
            v.memset(zero[:, :, :], 0.0).then_inc(zero_set, 1)

        @block.gpsimd
        def _(g):
            g.memset(core.mhalf[:, :], -0.5).then_inc(mhalf_set, 1)
            g.wait_ge(mhalf_set, 1)


def coupling_stage(core, w0, w0_in, tag):
    nc = core.nc
    CYCLES, LAYERS = 3, 5
    SUMS = 1.0 / T

    def w(name, rows=P):
        a, n = L0_COLS[name]
        return w0[0:rows, a:a + n]

    with ExitStack() as ctx:
        ln = LayerNorm(core, ctx, tag)
        hid = [core.sb(ctx, f"{tag}hid{i}", [r, NC, CH]) for i, r in enumerate((128, 64, 128))]
        gate = core.sb(ctx, tag + "gate", [P, NC, CH])
        prod = core.sb(ctx, tag + "prod", [P, NC, CH])
        ctx_sum = core.sb(ctx, tag + "ctx_sum", [P, NB])
        g1 = core.sb(ctx, tag + "g1", [64, NB])
        g2 = core.sb(ctx, tag + "g2", [32, NB])
        gth = core.sb(ctx, tag + "gth", [P, NB])
        half_b = core.sb(ctx, tag + "half_b", [P, 2])
        slope = core.sb(ctx, tag + "slope", [P, 2])
        shift = core.sb(ctx, tag + "shift", [P, NB])
        sum_ready = core.sem(ctx, tag + "sum_ready")
        ctx_pe = core.sem(ctx, tag + "ctx_pe")
        ctx_act = core.sem(ctx, tag + "ctx_act")
        dve_step = core.sem(ctx, tag + "dve_step")
        half_ready = core.sem(ctx, tag + "half_ready")
        shift_ready = core.sem(ctx, tag + "shift_ready")
        pe_out = core.sem(ctx, tag + "pe_out")
        hid_ready = core.sem(ctx, tag + "hid_ready")
        gate_ready = core.sem(ctx, tag + "gate_ready")
        prod_ready = core.sem(ctx, tag + "prod_ready")
        out_ready = core.sem(ctx, tag + "out_ready")
        back = core.sem(ctx, tag + "back")
        block = core.block(ctx)

        def out(c):
            return core.xnT[:, c * CH:(c + 1) * CH]

        def bank(layer, c, odd):
            return core.psum[:, 4 * ((layer + odd) % 2) + c, :]

        @block.gpsimd
        def _(g):
            ln.pool(g)

        @block.vector
        def _(v):
            s = Steps(v, dve_step)
            v.wait_ge(w0_in, 16)
            v.tensor_scalar(half_b[:, 0:1], w("cn_b4"), 0.5, None, ALU.mult).then_inc(half_ready, 1)
            v.tensor_scalar(half_b[:, 1:2], w("gc_b3"), 0.5, None, ALU.mult).then_inc(half_ready, 1)
            s.did(v.tensor_scalar(slope[:, 0:1], w("range"), 0.3, None, ALU.mult))
            s.did(v.tensor_scalar(slope[:, 1:2], w("range"), 0.7, None, ALU.mult))
            ln.vector(v)
            for b in range(NB):
                v.wait_ge(ln.xnT_ready, NC // NB * (b + 1))
                v.tensor_reduce(ctx_sum[:, b:b + 1], core.xnT[:, b * T:(b + 1) * T], AX.X, ALU.add).then_inc(sum_ready, 1)
            v.wait_ge(ctx_act, 3)
            s.after(2)
            s.chain(v.tensor_scalar(shift[:, :], gth[:, :], slope[:, 1:2], None, ALU.mult))
            v.tensor_scalar(shift[:, :], shift[:, :], 0.1, None, ALU.add).then_inc(shift_ready, 1)
            v.sem_inc(out_ready, 1)
            with v.Fori(0, CYCLES) as cyc:
                for c in range(NC):
                    v.wait_ge(gate_ready, cyc * 8 + 4 + c + 1)
                    v.wait_ge(pe_out, cyc * (LAYERS * NC) + 4 * NC + c + 1)
                    v.tensor_tensor(prod[:, c, :], gate[:, c, :], core.psum[:, c, :], ALU.mult).then_inc(prod_ready, 1)
                for c in range(NC):
                    v.wait_ge(prod_ready, cyc * NC + c + 1)
                    v.wait_ge(out_ready, cyc * NC + c + 1)
                    v.tensor_tensor(out(c), out(c), prod[:, c, :], ALU.add).then_inc(out_ready, 1)
            for c in range(NC):
                v.wait_ge(back, c + 1)
                xs = core.x[:, TPC * c:TPC * (c + 1), :].rearrange("p t d -> p (t d)")
                s.did(v.scalar_tensor_tensor(xs, core.psum[:, 4 + c, :], 0.5, xs, ALU.mult, ALU.add))

        @block.tensor
        def _(pe):
            pe.wait_ge(w0_in, 16)
            for c in range(NC):
                ln.tensor(pe, c)
            pe.wait_ge(sum_ready, NB)
            pe.matmul(core.psum[0:64, 0, 0:NB], w("gc_w1"), ctx_sum[:, :], start=True, stop=True).then_inc(ctx_pe, 1)
            pe.wait_ge(ctx_act, 1)
            pe.matmul(core.psum[0:32, 1, 0:NB], w("gc_w2", 64), g1[:, :], start=True, stop=True).then_inc(ctx_pe, 1)
            pe.wait_ge(ctx_act, 2)
            pe.matmul(core.psum[:, 2, 0:NB], w("gc_w3", 32), g2[:, :], start=True, stop=True).then_inc(ctx_pe, 1)
            pe.wait_ge(ctx_act, 3)
            pe.wait_ge(ln.xnT_ready, NC)
            with pe.Fori(0, CYCLES) as cyc:
                pe.wait_ge(out_ready, cyc * NC + 1)
                for c in range(NC):
                    pe.matmul(core.psum[:, 4 + c, :], w("cn_w1"), out(c), start=True, stop=True).then_inc(pe_out, 1)
                for layer, name, rows, cols in ((1, "cn_w2", 128, 64), (2, "cn_w3", 64, 128), (3, "cn_w4", 128, 128)):
                    for c in range(NC):
                        pe.wait_ge(hid_ready, cyc * (3 * NC) + (layer - 1) * NC + c + 1)
                        pe.matmul(core.psum[0:cols, 4 * ((layer + 1) % 2) + c, :], w(name, rows), hid[layer - 1][:, c, :],
                                  start=True, stop=True).then_inc(pe_out, 1)
                for c in range(NC):
                    pe.wait_ge(gate_ready, cyc * 8 + c + 1)
                    pe.matmul(core.psum[:, c, :], core.c("twist"), out(c), start=True, stop=True).then_inc(pe_out, 1)
            for c in range(NC):
                pe.wait_ge(out_ready, CYCLES * NC + 1)
                for t in range(TPC):
                    ins = pe.transpose(core.psum[:, 4 + c, t * P:(t + 1) * P], core.xnT[:, c * CH + t * P:c * CH + (t + 1) * P],
                                       core.c("ident"))
                ins.then_inc(back, 1)

        @block.scalar
        def _(act):
            act.wait_ge(w0_in, 16)
            for c in range(NC):
                ln.scalar(act, c)
            act.wait_ge(ctx_pe, 1)
            act.activation(g1[:, :], core.psum[0:64, 0, 0:NB], ACT.Gelu, bias=w("gc_b1", 64), scale=SUMS).then_inc(ctx_act, 1)
            act.wait_ge(ctx_pe, 2)
            act.activation(g2[:, :], core.psum[0:32, 1, 0:NB], ACT.Gelu, bias=w("gc_b2", 32)).then_inc(ctx_act, 1)
            act.wait_ge(ctx_pe, 3)
            act.wait_ge(half_ready, 2)
            act.activation(gth[:, :], core.psum[:, 2, 0:NB], ACT.Tanh, bias=half_b[:, 1:2], scale=0.5).then_inc(ctx_act, 1)
            act.wait_ge(shift_ready, 1)
            with act.Fori(0, CYCLES) as cyc:
                for layer, rows, bias in ((0, 128, "cn_b1"), (1, 64, "cn_b2"), (2, 128, "cn_b3")):
                    for c in range(NC):
                        act.wait_ge(pe_out, cyc * (LAYERS * NC) + layer * NC + c + 1)
                        act.activation(hid[layer][:, c, :], core.psum[0:rows, 4 * ((layer + 1) % 2) + c, :], ACT.Gelu,
                                       bias=w(bias, rows)).then_inc(hid_ready, 1)
                act.wait_ge(out_ready, cyc * NC + 1)
                for c in range(NC):
                    act.wait_ge(pe_out, cyc * (LAYERS * NC) + 3 * NC + c + 1)
                    act.activation(gate[:, c, :], core.psum[:, c, :], ACT.Tanh, bias=half_b[:, 0:1], scale=0.5).then_inc(gate_ready, 1)
                for c in range(NC):
                    act.wait_ge(gate_ready, cyc * 8 + c + 1)
                    b = c // (NC // NB)
                    act.activation(gate[:, c, :], gate[:, c, :], ACT.Identity, bias=shift[:, b:b + 1],
                                   scale=slope[:, 0:1]).then_inc(gate_ready, 1)


def scan_stage(core, w0, tag):
    nc = core.nc
    CPB = T // CH

    def w(name, rows=P):
        a, n = L0_COLS[name]
        return w0[0:rows, a:a + n]

    with ExitStack() as ctx:
        ln = LayerNorm(core, ctx, tag)
        decay = core.sb(ctx, tag + "decay", [P, 1])
        decays = core.sb(ctx, tag + "decays", [P, CH])
        bx = core.sb(ctx, tag + "bx", [P, NC, CH])
        h = core.sb(ctx, tag + "h", [P, N])
        yb = core.sb(ctx, tag + "yb", [P, NC, TPC, D])
        decay_ready = core.sem(ctx, tag + "decay_ready")
        dve_step = core.sem(ctx, tag + "dve_step")
        bx_pe = core.sem(ctx, tag + "bx_pe")
        bx_ready = core.sem(ctx, tag + "bx_ready")
        h_ready = core.sem(ctx, tag + "h_ready")
        y_pe = core.sem(ctx, tag + "y_pe")
        block = core.block(ctx)

        @block.gpsimd
        def _(g):
            ln.pool(g)

        @block.scalar
        def _(act):
            act.activation(decay[:, :], w("log_A"), ACT.Sigmoid).then_inc(decay_ready, 1)
            for c in range(NC):
                ln.scalar(act, c)
                act.wait_ge(bx_pe, c + 1)
                act.activation(bx[:, c, :], core.psum[:, c, :], ACT.Identity, bias=w("B_b")).then_inc(bx_ready, 1)

        @block.tensor
        def _(pe):
            def outputs(c):
                pe.wait_ge(h_ready, c + 1)
                for t in range(TPC):
                    ins = pe.matmul(core.psum[:, 4 + c % 2, t * P:(t + 1) * P], h[:, c * CH + t * P:c * CH + (t + 1) * P],
                                    w("C_wT"), start=True, stop=True)
                ins.then_inc(y_pe, 1)

            for c in range(NC):
                ln.tensor(pe, c)
                pe.wait_ge(ln.xnT_ready, c + 1)
                pe.matmul(core.psum[:, c, :], w("B_wT"), core.xnT[:, c * CH:(c + 1) * CH], start=True, stop=True).then_inc(bx_pe, 1)
            for c in range(NC):
                if c >= 2:
                    pe.wait_ge(dve_step, 2 + 2 * (c - 1))
                outputs(c)

        @block.vector
        def _(v):
            s = Steps(v, dve_step)
            ln.vector(v)
            s.chain(v.memset(decays[:, :], 1.0))
            v.wait_ge(decay_ready, 1)
            s.chain(v.tensor_scalar(decays[:, :], decays[:, :], decay[:, 0:1], None, ALU.mult))
            for c in range(NC):
                v.wait_ge(bx_ready, c + 1)
                if c % CPB:
                    v.wait_ge(h_ready, c)
                first = h[:, c * CH - 1:c * CH] if c % CPB else 0.0
                v.tensor_tensor_scan(h[:, c * CH:(c + 1) * CH], decays[:, :], bx[:, c, :], first, ALU.mult, ALU.add).then_inc(h_ready, 1)
            cb = w("C_b").unsqueeze(1).broadcast_to([P, TPC, D])
            for c in range(NC):
                v.wait_ge(y_pe, c + 1)
                s.chain(v.tensor_tensor(yb[:, c, :, :], core.psum[:, 4 + c % 2, :].rearrange("p (t d) -> p t d", d=D), cb, ALU.add))
                xs = core.x[:, TPC * c:TPC * (c + 1), :]
                s.did(v.tensor_tensor(xs, xs, yb[:, c, :, :], ALU.add))


def top1_stage(core, w1, w1_in, dram_experts, sorted_x, sorted_y, scattered, gathered, call, tag):
    nc = core.nc
    E, HT = 8, 4
    H = HT * P
    GATE_AT, UP_AT, DOWN_AT = 0, H, 2 * H
    BLOCKS = (N + (E - 1) * (P - 1)) // P
    HALF = NC // 2
    HID0, DOWN0 = HALF * HT, HALF
    HID1, DOWN1 = HID0 + BLOCKS, DOWN0 + BLOCKS
    GATE, UP, DOWN, TURN, HIDT = (0, 1), (2, 3), (4, 5), 6, 7
    LOGITS, RANKS = 6, 7
    ROUND = float(2 ** 23)

    with ExitStack() as ctx:
        ln = LayerNorm(core, ctx, tag)
        logit = core.sb(ctx, tag + "logit", [P, NT, E])
        prob = core.sb(ctx, tag + "prob", [P, NT, E])
        first = core.sb(ctx, tag + "first", [P, NT, E])
        chosen = core.sb(ctx, tag + "chosen", [P, E, NT])
        most = core.sb(ctx, tag + "most", [P, NT])
        total = core.sb(ctx, tag + "total", [P, NT])
        coef = core.sb(ctx, tag + "coef", [P, NT])
        count = core.sb(ctx, tag + "count", [P, E])
        whole = core.sb(ctx, tag + "whole", [P, E])
        taken = core.sb(ctx, tag + "taken", [P, E, NT])
        ends = core.sb(ctx, tag + "ends", [P, E, NT])
        place = core.sb(ctx, tag + "place", [P, NT])
        place_in = core.sb(ctx, tag + "place_in", [P, NT], I32)
        place_out = core.sb(ctx, tag + "place_out", [P, NT], I32)
        passed = core.sb(ctx, tag + "passed", [P, E - 1, BLOCKS])
        owner = core.sb(ctx, tag + "owner", [P, BLOCKS])
        table = core.sb(ctx, tag + "table", [P, BLOCKS], I32)
        experts = core.sb(ctx, tag + "experts", [P, E - 1, 3 * H])
        shared = core.sb(ctx, tag + "shared", [P, 3 * H])
        rows = [core.sb(ctx, f"{tag}rows{odd}", [P, D]) for odd in range(2)]
        routed = core.sb(ctx, tag + "routed", [P, NT, D])
        rowsT = core.sb(ctx, tag + "rowsT", [P, 2, P])
        silu = core.sb(ctx, tag + "silu", [P, 2, CH])
        hid = core.sb(ctx, tag + "hid", [P, 2, HT, CH])
        block_hid = core.sb(ctx, tag + "block_hid", [P, 2, H])
        block_hidT = core.sb(ctx, tag + "block_hidT", [P, 2, H])
        outs = core.sb(ctx, tag + "outs", [P, BLOCKS, D])
        logits_pe = core.sem(ctx, tag + "logits_pe")
        dve_step = core.sem(ctx, tag + "dve_step")
        shifted = core.sem(ctx, tag + "shifted")
        exps = core.sem(ctx, tag + "exps")
        chosen_ready = core.sem(ctx, tag + "chosen_ready")
        ranks_pe = core.sem(ctx, tag + "ranks_pe")
        place_ready = core.sem(ctx, tag + "place_ready")
        table_ready = core.sem(ctx, tag + "table_ready")
        rows_in = [core.sem(ctx, f"{tag}rows_in{odd}") for odd in range(2)]
        shared_in = core.sem(ctx, tag + "shared_in")
        experts_in = core.sem(ctx, tag + "experts_in")
        turn_pe = core.sem(ctx, tag + "turn_pe")
        rowsT_ready = core.sem(ctx, tag + "rowsT_ready")
        gate_pe = core.sem(ctx, tag + "gate_pe")
        up_pe = core.sem(ctx, tag + "up_pe")
        silu_ready = core.sem(ctx, tag + "silu_ready")
        hid_ready = core.sem(ctx, tag + "hid_ready")
        hidT_pe = core.sem(ctx, tag + "hidT_pe")
        hidT_ready = core.sem(ctx, tag + "hidT_ready")
        down_pe = core.sem(ctx, tag + "down_pe")
        out_read = core.sem(ctx, tag + "out_read")
        spilled = core.sem(ctx, tag + "spilled")
        block = core.block(ctx)

        def reach(eng, sem, count):
            if not isinstance(count, int) or count > 0:
                eng.wait_ge(sem, count)

        def blocks(eng, step):
            for odd in (0, 1):
                step(0, odd, range(0, odd + 1))
            with eng.Fori(1, BLOCKS // 2) as pair:
                for odd in (0, 1):
                    step(pair, odd, range(0, 3))
            for odd in (0, 1):
                step(BLOCKS // 2, odd, range(1 + odd, 3))

        @block.sync
        def _(sp):
            sp.dma_start(shared[:, :], dram_experts[E - 1].rearrange("p j d -> p (j d)")).then_inc(shared_in, 16)
            for e in range(E - 1):
                sp.dma_start(experts[:, e, :], dram_experts[e].rearrange("p j d -> p (j d)")).then_inc(experts_in, 16)
            sp.wait_ge(scattered, 16 * NT * (call + 1))
            blocks_x, blocks_y = (z.rearrange("(k p) d -> p k d", p=P) for z in (sorted_x, sorted_y))

            def load(pair, odd):
                reach(sp, turn_pe, pair * 2 + odd - 1)
                src = blocks_x[:, bass.ds(pair * 2 + odd, 1), :].rearrange("p o d -> p (o d)")
                sp.dma_start(rows[odd][:, :], src).then_inc(rows_in[odd], 16)

            def spill(pair):
                sp.wait_ge(out_read, pair * 2 + DOWN0 + 2)
                sp.dma_start(blocks_y[:, bass.ds(pair * 2, 2), :], outs[:, bass.ds(pair * 2, 2), :]).then_inc(spilled, 16)

            for pair in (0, 1):
                for odd in (0, 1):
                    load(pair, odd)
            with sp.Fori(2, BLOCKS // 2) as pair:
                for odd in (0, 1):
                    load(pair, odd)
                spill(pair - 2)
            load(BLOCKS // 2, 0)
            for pair in (BLOCKS // 2 - 2, BLOCKS // 2 - 1):
                spill(pair)

        @block.gpsimd
        def _(g):
            ln.pool(g)
            g.wait_ge(place_ready, 2)
            g.wait_ge(ln.xn_ready, NT)
            for t in range(NT):
                to = bass.IndirectOffsetOnAxis(ap=place_in[:, t:t + 1], axis=0)
                g.indirect_dma_start(sorted_x, to, core.xn[:, t, :], None).then_inc(scattered, 16)
            g.wait_ge(spilled, 16 * (BLOCKS // 2))
            for t in range(NT):
                at = bass.IndirectOffsetOnAxis(ap=place_out[:, t:t + 1], axis=0)
                g.indirect_dma_start(routed[:, t, :], None, sorted_y, at).then_inc(gathered[t], 16)

        @block.scalar
        def _(act):
            for c in range(NC):
                ln.scalar(act, c)
            act.wait_ge(shifted, 1)
            act.activation(prob[:, :, :], logit[:, :, :], ACT.Exp).then_inc(exps, 1)

            def gate(n, odd):
                reach(act, hid_ready, n - 1)
                act.wait_ge(gate_pe, n + 1)
                act.activation(silu[:, odd, :], core.psum[:, GATE[odd], :], ACT.Silu).then_inc(silu_ready, 1)

            def step(pair, odd, parts):
                k = pair * 2 + odd
                if 0 in parts:
                    gate(k + HID0, odd)
                if 1 in parts:
                    reach(act, down_pe, k + DOWN0 - 2)
                    act.wait_ge(hidT_pe, k)
                    act.activation(block_hidT[:, 1 - odd, :], core.psum[:, HIDT, :], ACT.Copy).then_inc(hidT_ready, 1)

            for n in range(HID0):
                gate(n, n % 2)
            blocks(act, step)
            for n in range(HID0):
                gate(HID1 + n, n % 2)

        @block.tensor
        def _(pe):
            for c in range(NC):
                ln.tensor(pe, c)
            pe.wait_ge(ln.xnT_ready, NC)
            pe.wait_ge(w1_in, 16)
            for t in range(NT):
                ins = pe.matmul(core.psum[:, LOGITS, t * E:(t + 1) * E], core.xnT[:, t * P:(t + 1) * P], w1[:, 0:E], start=True, stop=True)
            ins.then_inc(logits_pe, 1)

            def shared_up(n0, c, j):
                n = n0 + j
                xc = core.xnT[:, c * CH:(c + 1) * CH]
                reach(pe, silu_ready, n - 1)
                pe.matmul(core.psum[:, GATE[n % 2], :], shared[:, GATE_AT + j * P:GATE_AT + (j + 1) * P], xc, start=True, stop=True).then_inc(gate_pe, 1)
                reach(pe, hid_ready, n - 1)
                pe.matmul(core.psum[:, UP[n % 2], :], shared[:, UP_AT + j * P:UP_AT + (j + 1) * P], xc, start=True, stop=True).then_inc(up_pe, 1)

            def shared_down(n0, d, c):
                pe.wait_ge(hid_ready, n0 + HT)
                reach(pe, out_read, d - 1)
                for t in range(TPC):
                    for j in range(HT):
                        ins = pe.matmul(core.psum[:, DOWN[d % 2], t * P:(t + 1) * P], hid[:, c % 2, j, t * P:(t + 1) * P],
                                        shared[:, DOWN_AT + j * P:DOWN_AT + (j + 1) * P], start=(j == 0), stop=(j == HT - 1))
                ins.then_inc(down_pe, 1)

            def turn(pair, odd):
                pe.wait_ge(rows_in[odd], pair * 16 + 16)
                reach(pe, rowsT_ready, pair * 2 + odd)
                pe.transpose(core.psum[:, TURN, 0:P], rows[odd][:, :], core.c("ident")).then_inc(turn_pe, 1)

            def expert(k):
                return pe.value_load(table[0:1, bass.ds(k, 1)], min_val=0, max_val=E - 2)

            def weights(e, at, n):
                return experts[:, bass.ds(e, 1), at:at + n].rearrange("p o c -> p (o c)")

            def step(pair, odd, parts):
                k = pair * 2 + odd
                if 0 in parts:
                    e = expert(k)
                    turn(pair + odd, 1 - odd)
                    pe.wait_ge(rowsT_ready, k + 1)
                    pe.wait_ge(silu_ready, k + HID0 - 1)
                    pe.matmul(core.psum[:, GATE[odd], :], rowsT[:, odd, :], weights(e, GATE_AT, H), start=True, stop=True).then_inc(gate_pe, 1)
                    pe.wait_ge(hid_ready, k + HID0 - 1)
                    pe.matmul(core.psum[:, UP[odd], :], rowsT[:, odd, :], weights(e, UP_AT, H), start=True, stop=True).then_inc(up_pe, 1)
                if 1 in parts:
                    pe.wait_ge(hid_ready, k + HID0)
                    reach(pe, hidT_ready, k - 1)
                    for j in range(HT):
                        ins = pe.transpose(core.psum[:, HIDT, j * P:(j + 1) * P], block_hid[:, 1 - odd, j * P:(j + 1) * P], core.c("ident"))
                    ins.then_inc(hidT_pe, 1)
                if 2 in parts:
                    e = expert(k - 2)
                    pe.wait_ge(hidT_ready, k - 1)
                    pe.wait_ge(out_read, k + DOWN0 - 3)
                    for j in range(HT):
                        ins = pe.matmul(core.psum[:, DOWN[odd], 0:D], block_hidT[:, odd, j * P:(j + 1) * P], weights(e, DOWN_AT + j * P, D),
                                        start=(j == 0), stop=(j == HT - 1))
                    ins.then_inc(down_pe, 1)

            def shared_chunks(n0, d0, c0):
                for c in range(HALF):
                    for j in range(HT):
                        shared_up(n0 + c * HT, c0 + c, j)
                        if n0 == 0 and c == 0 and j == 1:
                            pe.wait_ge(chosen_ready, 1)
                            picks = chosen[:, :, :].rearrange("p e t -> p (e t)")
                            pe.matmul(core.psum[:, RANKS, 0:P], core.c("earlier"), picks, start=True, stop=True)
                            pe.matmul(core.psum[:, RANKS, P:2 * P], core.c("ones"), picks, start=True, stop=True).then_inc(ranks_pe, 1)
                    if c:
                        shared_down(n0 + (c - 1) * HT, d0 + c - 1, c0 + c - 1)
                shared_down(n0 + (HALF - 1) * HT, d0 + HALF - 1, c0 + HALF - 1)

            pe.wait_ge(shared_in, 16)
            shared_chunks(0, 0, 0)
            pe.wait_ge(table_ready, 1)
            pe.wait_ge(experts_in, 16 * (E - 1))
            turn(0, 0)
            blocks(pe, step)
            shared_chunks(HID1, DOWN1, HALF)

        @block.vector
        def _(v):
            s = Steps(v, dve_step)
            ln.vector(v)
            v.wait_ge(logits_pe, 1)
            lp = core.psum[:, LOGITS, 0:NT * E].rearrange("p (t e) -> p t e", e=E)

            def wide(a):
                return a.unsqueeze(2).broadcast_to([P, NT, E])

            s.chain(v.tensor_reduce(most[:, :], lp, AX.X, ALU.max))
            v.tensor_tensor(logit[:, :, :], lp, wide(most[:, :]), ALU.subtract).then_inc(shifted, 1)
            v.wait_ge(shifted, 1)
            order = core.c("first8").unsqueeze(1).broadcast_to([P, NT, E])
            s.chain(v.scalar_tensor_tensor(first[:, :, :], logit[:, :, :], 0.0, order, ALU.is_equal, ALU.mult))
            s.chain(v.tensor_reduce(most[:, :], first[:, :, :], AX.X, ALU.max))
            v.tensor_tensor(chosen[:, :, :].rearrange("p e t -> p t e"), first[:, :, :], wide(most[:, :]), ALU.is_equal).then_inc(chosen_ready, 1)
            v.wait_ge(exps, 1)
            s.chain(v.tensor_reduce(total[:, :], prob[:, :, :], AX.X, ALU.add))
            v.wait_ge(chosen_ready, 1)
            s.did(v.tensor_scalar(coef[:, :], chosen[:, E - 1, :], -1.0, 1.0, ALU.mult, ALU.add))
            s.chain(v.reciprocal(total[:, :], total[:, :]))
            s.did(v.tensor_tensor(coef[:, :], coef[:, :], total[:, :], ALU.mult))
            v.wait_ge(ranks_pe, 1)
            within = core.psum[:, RANKS, 0:P].rearrange("p (e t) -> p e t", e=E)
            in_tile = core.psum[:, RANKS, P:2 * P].rearrange("p (e t) -> p e t", e=E)
            s.did(v.tensor_reduce(count[:, :], in_tile, AX.X, ALU.add))
            s.chain(v.tensor_copy(taken[:, :, :], in_tile))
            s.chain(v.tensor_scalar(whole[:, :], count[:, :], 1.0 / P, (P - 1) / P - 0.498, ALU.mult, ALU.add))
            s.chain(v.tensor_scalar(whole[:, :], whole[:, :], ROUND, None, ALU.add))
            s.chain(v.tensor_scalar(whole[:, :], whole[:, :], ROUND, None, ALU.subtract))
            s.chain(v.scalar_tensor_tensor(count[:, :], whole[:, :], float(P), count[:, :], ALU.mult, ALU.subtract))
            s.chain(v.tensor_tensor(taken[:, :, NT - 1], taken[:, :, NT - 1], count[:, :], ALU.add))

            def flat(a):
                return a[:, :, :].rearrange("p e t -> p (e t)")

            s.chain(v.tensor_tensor_scan(flat(ends), core.c("ones"), flat(taken), 0.0, ALU.mult, ALU.add))
            s.chain(v.tensor_tensor(taken[:, :, :], ends[:, :, :], taken[:, :, :], ALU.subtract))
            s.chain(v.tensor_tensor(taken[:, :, :], within, taken[:, :, :], ALU.add))
            s.chain(v.tensor_tensor(taken[:, :, :], taken[:, :, :], chosen[:, :, :], ALU.mult))
            s.chain(v.tensor_reduce(place[:, :], taken[:, :, :].rearrange("p e t -> p t e"), AX.X, ALU.add))
            v.tensor_copy(place_in[:, :], place[:, :]).then_inc(place_ready, 1)
            v.tensor_scalar(place_out[:, :], place[:, :], float(BLOCKS * P - 1), None, ALU.min).then_inc(place_ready, 1)
            start = core.c("block_start")[:, 0:BLOCKS].unsqueeze(1).broadcast_to([P, E - 1, BLOCKS])
            s.chain(v.tensor_tensor(passed[:, :, :], start, ends[:, 0:E - 1, NT - 1].unsqueeze(2).broadcast_to([P, E - 1, BLOCKS]), ALU.is_ge))
            s.chain(v.tensor_reduce(owner[:, :], passed[:, :, :].rearrange("p e b -> p b e"), AX.X, ALU.add))
            v.tensor_scalar(table[:, :], owner[:, :], float(E - 2), None, ALU.min).then_inc(table_ready, 1)

            def multiply(n, odd, dst):
                v.wait_ge(silu_ready, n + 1)
                v.wait_ge(up_pe, n + 1)
                v.tensor_tensor(dst, silu[:, odd, :], core.psum[:, UP[odd], :], ALU.mult).then_inc(hid_ready, 1)

            def shared_add(d, c):
                v.wait_ge(down_pe, d + 1)
                xs = core.x[:, TPC * c:TPC * (c + 1), :].rearrange("p t d -> p (t d)")
                v.scalar_tensor_tensor(xs, core.psum[:, DOWN[d % 2], :], 0.5, xs, ALU.mult, ALU.add).then_inc(out_read, 1)

            def shared_chunks(n0, d0, c0):
                for c in range(HALF):
                    for j in range(HT):
                        multiply(n0 + c * HT + j, j % 2, hid[:, c, j, :])
                    if c:
                        shared_add(d0 + c - 1, c0 + c - 1)
                shared_add(d0 + HALF - 1, c0 + HALF - 1)

            def turned(k, odd):
                v.wait_ge(turn_pe, k + 1)
                v.wait_ge(up_pe, k + HID0 - 1)
                v.tensor_copy(rowsT[:, odd, :], core.psum[:, TURN, 0:P]).then_inc(rowsT_ready, 1)

            def step(pair, odd, parts):
                k = pair * 2 + odd
                if 0 in parts:
                    turned(k + 1, 1 - odd)
                    reach(v, hidT_pe, k - 1)
                    multiply(k + HID0, odd, block_hid[:, odd, :])
                if 2 in parts:
                    v.wait_ge(down_pe, k + DOWN0 - 1)
                    dst = outs[:, bass.ds(k - 2, 1), :].rearrange("p o d -> p (o d)")
                    v.tensor_copy(dst, core.psum[:, DOWN[odd], 0:D]).then_inc(out_read, 1)

            shared_chunks(0, 0, 0)
            turned(0, 0)
            blocks(v, step)
            shared_chunks(HID1, DOWN1, HALF)
            v.wait_ge(out_read, DOWN1 + HALF)
            for t in range(NT):
                v.wait_ge(gathered[t], 16 * (call + 1))
                xs = core.x[:, t, :]
                s.did(v.scalar_tensor_tensor(xs, routed[:, t, :], coef[:, t:t + 1], xs, ALU.mult, ALU.add))


def mlp_stage(core, w2, w2_in, tag):
    nc = core.nc
    HT = 4

    def w(name, j=0):
        a, n = L2_COLS[name]
        return w2[:, a + j * P:a + (j + 1) * P] if n > HT else w2[:, a + j:a + j + 1]

    with ExitStack() as ctx:
        ln = LayerNorm(core, ctx, tag)
        gate = core.sb(ctx, tag + "gate", [P, 2, CH])
        h0 = core.sb(ctx, tag + "h0", [P, HT, N])
        h1 = core.sb(ctx, tag + "h1", [P, HT, CH])
        h2 = core.sb(ctx, tag + "h2", [P, HT, CH])
        y = core.sb(ctx, tag + "y", [P, TPC, D])
        gate_pe = core.sem(ctx, tag + "gate_pe")
        up_pe = core.sem(ctx, tag + "up_pe")
        silu_ready = core.sem(ctx, tag + "silu_ready")
        h0_ready = core.sem(ctx, tag + "h0_ready")
        hid_pe = core.sem(ctx, tag + "hid_pe")
        gelu_ready = core.sem(ctx, tag + "gelu_ready")
        y_pe = core.sem(ctx, tag + "y_pe")
        scaled = core.sem(ctx, tag + "scaled")
        added = core.sem(ctx, tag + "added")
        block = core.block(ctx)
        GATE, UP, HID, Y = (0, 1), (2, 3), (0, 1), 4
        GELUS = 2 * HT

        @block.gpsimd
        def _(g):
            ln.pool(g)

        @block.scalar
        def _(act):
            act.wait_ge(w2_in, 16)
            for c in range(NC):
                ln.scalar(act, c)
                for j in range(HT):
                    n = c * HT + j
                    if n >= 2:
                        act.wait_ge(h0_ready, n - 1)
                    act.wait_ge(gate_pe, n + 1)
                    act.activation(gate[:, n % 2, :], core.psum[:, GATE[n % 2], :], ACT.Silu, scale=w("s1", j)).then_inc(silu_ready, 1)
            act.sem_inc(gelu_ready, 1)
            with act.Fori(0, NC) as c:
                for layer, dst, scale in ((0, h1, "sh1"), (1, h2, "sh2")):
                    for j in range(HT):
                        n = layer * HT + j
                        act.wait_ge(hid_pe, c * GELUS + n + 1)
                        act.activation(dst[:, j, :], core.psum[:, HID[n % 2], :], ACT.Gelu, scale=w(scale, j)).then_inc(gelu_ready, 1)

        @block.tensor
        def _(pe):
            pe.wait_ge(w2_in, 16)
            ln.tensor(pe, 0)
            for c in range(NC):
                if c + 1 < NC:
                    ln.tensor(pe, c + 1)
                pe.wait_ge(ln.xnT_ready, c + 1)
                xc = core.xnT[:, c * CH:(c + 1) * CH]
                for j in range(HT):
                    n = c * HT + j
                    if n >= 2:
                        pe.wait_ge(silu_ready, n - 1)
                    pe.matmul(core.psum[:, GATE[n % 2], :], w("w1T", j), xc, start=True, stop=True).then_inc(gate_pe, 1)
                    if n >= 2:
                        pe.wait_ge(h0_ready, n - 1)
                    pe.matmul(core.psum[:, UP[n % 2], :], w("w2T", j), xc, start=True, stop=True).then_inc(up_pe, 1)
            pe.wait_ge(h0_ready, NC * HT)
            with pe.Fori(0, NC) as c:
                for layer, name in ((0, "h1T"), (1, "h2T")):
                    for j in range(HT):
                        n = layer * HT + j
                        pe.wait_ge(gelu_ready, c * GELUS + 1 + (n - 1 if n >= 2 else 0))
                        if layer == 1 and j == 0:
                            pe.wait_ge(gelu_ready, c * GELUS + 1 + HT)
                        for i in range(HT):
                            src = h0[:, i, bass.ds(c * CH, CH)] if layer == 0 else h1[:, i, :]
                            ins = pe.matmul(core.psum[:, HID[n % 2], :], w(name, i * HT + j), src, start=(i == 0), stop=(i == HT - 1))
                        ins.then_inc(hid_pe, 1)
                pe.wait_ge(gelu_ready, c * GELUS + 1 + GELUS)
                pe.wait_ge(added, c + 1)
                for t in range(TPC):
                    for i in range(HT):
                        ins = pe.matmul(core.psum[:, Y, t * P:(t + 1) * P], h2[:, i, t * P:(t + 1) * P], w("w3T", i), start=(i == 0), stop=(i == HT - 1))
                ins.then_inc(y_pe, 1)

        @block.vector
        def _(v):
            v.wait_ge(w2_in, 16)
            ln.vector(v)
            for c in range(NC):
                for j in range(HT):
                    n = c * HT + j
                    v.wait_ge(silu_ready, n + 1)
                    v.wait_ge(up_pe, n + 1)
                    v.scalar_tensor_tensor(h0[:, j, c * CH:(c + 1) * CH], core.psum[:, UP[n % 2], :], w("s2", j), gate[:, n % 2, :],
                                           ALU.mult, ALU.mult).then_inc(h0_ready, 1)
            v.sem_inc(added, 1)
            a, n = L2_COLS["s3"]
            s3 = w2[:, a:a + n].unsqueeze(1).broadcast_to([P, TPC, D])
            with v.Fori(0, NC) as c:
                v.wait_ge(y_pe, c + 1)
                v.wait_ge(added, c + 1)
                v.tensor_tensor(y[:, :, :], core.psum[:, Y, :].rearrange("p (t d) -> p t d", d=D), s3, ALU.mult).then_inc(scaled, 1)
                v.wait_ge(scaled, c + 1)
                xs = core.x[:, bass.ds(c * TPC, TPC), :]
                v.scalar_tensor_tensor(xs, y[:, :, :], 0.5, xs, ALU.mult, ALU.add).then_inc(added, 1)


class Norm:

    BANKS = (6, 7)

    def __init__(self, core, ctx, tag, src, dst, rms=False, eps=LN_EPS):
        self.k, self.src, self.dst, self.rms, self.eps = core, src, dst, rms, eps
        self.square = core.sb(ctx, tag + "square", [P, NT])
        self.stat_step = core.sem(ctx, tag + "stat_step")
        self.var_ready = core.sem(ctx, tag + "var_ready")
        self.pool_step = core.sem(ctx, tag + "pool_step")
        self.rstd_ready = core.sem(ctx, tag + "rstd_ready")
        self.xn_ready = core.sem(ctx, tag + "xn_ready")
        self.turned = core.sem(ctx, tag + "turned")
        self.xnT_ready = core.sem(ctx, tag + "xnT_ready")

    def vector(self, v):
        k = self.k

        def statistics(c):
            tiles = range(TPC * c, TPC * (c + 1))
            for t in tiles:
                v.bn_stats(k.stats[:, t, :], self.src[:, t, :]).then_inc(self.stat_step, 1)
            for t in tiles:
                v.wait_ge(self.stat_step, t + 1)
                v.bn_aggr(k.meanvar[:, t, :], k.stats[:, t, :]).then_inc(self.var_ready, 1)

        def normalise(c):
            v.wait_ge(self.var_ready, TPC * (c + 1))
            v.wait_ge(self.rstd_ready, c + 1)
            for t in range(TPC * c, TPC * (c + 1)):
                if self.rms:
                    ins = v.tensor_scalar(self.dst[:, t, :], self.src[:, t, :], k.rstd[:, t:t + 1], None, ALU.mult)
                else:
                    ins = v.tensor_scalar(self.dst[:, t, :], self.src[:, t, :], k.meanvar[:, t, 0:1], k.rstd[:, t:t + 1],
                                          ALU.subtract, ALU.mult)
                ins.then_inc(self.xn_ready, 1)

        statistics(0)
        for c in range(NC):
            if c + 1 < NC:
                statistics(c + 1)
            normalise(c)

    def pool(self, g):
        k = self.k
        s = Steps(g, self.pool_step)
        for c in range(NC):
            a, b = TPC * c, TPC * (c + 1)
            g.wait_ge(self.var_ready, b)
            var, mean, r = k.meanvar[:, a:b, 1], k.meanvar[:, a:b, 0], k.rstd[:, a:b]
            if self.rms:
                s.chain(g.tensor_tensor(self.square[:, a:b], mean, mean, ALU.mult))
                s.chain(g.tensor_tensor(self.square[:, a:b], self.square[:, a:b], var, ALU.add))
                var = self.square[:, a:b]
            s.chain(g.tensor_scalar(r, var, self.eps, None, ALU.add))
            g.tensor_tensor(r, r, k.mhalf[:, a:b], ALU.pow).then_inc(self.rstd_ready, 1)

    def tensor(self, pe, c):
        k = self.k
        if c >= 2:
            pe.wait_ge(self.xnT_ready, c - 1)
        for t in range(TPC):
            pe.wait_ge(self.xn_ready, TPC * c + t + 1)
            ins = pe.transpose(k.psum[:, self.BANKS[c % 2], t * P:(t + 1) * P], self.dst[:, TPC * c + t, :], k.c("ident"))
        ins.then_inc(self.turned, 1)

    def scalar(self, act, c, gain=1.0, bias=0.0):
        k = self.k
        act.wait_ge(self.turned, c + 1)
        act.activation(k.xnT[:, c * CH:(c + 1) * CH], k.psum[:, self.BANKS[c % 2], :], ACT.Identity, bias=bias, scale=gain).then_inc(self.xnT_ready, 1)


def norm_stage(core, tag):
    with ExitStack() as ctx:
        ln = Norm(core, ctx, tag, core.x, core.xn)
        block = core.block(ctx)

        @block.gpsimd
        def _(g):
            ln.pool(g)

        @block.vector
        def _(v):
            ln.vector(v)


class Split:

    PARTS = 3

    def __init__(self, core, ctx, tag, rows, scratch):
        self.k, self.rows, self.scratch = core, rows, scratch
        self.parts = [core.sb(ctx, f"{tag}parts{i}", [r, self.PARTS, 2, CH], BF16) for i, r in enumerate(rows)]
        self.rest = [core.sb(ctx, f"{tag}rest{i}", [r, CH]) for i, r in enumerate(rows)]
        self.heads_pe = core.sem(ctx, tag + "heads_pe")
        self.part_ready = core.sem(ctx, tag + "part_ready")
        self.rest_ready = core.sem(ctx, tag + "rest_ready")
        self.spilled = [[core.sem(ctx, f"{tag}spilled{i}{odd}") for odd in range(2)] for i in range(2)]

    def scalar(self, act, c, i, source):
        n = 2 * c + i
        act.wait_ge(self.heads_pe, n + 1)
        if c >= 2:
            act.wait_ge(self.spilled[i][c % 2], 16 * (c // 2))
        act.activation(self.parts[i][:, 0, c % 2, :], source, ACT.Copy).then_inc(self.part_ready, 1)
        for p in range(1, self.PARTS):
            act.wait_ge(self.rest_ready, 2 * n + p)
            act.activation(self.parts[i][:, p, c % 2, :], self.rest[i][:, :], ACT.Copy).then_inc(self.part_ready, 1)

    def vector(self, v, c, i, source):
        n = 2 * c + i
        for p in range(1, self.PARTS):
            v.wait_ge(self.part_ready, self.PARTS * n + p)
            if n:
                v.wait_ge(self.rest_ready, 2 * n + p - 1)
            v.tensor_tensor(self.rest[i][:, :], source if p == 1 else self.rest[i][:, :], self.parts[i][:, p - 1, c % 2, :],
                            ALU.subtract).then_inc(self.rest_ready, 1)

    def sync(self, sp, c, i):
        n = 2 * c + i
        b, at = divmod(c * CH, T)
        sp.wait_ge(self.part_ready, self.PARTS * (n + 1))
        dst = self.scratch[i][:, b, :, at:at + CH].rearrange("p r t -> r p t")
        sp.dma_start(dst, self.parts[i][:, :, c % 2, :]).then_inc(self.spilled[i][c % 2], 16)

    def landed(self, sp):
        for i in range(2):
            for odd in range(2):
                sp.wait_ge(self.spilled[i][odd], 16 * NC // 2)


HEADS, HD = 16, 8


def rope_project_stage(core, w3, w3_in, v_all, scratch, tag):
    nc = core.nc
    QK = 2 * 2 * D

    def w(name, rows=P):
        a, n = L1_COLS[name]
        return w3[0:rows, a:a + n]

    with ExitStack() as ctx:
        ln = LayerNorm(core, ctx, tag)
        sp_ = Split(core, ctx, tag, (P, P), scratch)
        cosed = core.sb(ctx, tag + "cosed", [P, 2, D])
        sined = core.sb(ctx, tag + "sined", [P, 2, D])
        heads = core.sb(ctx, tag + "heads", [P, 2, 2, D])
        qk_pe = core.sem(ctx, tag + "qk_pe")
        v_ready = core.sem(ctx, tag + "v_ready")
        cos_step = core.sem(ctx, tag + "cos_step")
        heads_ready = core.sem(ctx, tag + "heads_ready")
        turned = core.sem(ctx, tag + "turned_qk")
        block = core.block(ctx)
        QK_BANK, V_BANK, T_BANK = (0, 1), (2, 3), (4, 5)

        @block.gpsimd
        def _(g):
            ln.pool(g)

        @block.sync
        def _(sp):
            for c in range(NC):
                for i in range(2):
                    sp_.sync(sp, c, i)
            sp_.landed(sp)

        @block.tensor
        def _(pe):
            pe.wait_ge(w3_in, 16)
            for c in range(NC):
                ln.tensor(pe, c)

            def turn(t):
                c = t // TPC
                if t % TPC == 0 and c:
                    pe.wait_ge(sp_.rest_ready, 4 * c - 1)
                    pe.wait_ge(sp_.part_ready, 3 * (2 * c) - 2)
                pe.wait_ge(heads_ready, t + 1)
                for i in range(2):
                    ins = pe.transpose(core.psum[:, T_BANK[i], (t % TPC) * P:(t % TPC + 1) * P], heads[:, t % 2, i, :], core.c("ident"))
                    if t % TPC == TPC - 1:
                        ins.then_inc(sp_.heads_pe, 1)
                    elif i == 1:
                        ins.then_inc(turned, 1)

            for t in range(NT):
                pe.wait_ge(ln.xnT_ready, t // TPC + 1)
                if t >= 2:
                    pe.wait_ge(cos_step, 2 * (t - 1))
                    pe.wait_ge(v_ready, t - 1)
                xt = core.xnT[:, t * P:(t + 1) * P]
                for bank, name, bias, n in ((QK_BANK, "qk", "qk_b", QK), (V_BANK, "v", "v_b", D)):
                    pe.matmul(core.psum[:, bank[t % 2], 0:n], w("ones", 1), w(bias, 1), start=True, stop=False)
                    ins = pe.matmul(core.psum[:, bank[t % 2], 0:n], xt, w(name), start=False, stop=True)
                ins.then_inc(qk_pe, 1)
                if t:
                    turn(t - 1)
            turn(NT - 1)

        @block.scalar
        def _(act):
            act.wait_ge(w3_in, 16)
            for c in range(NC):
                ln.scalar(act, c)
            for t in range(NT):
                act.wait_ge(qk_pe, t + 1)
                act.activation(v_all[:, t, :], core.psum[:, V_BANK[t % 2], 0:D], ACT.Copy).then_inc(v_ready, 1)
                if t % TPC == 1 and t > TPC:
                    for i in range(2):
                        sp_.scalar(act, t // TPC - 1, i, core.psum[:, T_BANK[i], :])
            for i in range(2):
                sp_.scalar(act, NC - 1, i, core.psum[:, T_BANK[i], :])

        @block.vector
        def _(v):
            v.wait_ge(w3_in, 16)
            ln.vector(v)

            def table(name, t):
                a, n = L1_COLS[name]
                tab = w3[:, a + (t % (T // P)) * HD:a + (t % (T // P)) * HD + HD]
                return tab.unsqueeze(1).unsqueeze(1).broadcast_to([P, 2, HEADS, HD])

            def four(a):
                return a.rearrange("p i (h d) -> p i h d", d=HD)

            for t in range(NT):
                ps = core.psum[:, QK_BANK[t % 2], :].rearrange("p (i r f) -> p i r f", i=2, r=2)
                v.wait_ge(qk_pe, t + 1)
                if t:
                    v.wait_ge(heads_ready, t)
                v.tensor_tensor(four(cosed[:, :, :]), four(ps[:, :, 0, :]), table("cos", t), ALU.mult).then_inc(cos_step, 1)
                v.tensor_tensor(four(sined[:, :, :]), four(ps[:, :, 1, :]), table("sin", t), ALU.mult).then_inc(cos_step, 1)
                v.wait_ge(cos_step, 2 * t + 2)
                if t >= 2:
                    u = t - 2
                    v.wait_ge(turned, u // TPC * (TPC - 1) + min(u % TPC + 1, TPC - 1))
                    if u // TPC * TPC + TPC - 1 == u:
                        v.wait_ge(sp_.heads_pe, 2 * (u // TPC + 1))
                v.tensor_tensor(heads[:, t % 2, :, :], cosed[:, :, :], sined[:, :, :], ALU.add).then_inc(heads_ready, 1)
                if t % TPC == 1 and t > TPC:
                    for i in range(2):
                        sp_.vector(v, t // TPC - 1, i, core.psum[:, T_BANK[i], :])
            for i in range(2):
                sp_.vector(v, NC - 1, i, core.psum[:, T_BANK[i], :])


def attend_stage(core, masks, masks_in, v_all, scratch, kv_heads, guard, w_out, w_out_in, b_out, out, tag):
    nc = core.nc
    PARTS = Split.PARTS
    PAIRS = PARTS ** 2
    ROWS = PAIRS * HD
    KROWS = ROWS + (PARTS if guard else 0)
    SCALE = HD ** -0.5
    KT = T // P
    G = 4
    GPB = HEADS // G
    GROUPS = NB * GPB
    VH = 1 if kv_heads < HEADS else G
    RING = 4
    STACK = 2 * PAIRS * 16
    EXPS = KT * G
    LEAD = 2
    O_BANK, MAX_BANK = 4, 6

    units = [(hh, qt, lo, min(lo + CH, (qt + 1) * P)) for hh in range(G) for qt in range(KT) for lo in range(0, (qt + 1) * P, CH)] if guard else []
    UNITS = len(units)
    MAXES = 2 * KT
    MAX_STEPS = 2 * PARTS + 1
    weight = np.cumsum([KT - kt + 1 for kt in range(KT) for _ in range(G)])
    upto = [int(round(UNITS * w / weight[-1])) for w in weight]

    def unit_range(slot):
        return range(upto[slot - 1] if slot else 0, upto[slot])

    def spans(lo, hi):
        return [(a, b) for a, b in ((lo, min(hi, CH)), (max(lo, CH), hi)) if a < b]

    def reach(eng, sem, count):
        if not isinstance(count, int) or count > 0:
            eng.wait_ge(sem, count)

    def groups(eng, step):
        lead = LEAD if guard else 0
        step(0, True)
        with eng.Fori(1, GROUPS - lead) as n:
            step(n, True)
        for n in range(GROUPS - lead, GROUPS):
            step(n, False)

    with ExitStack() as ctx:
        qs = core.sb(ctx, tag + "qs", [KROWS, RING, G, T], BF16)
        ks = core.sb(ctx, tag + "ks", [96, RING, VH, T], BF16)
        vslot = core.sb(ctx, tag + "vslot", [P, KT, VH, 32])
        probs = core.sb(ctx, tag + "probs", [P, 2, G, T])
        o = core.sb(ctx, tag + "o", [P, T])
        otok = core.sb(ctx, tag + "otok", [P, NT, D])
        sums = core.sb(ctx, tag + "sums", [P, KT, G])
        most = core.sb(ctx, tag + "most", [P, G, MAXES])
        least = core.sb(ctx, tag + "least", [P, G, KT])
        rest = core.sb(ctx, tag + "rest", [G * KT, 2, P])
        most_parts = core.sb(ctx, tag + "most_parts", [G * KT, PARTS, P], BF16)
        stack_in = core.sem(ctx, tag + "stack_in")
        started = core.sem(ctx, tag + "started")
        set_up = core.sem(ctx, tag + "set_up")
        max_pe = core.sem(ctx, tag + "max_pe")
        max_read = core.sem(ctx, tag + "max_read")
        max_turned = core.sem(ctx, tag + "max_turned")
        max_step = core.sem(ctx, tag + "max_step")
        max_in = core.sem(ctx, tag + "max_in")
        vslot_ready = core.sem(ctx, tag + "vslot_ready")
        score_pe = core.sem(ctx, tag + "score_pe")
        probs_ready = core.sem(ctx, tag + "probs_ready")
        pv_pe = core.sem(ctx, tag + "pv_pe")
        o_copied = core.sem(ctx, tag + "o_copied")
        o_turned = core.sem(ctx, tag + "o_turned")
        sums_ready = core.sem(ctx, tag + "sums_ready")
        o_ready = core.sem(ctx, tag + "o_ready")
        oT_pe = core.sem(ctx, tag + "oT_pe")
        oT_ready = core.sem(ctx, tag + "oT_ready")
        y_pe = core.sem(ctx, tag + "y_pe")
        y_added = core.sem(ctx, tag + "y_added")
        block = core.block(ctx)

        def flat(bank):
            return core.psum[:, bank:bank + 2, :].rearrange("p b c -> p (b c)")

        def mask(name):
            a, n = MASK_COLS[name]
            return masks[:, a:a + n]

        def stack(tile, rows, n, head, lo, hi):
            return tile[0:rows, bass.ds(n % RING, 1), head, lo:hi].rearrange("r o t -> r (o t)")

        @block.sync
        def _(sp):
            def place(n):
                return n % RING if isinstance(n, int) else sp.snap(n % RING)

            def load(n, slot):
                for i in range(PARTS):
                    for j in range(PARTS):
                        r = (i * PARTS + j) * HD
                        for tile, src, heads in ((qs, scratch[0][i], G), (ks, scratch[1][j], VH)):
                            rows = src.rearrange("b r t -> (b r) t")[bass.ds(n * (heads * HD), heads * HD), :]
                            dst = tile[r:r + HD, bass.ds(slot, 1), :, :].rearrange("r o h t -> r (o h) t")
                            sp.dma_start(dst, rows.rearrange("(h d) t -> d h t", d=HD)).then_inc(stack_in, 16)

            def maximum(n, slot):
                sp.wait_ge(max_step, n * MAX_STEPS + MAX_STEPS)
                for p in range(PARTS):
                    dst = qs[ROWS + p:ROWS + p + 1, bass.ds(slot, 1), :, :].rearrange("r o h (k q) -> r (o h k) q", q=P)
                    sp.dma_start(dst, most_parts[:, p:p + 1, :]).then_inc(max_in, 16)

            sp.wait_ge(set_up, 1)
            load(0, 0)
            if guard:
                sp.wait_ge(started, 1)
                load(1, 1)
                maximum(0, 0)
                sp.wait_ge(started, 2)
                load(2, 2)
                maximum(1, 1)
                sp.wait_ge(started, 3)
                load(3, 3)
                with sp.Fori(1, GROUPS - RING + 1) as n:
                    max_slot, slot = place(n + 1), place(n + 3)
                    maximum(n + 1, max_slot)
                    sp.wait_ge(started, n + 3)
                    load(n + 3, slot)
                for n in range(GROUPS - RING + 2, GROUPS):
                    maximum(n, n % RING)
            else:
                with sp.Fori(1, GROUPS) as n:
                    slot = place(n)
                    sp.wait_ge(started, n)
                    load(n, slot)

        @block.gpsimd
        def _(g):
            s = Steps(g, set_up)
            s.chain(g.memset(ks[64:96, :, :, :], 1.0))
            s.chain(g.memset(vslot[:, :, :, :], 0.0))
            s.chain(g.memset(vslot[:, :, :, HD:HD + 1], 1.0))

            def values_of(n):
                src = v_all[:, bass.ds(n // GPB * KT, KT), bass.ds(n % GPB * (VH * HD), VH * HD)].rearrange("p k (h d) -> p k h d", d=HD)
                g.tensor_copy(vslot[:, :, :, 0:HD], src).then_inc(vslot_ready, 1)

            values_of(0)
            with g.Fori(1, GROUPS) as n:
                g.wait_ge(pv_pe, n * KT)
                values_of(n)

        @block.tensor
        def _(pe):
            pe.wait_ge(masks_in, 16)

            def max_unit(n, u):
                hh, qt, lo, hi = units[u]
                if u == 0:
                    pe.wait_ge(stack_in, n * STACK + STACK)
                reach(pe, max_read, n * UNITS + u - 1)
                if u == 1:
                    reach(pe, max_step, n * MAX_STEPS)
                s = core.psum[:, MAX_BANK + (u + 1) % 2, :]
                last = hi == (qt + 1) * P
                ins = pe.matmul(s[:, 0:hi - lo], stack(qs, ROWS, n, hh, qt * P, (qt + 1) * P), stack(ks, ROWS, n, hh if VH == G else 0, lo, hi),
                                start=True, stop=not last)
                if u == 0:
                    ins.then_inc(started, 1)
                if last:
                    ins = pe.matmul(s[:, hi - lo - P:hi - lo], mask("ident"), mask("future_key"), start=False, stop=True)
                ins.then_inc(max_pe, 1)

            def max_turn(n):
                pe.wait_ge(max_step, n * MAX_STEPS + 2)
                pe.transpose(core.psum[0:G * KT, MAX_BANK, 0:P], least[:, :, :].rearrange("p h k -> p (h k)"), core.c("ident")).then_inc(max_turned, 1)

            def scores(n, kt, hh):
                m = kt * G + hh
                if m == 0:
                    if guard:
                        pe.wait_ge(max_in, n * (PARTS * 16) + PARTS * 16)
                    else:
                        pe.wait_ge(stack_in, n * STACK + STACK)
                reach(pe, probs_ready, n * EXPS + m - 1)
                s = flat(2 * (m % 2))
                for lo, hi in spans(kt * P, T):
                    ins = pe.matmul(s[:, lo:hi], stack(ks, KROWS, n, hh if VH == G else 0, kt * P, (kt + 1) * P), stack(qs, KROWS, n, hh, lo, hi),
                                    start=True, stop=lo != kt * P)
                if m == 0 and not guard:
                    ins.then_inc(started, 1)
                pe.matmul(s[:, kt * P:(kt + 1) * P], mask("ident"), mask("past_query"), start=False, stop=True).then_inc(score_pe, 1)

            def values(n, kt, part, parts):
                if part == 0:
                    pe.wait_ge(probs_ready, n * EXPS + (kt + 1) * G)
                    if kt == 0:
                        pe.wait_ge(vslot_ready, n + 1)
                        reach(pe, o_ready, n)
                width = (T - kt * P) // parts
                for lo, hi in spans(kt * P + part * width, kt * P + (part + 1) * width):
                    for hh in range(G):
                        ins = pe.matmul(flat(O_BANK)[32 * hh:32 * hh + 32, lo:hi], vslot[:, kt, hh if VH == G else 0, :],
                                        probs[:, kt % 2, hh, lo:hi], start=kt == 0 and lo % CH == 0, stop=kt == KT - 1,
                                        tile_position=(0, 32 * hh), skip_group_check=True)
                if part == parts - 1:
                    ins.then_inc(pv_pe, 1)

            def turn(n):
                pe.wait_ge(o_copied, n + 1)
                for t in range(KT):
                    ins = pe.transpose(flat(O_BANK)[:, t * P:(t + 1) * P], o[:, t * P:(t + 1) * P], core.c("ident"))
                ins.then_inc(o_turned, 1)

            def step(n, ahead):
                later = not (isinstance(n, int) and n == 0)
                last = isinstance(n, int) and n == GROUPS - 1
                for kt in range(KT):
                    for hh in range(G):
                        scores(n, kt, hh)
                        if kt:
                            values(n, kt - 1, hh, G)
                        elif hh == 0:
                            if later:
                                values(n - 1, KT - 1, 0, 1)
                            if guard and not last:
                                max_turn(n + 1)
                        elif hh == G - 1 and later:
                            turn(n - 1)
                        if ahead:
                            for u in unit_range(kt * G + hh):
                                max_unit(n + LEAD, u)

            if guard:
                for n in range(LEAD):
                    for u in range(UNITS):
                        max_unit(n, u)
                    if n < LEAD - 1:
                        max_turn(n)
            groups(pe, step)
            values(GROUPS - 1, KT - 1, 0, 1)
            turn(GROUPS - 1)
            pe.wait_ge(w_out_in, 16)
            pe.wait_ge(o_ready, GROUPS)
            for c in range(NC):
                if c >= 2:
                    pe.wait_ge(oT_ready, c - 1)
                for t in range(TPC):
                    ins = pe.transpose(core.psum[:, c % 2, t * P:(t + 1) * P], otok[:, TPC * c + t, :], core.c("ident"))
                ins.then_inc(oT_pe, 1)
            for c in range(NC):
                pe.wait_ge(oT_ready, c + 1)
                if c >= 2:
                    pe.wait_ge(y_added, c - 1)
                for t in range(TPC):
                    dst = core.psum[:, 2 + c % 2, t * P:(t + 1) * P]
                    if b_out is not None:
                        pe.matmul(dst, b_out[0], b_out[1], start=True, stop=False)
                    ins = pe.matmul(dst, core.xnT[:, c * CH + t * P:c * CH + (t + 1) * P], w_out, start=b_out is None, stop=True)
                ins.then_inc(y_pe, 1)

        @block.scalar
        def _(act):
            def copy_o(n):
                act.wait_ge(pv_pe, n * KT + KT)
                reach(act, o_turned, n)
                act.activation(o[:, :], flat(O_BANK), ACT.Copy).then_inc(o_copied, 1)

            def step(n, ahead):
                later = not (isinstance(n, int) and n == 0)
                for kt in range(KT):
                    for hh in range(G):
                        m = kt * G + hh
                        if hh == 0:
                            reach(act, pv_pe, n * KT + kt - 1)
                        act.wait_ge(score_pe, n * EXPS + m + 1)
                        act.activation(probs[:, kt % 2, hh, kt * P:T], flat(2 * (m % 2))[:, kt * P:T], ACT.Exp, scale=SCALE).then_inc(probs_ready, 1)
                        if m == 1 and later:
                            copy_o(n - 1)

            groups(act, step)
            copy_o(GROUPS - 1)
            for c in range(NC):
                act.wait_ge(oT_pe, c + 1)
                act.activation(core.xnT[:, c * CH:(c + 1) * CH], core.psum[:, c % 2, :], ACT.Copy).then_inc(oT_ready, 1)

        @block.vector
        def _(v):
            def max_unit(n, u):
                hh, qt, lo, hi = units[u]
                v.wait_ge(max_pe, n * UNITS + u + 1)
                at = qt if lo == 0 else KT + qt
                v.tensor_reduce(most[:, hh:hh + 1, at], core.psum[:, MAX_BANK + (u + 1) % 2, 0:hi - lo], AX.X, ALU.max).then_inc(max_read, 1)

            def negate(n):
                v.wait_ge(max_read, n * UNITS + UNITS)
                both = KT // 2
                v.tensor_tensor(most[:, :, both:KT], most[:, :, both:KT], most[:, :, KT + both:2 * KT], ALU.max).then_inc(max_step, 1)
                v.wait_ge(max_step, n * MAX_STEPS + 1)
                v.tensor_scalar(least[:, :, :], most[:, :, 0:KT], -1.0, None, ALU.mult).then_inc(max_step, 1)

            def split(n):
                v.wait_ge(max_turned, n + 1)
                reach(v, max_in, n * (PARTS * 16))
                left = core.psum[0:G * KT, MAX_BANK, 0:P]
                for p in range(PARTS):
                    v.tensor_copy(most_parts[:, p, :], left).then_inc(max_step, 1)
                    if p < PARTS - 1:
                        v.wait_ge(max_step, n * MAX_STEPS + 3 + 2 * p)
                        v.tensor_tensor(rest[:, p, :], left, most_parts[:, p, :], ALU.subtract).then_inc(max_step, 1)
                        v.wait_ge(max_step, n * MAX_STEPS + 4 + 2 * p)
                        left = rest[:, p, :]

            def normalise(n):
                v.wait_ge(o_turned, n + 1)
                turned = flat(O_BANK).rearrange("p (t h f) -> p t h f", h=G, f=32)
                v.reciprocal(sums[:, :, :], turned[:, :, :, HD]).then_inc(sums_ready, 1)
                v.wait_ge(sums_ready, n + 1)
                dst = otok[:, bass.ds(n // GPB * KT, KT), bass.ds(n % GPB * (G * HD), G * HD)].rearrange("p t (h d) -> p t h d", d=HD)
                v.tensor_tensor(dst, turned[:, :, :, 0:HD], sums[:, :, :].unsqueeze(3).broadcast_to([P, KT, G, HD]), ALU.mult).then_inc(o_ready, 1)

            def step(n, ahead):
                later = not (isinstance(n, int) and n == 0)
                last = isinstance(n, int) and n == GROUPS - 1
                if guard and not last:
                    split(n + 1)
                for slot in range(EXPS):
                    if slot == G and later:
                        normalise(n - 1)
                    if ahead:
                        for u in unit_range(slot):
                            max_unit(n + LEAD, u)
                if guard and ahead:
                    negate(n + LEAD)

            if guard:
                for n in range(LEAD):
                    for u in range(UNITS):
                        max_unit(n, u)
                    negate(n)
                    if n < LEAD - 1:
                        split(n)
            groups(v, step)
            normalise(GROUPS - 1)
            for c in range(NC):
                v.wait_ge(y_pe, c + 1)
                tiles = slice(TPC * c, TPC * (c + 1))
                y = core.psum[:, 2 + c % 2, :].rearrange("p (t d) -> p t d", d=D)
                v.tensor_tensor(out[:, tiles, :], out[:, tiles, :], y, ALU.add).then_inc(y_added, 1)


def attend_window_stage(core, masks, masks_in, v_all, scratch, kv_heads, guard, window, w_out, w_out_in, b_out, addends, tag):
    nc = core.nc
    PAIRS = Split.PARTS ** 2
    ROWS = PAIRS * HD
    KROWS = ROWS + (Split.PARTS if guard else 0)
    SCALE = HD ** -0.5
    KT = T // P
    G = 4
    GROUPS = HEADS // G
    VH = 1 if kv_heads < HEADS else G
    STEPS = KT * G
    WIDE = P + window if window else 0

    def spans(kt):
        a, b = kt * P, min(T, kt * P + WIDE) if window else T
        return [(lo, hi) for lo, hi in ((a, min(b, CH)), (max(a, CH), b)) if lo < hi]

    with ExitStack() as ctx:
        qs = core.sb(ctx, tag + "qs", [KROWS, HEADS, T], BF16)
        ks = core.sb(ctx, tag + "ks", [96, kv_heads, T], BF16)
        vslot = core.sb(ctx, tag + "vslot", [P, KT, VH, 32])
        probs = core.sb(ctx, tag + "probs", [P, 2, G, WIDE or T])
        o = core.sb(ctx, tag + "o", [P, T])
        otok = core.sb(ctx, tag + "otok", [P, NT, D])
        sums = core.sb(ctx, tag + "sums", [P, KT, G])
        most = core.sb(ctx, tag + "most", [P, HEADS, KT])
        mostT = core.sb(ctx, tag + "mostT", [P, 2, P])
        most_parts = core.sb(ctx, tag + "most_parts", [P, Split.PARTS, P], BF16)
        stack_in = core.sem(ctx, tag + "stack_in")
        stack_free = core.sem(ctx, tag + "stack_free")
        set_up = core.sem(ctx, tag + "set_up")
        max_pe = core.sem(ctx, tag + "max_pe")
        max_read = core.sem(ctx, tag + "max_read")
        max_turned = core.sem(ctx, tag + "max_turned")
        max_step = core.sem(ctx, tag + "max_step")
        max_in = core.sem(ctx, tag + "max_in")
        vslot_ready = core.sem(ctx, tag + "vslot_ready")
        score_pe = core.sem(ctx, tag + "score_pe")
        probs_ready = core.sem(ctx, tag + "probs_ready")
        pv_pe = core.sem(ctx, tag + "pv_pe")
        o_copied = core.sem(ctx, tag + "o_copied")
        o_turned = core.sem(ctx, tag + "o_turned")
        sums_ready = core.sem(ctx, tag + "sums_ready")
        o_ready = core.sem(ctx, tag + "o_ready")
        oT_pe = core.sem(ctx, tag + "oT_pe")
        oT_ready = core.sem(ctx, tag + "oT_ready")
        y_pe = core.sem(ctx, tag + "y_pe")
        y_added = core.sem(ctx, tag + "y_added")
        block = core.block(ctx)
        O_BANK, T_BANK = 4, 6
        SCORES = 1 if window else G
        if window:
            assert 2 * WIDE <= CH

        def flat(bank):
            return core.psum[:, bank:bank + 2, :].rearrange("p b c -> p (b c)")

        def mask(name):
            a, n = MASK_COLS[name]
            return masks[:, a:a + n]

        @block.sync
        def _(sp):
            sp.wait_ge(set_up, 1)
            with sp.Fori(0, NB) as b:
                sp.wait_ge(stack_free, b + 1)
                for i in range(Split.PARTS):
                    for j in range(Split.PARTS):
                        r = (i * Split.PARTS + j) * HD
                        for tile, src in ((qs, scratch[0][i]), (ks, scratch[1][j])):
                            sp.dma_start(tile[r:r + HD, :, :], src[bass.ds(b, 1), :, :].rearrange("o (h d) t -> (o d) h t", d=HD)).then_inc(stack_in, 16)
                if guard:
                    sp.wait_ge(max_step, b * 6 + 6)
                    for p in range(Split.PARTS):
                        dst = qs[ROWS + p:ROWS + p + 1, :, :].rearrange("o h (k q) -> o (h k) q", q=P)
                        sp.dma_start(dst, most_parts[:, p:p + 1, :]).then_inc(max_in, 16)

        @block.gpsimd
        def _(g):
            s = Steps(g, set_up)
            s.chain(g.memset(ks[64:96, :, :], 1.0))
            s.chain(g.memset(vslot[:, :, :, :], 0.0))
            s.chain(g.memset(vslot[:, :, :, HD:HD + 1], 1.0))
            g.sem_inc(stack_free, 1)
            with g.Fori(0, NB) as b:
                with g.Fori(0, GROUPS) as h:
                    g.wait_ge(pv_pe, (b * GROUPS + h) * KT + 1)
                    src = v_all[:, bass.ds(b * KT, KT), bass.ds(h * (VH * HD), VH * HD)].rearrange("p k (h d) -> p k h d", d=HD)
                    g.tensor_copy(vslot[:, :, :, 0:HD], src).then_inc(vslot_ready, 1)

        @block.tensor
        def _(pe):
            pe.wait_ge(masks_in, 16)
            pe.sem_inc(pv_pe, 1)
            with pe.Fori(0, NB) as b:
                if guard:
                    with pe.Fori(0, HEADS) as h:
                        pe.wait_ge(stack_in, b * (2 * PAIRS * 16) + 2 * PAIRS * 16)
                        for qt in range(KT):
                            pe.wait_ge(max_read, (b * HEADS + h) * KT + max(qt, 1))
                            s = flat(2 * (qt % 2))
                            q = qs[0:ROWS, bass.ds(h, 1), qt * P:(qt + 1) * P].rearrange("r o t -> r (o t)")
                            for lo in range(0, (qt + 1) * P, CH):
                                hi = min(lo + CH, (qt + 1) * P)
                                k = ks[0:ROWS, bass.ds(h, 1), lo:hi].rearrange("r o t -> r (o t)")
                                pe.matmul(s[:, lo:hi], q, k, start=True, stop=hi < (qt + 1) * P)
                            pe.matmul(s[:, qt * P:(qt + 1) * P], mask("ident"), mask("future_key"), start=False, stop=True).then_inc(max_pe, 1)
                    pe.wait_ge(max_step, b * 6 + 1)
                    pe.transpose(core.psum[:, T_BANK, 0:P], most[:, :, :].rearrange("p h k -> p (h k)"), core.c("ident")).then_inc(max_turned, 1)
                with pe.Fori(0, GROUPS) as g:
                    n = b * GROUPS + g
                    pe.wait_ge(stack_in, b * (2 * PAIRS * 16) + 2 * PAIRS * 16)
                    if guard:
                        pe.wait_ge(max_in, b * (Split.PARTS * 16) + Split.PARTS * 16)

                    def scores(kt):
                        for hh in range(G):
                            m = kt * SCORES + (0 if window else hh)
                            kh = g * G + hh if kv_heads == HEADS else g
                            k = ks[0:KROWS, bass.ds(kh, 1), kt * P:(kt + 1) * P].rearrange("r o t -> r (o t)")
                            if not window or hh == 0:
                                pe.wait_ge(probs_ready, n * (KT * SCORES) + max(m, 1))
                            for lo, hi in spans(kt):
                                q = qs[0:KROWS, bass.ds(g * G + hh, 1), lo:hi].rearrange("r o t -> r (o t)")
                                if window:
                                    at = (hh % 2) * WIDE - kt * P
                                    dst = core.psum[:, 2 * (m % 2) + hh // 2, at + lo:at + hi]
                                    pe.matmul(dst, k, q, start=(hh % 2 == 0 and lo == kt * P), stop=False, skip_group_check=True)
                                else:
                                    pe.matmul(flat(2 * (m % 2))[:, lo:hi], k, q, start=True, stop=lo != kt * P)
                            if window:
                                wd = spans(kt)[-1][1] - kt * P
                                at = (hh % 2) * WIDE
                                ins = pe.matmul(core.psum[:, 2 * (m % 2) + hh // 2, at:at + wd], mask("ident"), mask("band")[:, 0:wd],
                                                start=False, stop=hh % 2 == 1, skip_group_check=True)
                            else:
                                ins = pe.matmul(flat(2 * (m % 2))[:, kt * P:(kt + 1) * P], mask("ident"), mask("past_query"), start=False, stop=True)
                            if not window or hh == G - 1:
                                ins.then_inc(score_pe, 1)

                    def values(kt):
                        if kt == 0:
                            pe.wait_ge(vslot_ready, n + 1)
                            pe.wait_ge(o_copied, n + 1)
                        pe.wait_ge(probs_ready, n * (KT * SCORES) + (kt + 1) * SCORES + 1)
                        for lo, hi in spans(kt):
                            fresh = kt == 0 or bool(window and lo == CH and kt * P < CH)
                            off = kt * P if window else 0
                            for hh in range(G):
                                ins = pe.matmul(flat(O_BANK)[32 * hh:32 * hh + 32, lo:hi], vslot[:, kt, hh if VH == G else 0, :],
                                                probs[:, kt % 2, hh, lo - off:hi - off], start=fresh, stop=kt == KT - 1,
                                                tile_position=(0, 32 * hh), skip_group_check=True)
                        ins.then_inc(pv_pe, 1)

                    scores(0)
                    for kt in range(1, KT):
                        scores(kt)
                        values(kt - 1)
                    values(KT - 1)
                    pe.wait_ge(o_copied, n + 2)
                    pe.wait_ge(o_ready, n + 1)
                    for t in range(KT):
                        ins = pe.transpose(flat(T_BANK)[:, t * P:(t + 1) * P], o[:, t * P:(t + 1) * P], core.c("ident"))
                    ins.then_inc(o_turned, 1)
                pe.wait_ge(o_turned, b * GROUPS + GROUPS)
                pe.sem_inc(stack_free, 1)
            pe.wait_ge(w_out_in, 16)
            pe.wait_ge(o_ready, NB * GROUPS + 1)
            for c in range(NC):
                if c >= 2:
                    pe.wait_ge(oT_ready, c - 1)
                for t in range(TPC):
                    ins = pe.transpose(core.psum[:, c % 2, t * P:(t + 1) * P], otok[:, TPC * c + t, :], core.c("ident"))
                ins.then_inc(oT_pe, 1)
            for c in range(NC):
                pe.wait_ge(oT_ready, c + 1)
                if c >= 2:
                    pe.wait_ge(y_added, c - 1)
                for t in range(TPC):
                    dst = core.psum[:, 2 + c % 2, t * P:(t + 1) * P]
                    if b_out is not None:
                        pe.matmul(dst, b_out[0], b_out[1], start=True, stop=False)
                    ins = pe.matmul(dst, core.xnT[:, c * CH + t * P:c * CH + (t + 1) * P], w_out, start=b_out is None, stop=True)
                ins.then_inc(y_pe, 1)

        @block.scalar
        def _(act):
            act.sem_inc(probs_ready, 1)
            with act.Fori(0, NB) as b:
                with act.Fori(0, GROUPS) as g:
                    n = b * GROUPS + g
                    for kt in range(KT):
                        act.wait_ge(pv_pe, n * KT + max(kt, 1))
                        for hh in range(SCORES):
                            m = kt * SCORES + hh
                            act.wait_ge(score_pe, n * (KT * SCORES) + m + 1)
                            if window:
                                wd = spans(kt)[-1][1] - kt * P
                                src = core.psum[:, 2 * (m % 2):2 * (m % 2) + 2, 0:2 * WIDE].rearrange("p b (h q) -> p b h q", q=WIDE)[:, :, :, 0:wd]
                                dst = probs[:, kt % 2, :, 0:wd].rearrange("p (b h) q -> p b h q", b=2)
                            else:
                                src, dst = flat(2 * (m % 2))[:, kt * P:T], probs[:, kt % 2, hh, kt * P:T]
                            act.activation(dst, src, ACT.Exp, scale=SCALE).then_inc(probs_ready, 1)
            for c in range(NC):
                act.wait_ge(oT_pe, c + 1)
                act.activation(core.xnT[:, c * CH:(c + 1) * CH], core.psum[:, c % 2, :], ACT.Copy).then_inc(oT_ready, 1)

        @block.vector
        def _(v):
            v.sem_inc(max_read, 1)
            v.sem_inc(o_copied, 1)
            v.sem_inc(o_ready, 1)
            with v.Fori(0, NB) as b:
                if guard:
                    with v.Fori(0, HEADS) as h:
                        for qt in range(KT):
                            v.wait_ge(max_pe, (b * HEADS + h) * KT + qt + 1)
                            v.tensor_reduce(most[:, bass.ds(h, 1), qt], flat(2 * (qt % 2))[:, 0:(qt + 1) * P], AX.X, ALU.max).then_inc(max_read, 1)

                    def step(ins, k):
                        ins.then_inc(max_step, 1)
                        if k < 6:
                            v.wait_ge(max_step, b * 6 + k)

                    v.wait_ge(max_read, b * (HEADS * KT) + HEADS * KT + 1)
                    m2 = most[:, :, :].rearrange("p h k -> p (h k)")
                    step(v.tensor_scalar(m2, m2, -1.0, None, ALU.mult), 1)
                    v.wait_ge(max_turned, b + 1)
                    rest = core.psum[:, T_BANK, 0:P]
                    for p in range(Split.PARTS):
                        step(v.tensor_copy(most_parts[:, p, :], rest), 2 + 2 * p)
                        if p < Split.PARTS - 1:
                            step(v.tensor_tensor(mostT[:, p, :], rest, most_parts[:, p, :], ALU.subtract), 3 + 2 * p)
                            rest = mostT[:, p, :]
                with v.Fori(0, GROUPS) as g:
                    n = b * GROUPS + g
                    v.wait_ge(pv_pe, n * KT + KT + 1)
                    v.wait_ge(o_ready, n + 1)
                    v.tensor_copy(o[:, :], flat(O_BANK)).then_inc(o_copied, 1)
                    v.wait_ge(o_turned, n + 1)
                    turned = flat(T_BANK).rearrange("p (t h f) -> p t h f", h=G, f=32)
                    v.reciprocal(sums[:, :, :], turned[:, :, :, HD]).then_inc(sums_ready, 1)
                    v.wait_ge(sums_ready, n + 1)
                    dst = otok[:, bass.ds(b * KT, KT), bass.ds(g * (G * HD), G * HD)].rearrange("p t (h d) -> p t h d", d=HD)
                    v.tensor_tensor(dst, turned[:, :, :, 0:HD], sums[:, :, :].unsqueeze(3).broadcast_to([P, KT, G, HD]), ALU.mult).then_inc(o_ready, 1)
            for c in range(NC):
                v.wait_ge(y_pe, c + 1)
                tiles = slice(TPC * c, TPC * (c + 1))
                y = core.psum[:, 2 + c % 2, :].rearrange("p (t d) -> p t d", d=D)
                dst = addends[0]
                if len(addends) == 2:
                    v.tensor_tensor(dst[:, tiles, :], dst[:, tiles, :], addends[1][:, tiles, :], ALU.add).then_inc(sums_ready, 1)
                    v.wait_ge(sums_ready, NB * GROUPS + c + 1)
                v.tensor_tensor(dst[:, tiles, :], dst[:, tiles, :], y, ALU.add).then_inc(y_added, 1)


def channels_stage(core, w4, w4_in, tag):
    nc = core.nc
    SCALE = 1.0 / T ** 0.5
    KT = T // P
    S_BANK, M_BANK = (4, 5), (6, 7)

    def w(name, rows=P):
        a, n = L2A_COLS[name]
        return w4[0:rows, a:a + n]

    with ExitStack() as ctx:
        xr = core.sb(ctx, tag + "xr", [P, NT, D])
        ln = Norm(core, ctx, tag, core.xn, xr)
        qk = core.sb(ctx, tag + "qk", [P, NT, 2, D])
        vT = core.sb(ctx, tag + "vT", [P, N])
        prob = core.sb(ctx, tag + "prob", [P, NB, D])
        mixed = core.sb(ctx, tag + "mixed", [P, NB, D])
        most = core.sb(ctx, tag + "most", [P, NB])
        total = core.sb(ctx, tag + "total", [P, NB])
        qk_pe = core.sem(ctx, tag + "qk_pe")
        qk_ready = core.sem(ctx, tag + "qk_ready")
        v_pe = core.sem(ctx, tag + "v_pe")
        v_ready = core.sem(ctx, tag + "v_ready")
        score_pe = core.sem(ctx, tag + "score_pe")
        dve_step = core.sem(ctx, tag + "dve_step")
        most_ready = core.sem(ctx, tag + "most_ready")
        exps = core.sem(ctx, tag + "exps")
        prob_ready = core.sem(ctx, tag + "prob_ready")
        mixed_pe = core.sem(ctx, tag + "mixed_pe")
        mixed_ready = core.sem(ctx, tag + "mixed_ready")
        y_pe = core.sem(ctx, tag + "y_pe")
        y_added = core.sem(ctx, tag + "y_added")
        block = core.block(ctx)

        @block.gpsimd
        def _(g):
            ln.pool(g)

        @block.tensor
        def _(pe):
            pe.wait_ge(w4_in, 16)

            def score(t):
                pe.wait_ge(qk_ready, t + 1)
                ins = pe.matmul(core.psum[:, S_BANK[t // KT], 0:D], qk[:, t, 0, :], qk[:, t, 1, :], start=t % KT == 0, stop=t % KT == KT - 1)
                if t % KT == KT - 1:
                    ins.then_inc(score_pe, 1)

            ln.tensor(pe, 0)
            for c in range(NC):
                if c + 1 < NC:
                    ln.tensor(pe, c + 1)
                pe.wait_ge(ln.xnT_ready, c + 1)
                if c >= 2:
                    pe.wait_ge(v_ready, c - 1)
                pe.matmul(core.psum[:, 2 + c % 2, :], w("vT"), core.xnT[:, c * CH:(c + 1) * CH], start=True, stop=True).then_inc(v_pe, 1)
                for t in range(TPC * c, TPC * (c + 1)):
                    if t >= 2:
                        pe.wait_ge(qk_ready, t - 1)
                    dst = core.psum[:, t % 2, 0:2 * D]
                    pe.matmul(dst, w("ones", 1), w("qk_b", 1), start=True, stop=False)
                    pe.matmul(dst, core.xnT[:, t * P:(t + 1) * P], w("qkT"), start=False, stop=True).then_inc(qk_pe, 1)
                    if t:
                        score(t - 1)
            score(NT - 1)
            for b in range(NB):
                pe.wait_ge(prob_ready, b + 1)
                pe.matmul(core.psum[:, M_BANK[b], 0:D], prob[:, b, :], w("projT"), start=True, stop=True).then_inc(mixed_pe, 1)
            for c in range(NC):
                b = c // (NC // NB)
                pe.wait_ge(mixed_ready, b + 1)
                pe.wait_ge(v_ready, c + 1)
                if c >= 2:
                    pe.wait_ge(y_added, c - 1)
                for t in range(TPC):
                    dst = core.psum[:, c % 2, t * P:(t + 1) * P]
                    pe.matmul(dst, w("ones", 1), w("proj_b", 1), start=True, stop=False)
                    ins = pe.matmul(dst, vT[:, c * CH + t * P:c * CH + (t + 1) * P], mixed[:, b, :], start=False, stop=True)
                ins.then_inc(y_pe, 1)

        @block.scalar
        def _(act):
            act.wait_ge(w4_in, 16)
            for c in range(NC):
                ln.scalar(act, c, gain=w("norm_w"), bias=w("norm_b"))
                act.wait_ge(v_pe, c + 1)
                act.activation(vT[:, c * CH:(c + 1) * CH], core.psum[:, 2 + c % 2, :], ACT.Identity, bias=w("v_b")).then_inc(v_ready, 1)
            for b in range(NB):
                act.wait_ge(most_ready, b + 1)
                act.activation(prob[:, b, :], core.psum[:, S_BANK[b], 0:D], ACT.Exp, bias=most[:, b:b + 1], scale=SCALE,
                               accum_out=total[:, b:b + 1]).then_inc(exps, 1)
            for b in range(NB):
                act.wait_ge(mixed_pe, b + 1)
                act.activation(mixed[:, b, :], core.psum[:, M_BANK[b], 0:D], ACT.Copy).then_inc(mixed_ready, 1)

        @block.vector
        def _(v):
            s = Steps(v, dve_step)
            ln.vector(v)
            for t in range(NT):
                v.wait_ge(qk_pe, t + 1)
                v.tensor_copy(qk[:, t, :, :].rearrange("p i d -> p (i d)"), core.psum[:, t % 2, 0:2 * D]).then_inc(qk_ready, 1)
            for b in range(NB):
                v.wait_ge(score_pe, b + 1)
                s.chain(v.tensor_reduce(most[:, b:b + 1], core.psum[:, S_BANK[b], 0:D], AX.X, ALU.max))
                v.tensor_scalar(most[:, b:b + 1], most[:, b:b + 1], -SCALE, None, ALU.mult).then_inc(most_ready, 1)
            added = []
            for c in range(NC):
                tiles = slice(TPC * c, TPC * (c + 1))
                added.append(s.did(v.tensor_tensor(core.x[:, tiles, :], core.x[:, tiles, :], core.xn[:, tiles, :], ALU.add)))
            for b in range(NB):
                v.wait_ge(exps, b + 1)
                s.chain(v.reciprocal(total[:, b:b + 1], total[:, b:b + 1]))
                v.tensor_scalar(prob[:, b, :], prob[:, b, :], total[:, b:b + 1], None, ALU.mult).then_inc(prob_ready, 1)
            for c in range(NC):
                tiles = slice(TPC * c, TPC * (c + 1))
                v.wait_ge(y_pe, c + 1)
                s.after(added[c])
                v.tensor_tensor(core.x[:, tiles, :], core.x[:, tiles, :], core.psum[:, c % 2, :].rearrange("p (t d) -> p t d", d=D), ALU.add).then_inc(y_added, 1)


def top4_stage(core, w5, w5_in, select, select_in, dram_experts, tag):
    nc = core.nc
    E, TOP, CAPACITY = 32, 4, 4 * N * 4 // 32
    PAIRS = E // 2
    SLOTS = 2
    STEPS = SLOTS * NC
    PARTS = 3
    G_BANK, U_BANK, C_BANK = 4, 5, 6

    with ExitStack() as ctx:
        ln = LayerNorm(core, ctx, tag)
        logit = core.sb(ctx, tag + "logit", [P, NT, E])
        prob = core.sb(ctx, tag + "prob", [P, NT, E])
        above = core.sb(ctx, tag + "above", [P, NT, E])
        equal = core.sb(ctx, tag + "equal", [P, NT, E])
        inside = core.sb(ctx, tag + "inside", [P, NT, E])
        order = core.sb(ctx, tag + "order", [P, NT, E])
        top = core.sb(ctx, tag + "top", [P, NT, 8])
        most = core.sb(ctx, tag + "most", [P, NT])
        total = core.sb(ctx, tag + "total", [P, NT])
        places = core.sb(ctx, tag + "places", [P, NT])
        ones = core.sb(ctx, tag + "ones", [E, N])
        served = core.sb(ctx, tag + "served", [E, N])
        factor = core.sb(ctx, tag + "factor", [E, N])
        rounded = core.sb(ctx, tag + "rounded", [E, N], BF16)
        parts = core.sb(ctx, tag + "parts", [PARTS * E, N], BF16)
        slot = [core.sb(ctx, f"{tag}slot{s}", [P, 3, P]) for s in range(SLOTS + 1)]
        silu = core.sb(ctx, tag + "silu", [P, 2, CH])
        prod = core.sb(ctx, tag + "prod", [P, 2, CH])
        hid = core.sb(ctx, tag + "hid", [P, 2, CH])
        logits_pe = core.sem(ctx, tag + "logits_pe")
        set_up = core.sem(ctx, tag + "set_up")
        dve_step = core.sem(ctx, tag + "dve_step")
        shifted = core.sem(ctx, tag + "shifted")
        exps = core.sem(ctx, tag + "exps")
        chosen = core.sem(ctx, tag + "chosen")
        chosen_pe = core.sem(ctx, tag + "chosen_pe")
        factor_ready = core.sem(ctx, tag + "factor_ready")
        part_ready = core.sem(ctx, tag + "part_ready")
        slot_in = [core.sem(ctx, f"{tag}slot_in{s}") for s in range(SLOTS + 1)]
        slot_free = [core.sem(ctx, f"{tag}slot_free{s}") for s in range(SLOTS)]
        gate_pe = core.sem(ctx, tag + "gate_pe")
        up_pe = core.sem(ctx, tag + "up_pe")
        factor_pe = core.sem(ctx, tag + "factor_pe")
        silu_ready = core.sem(ctx, tag + "silu_ready")
        prod_ready = core.sem(ctx, tag + "prod_ready")
        hid_ready = core.sem(ctx, tag + "hid_ready")
        down_pe = core.sem(ctx, tag + "down_pe")
        block = core.block(ctx)

        def banks(a):
            return core.psum[0:E, a:a + NC, :].rearrange("p b c -> p (b c)")

        @block.gpsimd
        def _(g):
            g.memset(inside[:, :, :], 1.0).then_inc(set_up, 1)
            g.wait_ge(set_up, 1)
            g.memset(inside[:, :, 0:1], 0.0).then_inc(set_up, 1)
            g.memset(ones[:, :], 1.0).then_inc(set_up, 1)
            ln.pool(g)

        @block.sync
        def _(sp):
            for s in range(SLOTS):
                sp.sem_inc(slot_free[s], 1)
            sp.dma_start(slot[SLOTS][:, :, :], dram_experts[PAIRS]).then_inc(slot_in[SLOTS], 16)
            with sp.Fori(0, PAIRS // SLOTS) as i:
                for s in range(SLOTS):
                    sp.wait_ge(slot_free[s], i + 1)
                    sp.dma_start(slot[s][:, :, :], dram_experts[bass.ds(i * SLOTS + s, 1), :, :, :].rearrange("e p j d -> (e p) j d")).then_inc(slot_in[s], 16)

        @block.scalar
        def _(act):
            for c in range(NC):
                ln.scalar(act, c)
            act.wait_ge(shifted, 1)
            act.activation(prob[:, :, :], logit[:, :, :], ACT.Exp).then_inc(exps, 1)

            def silus(n, buf):
                act.wait_ge(gate_pe, n + 1)
                act.activation(silu[:, buf, :], core.psum[:, G_BANK, :], ACT.Silu).then_inc(silu_ready, 1)

            for p in range(PARTS):
                act.wait_ge(factor_ready, p + 1)
                act.activation(parts[p * E:(p + 1) * E, :], factor[:, :], ACT.Copy).then_inc(part_ready, 1)
            for c in range(NC):
                if c >= 2:
                    act.wait_ge(prod_ready, c - 1)
                silus(c, c % 2)
            with act.Fori(0, PAIRS // SLOTS) as i:
                for k in range(STEPS):
                    n = i * STEPS + NC + k
                    act.wait_ge(prod_ready, i * STEPS + NC + k - 1)
                    silus(n, k % 2)

        @block.tensor
        def _(pe):
            pe.wait_ge(w5_in, 16)
            pe.wait_ge(select_in, 16)
            for c in range(NC):
                ln.tensor(pe, c)
            wa, wn = L3_COLS["router"]
            for t in range(NT):
                pe.wait_ge(ln.xnT_ready, t // TPC + 1)
                ins = pe.matmul(core.psum[:, G_BANK, t * E:(t + 1) * E], core.xnT[:, t * P:(t + 1) * P], w5[:, wa:wa + wn], start=True, stop=True)
            ins.then_inc(logits_pe, 1)
            pe.wait_ge(chosen, 1)
            for t in range(NT):
                pe.transpose(banks(0)[:, t * P:(t + 1) * P], above[:, t, :], core.c("ident"))
            pe.wait_ge(chosen, 2)
            pe.wait_ge(ln.xnT_ready, NC)
            for t in range(NT):
                ins = pe.transpose(banks(4)[:, t * P:(t + 1) * P], prob[:, t, :], core.c("ident"))
            ins.then_inc(chosen_pe, 1)
            pe.wait_ge(factor_ready, 1)

            def up(n, sl, c, pair=None):
                xc = core.xnT[:, c * CH:(c + 1) * CH]
                if pair is not None or c:
                    pe.wait_ge(silu_ready, n)
                pe.matmul(core.psum[:, G_BANK, :], sl[:, 0, :], xc, start=True, stop=True).then_inc(gate_pe, 1)
                if pair is not None or c:
                    pe.wait_ge(prod_ready, n)
                pe.matmul(core.psum[:, U_BANK, :], sl[:, 1, :], xc, start=True, stop=True).then_inc(up_pe, 1)
                if pair is not None:
                    pe.wait_ge(hid_ready, n)
                    pe.matmul(core.psum[:, C_BANK, :], select[:, bass.ds(pair * P, P)], parts[:, c * CH:(c + 1) * CH],
                              start=True, stop=True).then_inc(factor_pe, 1)

            def down(n, buf, sl, c, first=False):
                pe.wait_ge(hid_ready, n + 1)
                for t in range(TPC):
                    ins = pe.matmul(core.psum[:, c, t * P:(t + 1) * P], hid[:, buf, t * P:(t + 1) * P], sl[:, 2, :],
                                    start=first and t == 0, stop=False, skip_group_check=True)
                ins.then_inc(down_pe, 1)

            shared = slot[SLOTS]
            pe.wait_ge(slot_in[SLOTS], 16)
            up(0, shared, 0)
            for c in range(1, NC):
                up(c, shared, c)
                down(c - 1, (c - 1) % 2, shared, c - 1, True)
            down(NC - 1, (NC - 1) % 2, shared, NC - 1, True)
            pe.wait_ge(part_ready, PARTS)
            with pe.Fori(0, PAIRS // SLOTS) as i:
                def at(k):
                    s, c = divmod(k, NC)
                    return i * STEPS + NC + k, s, c

                def drop(k):
                    n, s, c = at(k)
                    down(n, k % 2, slot[s], c)
                    if c == NC - 1:
                        pe.wait_ge(down_pe, n + 1)
                        pe.sem_inc(slot_free[s], 1)

                for k in range(STEPS):
                    n, s, c = at(k)
                    if c == 0:
                        pe.wait_ge(slot_in[s], i * 16 + 16)
                    up(n, slot[s], c, i * SLOTS + s)
                    if k:
                        drop(k - 1)
                drop(STEPS - 1)

        @block.vector
        def _(v):
            s = Steps(v, dve_step)
            ln.vector(v)
            v.wait_ge(logits_pe, 1)
            lp = core.psum[:, G_BANK, :].rearrange("p (t e) -> p t e", e=E)

            def wide(a):
                return a.unsqueeze(2).broadcast_to([P, NT, E])

            s.chain(v.tensor_reduce(most[:, :], lp, AX.X, ALU.max))
            v.tensor_tensor(logit[:, :, :], lp, wide(most[:, :]), ALU.subtract).then_inc(shifted, 1)
            v.wait_ge(shifted, 1)
            for t in range(NT):
                last = s.did(v.max(top[:, t, :], logit[:, t, :]))
            s.after(last)
            fourth = wide(top[:, :, TOP - 1])
            s.did(v.tensor_tensor(equal[:, :, :], logit[:, :, :], fourth, ALU.is_equal))
            s.chain(v.tensor_tensor(above[:, :, :], logit[:, :, :], fourth, ALU.is_gt))
            s.chain(v.tensor_reduce(places[:, :], above[:, :, :], AX.X, ALU.add))
            s.chain(v.tensor_scalar(places[:, :], places[:, :], -1.0, float(TOP), ALU.mult, ALU.add))
            v.wait_ge(set_up, 3)

            def flat(a):
                return a[:, :, :].rearrange("p t e -> p (t e)")

            s.chain(v.tensor_tensor_scan(flat(order), flat(inside), flat(equal), 0.0, ALU.mult, ALU.add))
            s.chain(v.tensor_tensor(order[:, :, :], order[:, :, :], wide(places[:, :]), ALU.is_le))
            s.chain(v.tensor_tensor(equal[:, :, :], equal[:, :, :], order[:, :, :], ALU.mult))
            v.tensor_tensor(above[:, :, :], above[:, :, :], equal[:, :, :], ALU.add).then_inc(chosen, 1)
            v.wait_ge(exps, 1)
            s.chain(v.tensor_reduce(total[:, :], prob[:, :, :], AX.X, ALU.add))
            s.chain(v.reciprocal(total[:, :], total[:, :]))
            s.chain(v.tensor_tensor(prob[:, :, :], prob[:, :, :], wide(total[:, :]), ALU.mult))
            v.wait_ge(chosen, 1)
            v.tensor_tensor(prob[:, :, :], prob[:, :, :], above[:, :, :], ALU.mult).then_inc(chosen, 1)
            v.wait_ge(chosen_pe, 1)
            s.chain(v.tensor_tensor_scan(served[:, :], ones[:, :], banks(0), 0.0, ALU.mult, ALU.add))
            v.scalar_tensor_tensor(factor[:, :], served[:, :], float(CAPACITY), banks(4), ALU.is_le, ALU.mult).then_inc(factor_ready, 1)
            for p in range(PARTS - 1):
                v.wait_ge(factor_ready, p + 1)
                s.chain(v.tensor_copy(rounded[:, :], factor[:, :]))
                v.wait_ge(part_ready, p + 1)
                v.tensor_tensor(factor[:, :], factor[:, :], rounded[:, :], ALU.subtract).then_inc(factor_ready, 1)

            def multiply(n, k, by_factor):
                v.wait_ge(silu_ready, n + 1)
                v.wait_ge(up_pe, n + 1)
                v.tensor_tensor(prod[:, k % 2, :], silu[:, k % 2, :], core.psum[:, U_BANK, :], ALU.mult).then_inc(prod_ready, 1)
                v.wait_ge(prod_ready, n + 1)
                if by_factor or k >= 2:
                    v.wait_ge(down_pe, n - 1)
                if by_factor:
                    v.wait_ge(factor_pe, n - NC + 1)
                    ins = v.tensor_tensor(hid[:, k % 2, :], prod[:, k % 2, :], core.psum[:, C_BANK, :], ALU.mult)
                else:
                    ins = v.tensor_copy(hid[:, k % 2, :], prod[:, k % 2, :])
                ins.then_inc(hid_ready, 1)

            for c in range(NC):
                multiply(c, c, False)
            with v.Fori(0, PAIRS // SLOTS) as i:
                for k in range(STEPS):
                    multiply(i * STEPS + NC + k, k, True)
            for c in range(NC):
                v.wait_ge(down_pe, NC + PAIRS * NC - (NC - 1 - c))
                xs = core.x[:, TPC * c:TPC * (c + 1), :].rearrange("p t d -> p (t d)")
                s.did(v.scalar_tensor_tensor(xs, core.psum[:, c, :], 0.5, xs, ALU.mult, ALU.add))


def gqa_project_stage(core, w5, w5_in, v_all, scratch, kind, tag):
    nc = core.nc
    EPS = 1e-6
    KV = 4
    QK = D + KV * HD
    VW = KV * HD
    LATENT = 32

    def w(name, rows=P):
        a, n = L3_COLS[name]
        return w5[0:rows, a:a + n]

    with ExitStack() as ctx:
        xr = core.sb(ctx, tag + "xr", [P, NT, D])
        ln = Norm(core, ctx, tag, core.xn, xr, rms=True, eps=EPS)
        sp_ = Split(core, ctx, tag, (P, VW), scratch)
        latent = core.sb(ctx, tag + "latent", [LATENT, N])
        cosed = core.sb(ctx, tag + "cosed", [P, TPC, QK])
        sined = core.sb(ctx, tag + "sined", [P, TPC, QK])
        heads = core.sb(ctx, tag + "heads", [P, 2, TPC, QK])
        square = core.sb(ctx, tag + "squares", [P, TPC, QK])
        HN = QK // HD
        mean = core.sb(ctx, tag + "mean", [P, TPC, HN])
        mhalf = core.sb(ctx, tag + "mhalf", [P, TPC, HN])
        set_up = core.sem(ctx, tag + "set_up")
        latent_pe = core.sem(ctx, tag + "latent_pe")
        latent_ready = core.sem(ctx, tag + "latent_ready")
        qkv_pe = core.sem(ctx, tag + "qkv_pe")
        v_ready = core.sem(ctx, tag + "v_ready")
        cos_step = core.sem(ctx, tag + "cos_step")
        dve_step = core.sem(ctx, tag + "dve_step")
        mean_ready = core.sem(ctx, tag + "mean_ready")
        pool_step2 = core.sem(ctx, tag + "pool_step2")
        root_ready = core.sem(ctx, tag + "root_ready")
        heads_ready = core.sem(ctx, tag + "heads_ready")
        block = core.block(ctx)
        QKV_BANK, LAT_BANK, T_BANK = (0, 1), (2, 3), (4, 5)

        @block.gpsimd
        def _(g):
            g.memset(mhalf[:, :, :], -0.5).then_inc(set_up, 1)
            ln.pool(g)
            g.wait_ge(set_up, 1)
            for c in range(NC):
                g.wait_ge(mean_ready, c + 1)
                g.tensor_scalar(mean[:, :, :], mean[:, :, :], 1.0 / HD, EPS, ALU.mult, ALU.add).then_inc(pool_step2, 1)
                g.wait_ge(pool_step2, c + 1)
                g.tensor_tensor(mean[:, :, :], mean[:, :, :], mhalf[:, :, :], ALU.pow).then_inc(root_ready, 1)

        @block.sync
        def _(sp):
            for c in range(NC):
                for i in range(2):
                    sp_.sync(sp, c, i)
            sp_.landed(sp)

        @block.tensor
        def _(pe):
            pe.wait_ge(w5_in, 16)
            for c in range(NC):
                ln.tensor(pe, c)
            if kind == "g":
                for c in range(NC):
                    pe.wait_ge(ln.xnT_ready, c + 1)
                    if c >= 2:
                        pe.wait_ge(latent_ready, c - 1)
                    pe.matmul(core.psum[0:LATENT, LAT_BANK[c % 2], :], w("g_down"), core.xnT[:, c * CH:(c + 1) * CH],
                              start=True, stop=True).then_inc(latent_pe, 1)

            def turn(c):
                pe.wait_ge(heads_ready, c + 1)
                if c:
                    pe.wait_ge(sp_.rest_ready, 4 * c - 1)
                    pe.wait_ge(sp_.part_ready, 3 * (2 * c) - 2)
                for i, (a, n) in enumerate(((0, D), (D, VW))):
                    for t in range(TPC):
                        ins = pe.transpose(core.psum[0:n, T_BANK[i], t * P:(t + 1) * P], heads[:, c % 2, t, a:a + n], core.c("ident"))
                    ins.then_inc(sp_.heads_pe, 1)

            for t in range(NT):
                if t >= 2:
                    pe.wait_ge(cos_step, 2 * (t - 1))
                    pe.wait_ge(v_ready, t - 1)
                pe.wait_ge(ln.xnT_ready, t // TPC + 1)
                xt = core.xnT[:, t * P:(t + 1) * P]
                bank = core.psum[:, QKV_BANK[t % 2], :]
                if kind == "l":
                    ins = pe.matmul(bank[:, 0:2 * QK + VW], xt, w("l_qkv"), start=True, stop=True)
                else:
                    pe.wait_ge(latent_ready, t // TPC + 1)
                    lt = latent[:, t * P:(t + 1) * P]
                    pe.matmul(bank[:, 0:D], xt, w("g_q"), start=True, stop=True)
                    pe.matmul(bank[:, QK:QK + D], xt, w("g_qr"), start=True, stop=True)
                    pe.matmul(bank[:, D:QK], lt, w("g_k", LATENT), start=True, stop=True)
                    ins = pe.matmul(bank[:, QK + D:2 * QK + VW], lt, w("g_krv", LATENT), start=True, stop=True)
                ins.then_inc(qkv_pe, 1)
                if t % TPC == 1 and t > TPC:
                    turn(t // TPC - 1)
            turn(NC - 1)

        @block.scalar
        def _(act):
            act.wait_ge(w5_in, 16)
            for c in range(NC):
                ln.scalar(act, c, gain=w("norm1" if kind == "g" else "norm2"))
            if kind == "g":
                for c in range(NC):
                    act.wait_ge(latent_pe, c + 1)
                    act.activation(latent[:, c * CH:(c + 1) * CH], core.psum[0:LATENT, LAT_BANK[c % 2], :], ACT.Copy).then_inc(latent_ready, 1)
            for t in range(NT):
                act.wait_ge(cos_step, 2 * (t + 1))
                act.activation(v_all[:, t, :], core.psum[:, QKV_BANK[t % 2], 2 * QK:2 * QK + VW], ACT.Copy).then_inc(v_ready, 1)
                if t % TPC == 2 and t > TPC:
                    for i, n in enumerate((D, VW)):
                        sp_.scalar(act, t // TPC - 1, i, core.psum[0:n, T_BANK[i], :])
            for i, n in enumerate((D, VW)):
                sp_.scalar(act, NC - 1, i, core.psum[0:n, T_BANK[i], :])

        @block.vector
        def _(v):
            v.wait_ge(w5_in, 16)
            s = Steps(v, dve_step)
            ln.vector(v)

            def table(name, t):
                a, n = L3_COLS[kind + name]
                tab = w5[:, a + (t % (T // P)) * HD:a + (t % (T // P)) * HD + HD]
                return tab.unsqueeze(1).broadcast_to([P, HN, HD])

            def split(c):
                for i, n in enumerate((D, VW)):
                    v.wait_ge(sp_.heads_pe, 2 * c + i + 1)
                    sp_.vector(v, c, i, core.psum[0:n, T_BANK[i], :])

            for c in range(NC):
                for k in range(TPC):
                    t = c * TPC + k
                    ps = core.psum[:, QKV_BANK[t % 2], :]
                    v.wait_ge(qkv_pe, t + 1)
                    if c:
                        v.wait_ge(dve_step, 2 * c)
                    for dst, a, name in ((cosed, 0, "cos"), (sined, QK, "sin")):
                        v.tensor_tensor(dst[:, k, :].rearrange("p (h d) -> p h d", d=HD), ps[:, a:a + QK].rearrange("p (h d) -> p h d", d=HD),
                                        table(name, t), ALU.mult).then_inc(cos_step, 1)
                    if k == 2 and c:
                        split(c - 1)
                hc = heads[:, c % 2, :, :]
                v.wait_ge(cos_step, 2 * TPC * (c + 1))
                s.chain(v.tensor_tensor(hc, cosed[:, :, :], sined[:, :, :], ALU.add))
                s.chain(v.tensor_tensor(square[:, :, :], hc, hc, ALU.mult))
                if c:
                    v.wait_ge(root_ready, c)
                v.tensor_reduce(mean[:, :, :], square[:, :, :].rearrange("p t (h d) -> p t h d", d=HD), AX.X, ALU.add).then_inc(mean_ready, 1)
                v.wait_ge(root_ready, c + 1)
                h4 = hc.rearrange("p t (h d) -> p (t h) d", d=HD)
                v.tensor_tensor(h4, h4, mean[:, :, :].rearrange("p t h -> p (t h)").unsqueeze(2).broadcast_to([P, TPC * HN, HD]), ALU.mult).then_inc(heads_ready, 1)
            split(NC - 1)


def store_stage(core, dram_out, loads):
    nc = core.nc
    with ExitStack() as ctx:
        stored = core.sem(ctx, "stored")
        block = core.block(ctx)

        @block.sync
        def _(sp):
            sp.dma_start(dram_out.rearrange("(t p) d -> p t d", p=P), core.x[:, :, :]).then_inc(stored, 16)
            sp.wait_ge(stored, 16)
            for _, _, sem in loads:
                sp.wait_ge(sem, 16)


def build(nc, dram, dram_out):
    with ExitStack() as ctx:
        core = Core(nc, ctx)
        w0 = core.sb(ctx, "w0", [P, L0_W])
        w1 = core.sb(ctx, "w1", [P, 8])
        w2 = core.sb(ctx, "w2", [P, L2_W])
        w3 = core.sb(ctx, "w3", [P, L1_W])
        w4 = core.sb(ctx, "w4", [P, L2A_W])
        w5 = core.sb(ctx, "w5", [P, L3_W])
        select = core.sb(ctx, "select", [96, 16 * P], BF16)
        masks = core.sb(ctx, "masks", [P, MASK_W], BF16)
        w0_in, w1_in, w2_in, w3_in, w4_in, w5_in, masks_in, select_in = (
            core.weight_sem(ctx, f"{n}_in") for n in ("w0", "w1", "w2", "w3", "w4", "w5", "masks", "select"))
        scattered = core.weight_sem(ctx, "scattered")
        gathered = [core.weight_sem(ctx, f"gathered{t}") for t in range(NT)]
        loads = [(w0[:, :], "w0", w0_in), (w1[:, :], "w1", w1_in), (w3[:, :], "w3", w3_in), (masks[:, :].bitcast(U16), "masks", masks_in),
                 (w2[:, :], "w2", w2_in), (w4[:, :], "w4", w4_in), (w5[:, :], "w5", w5_in), (select[:, :].bitcast(U16), "select", select_in)]
        scratch = [nc.dram_tensor(f"scratch_{n}", (Split.PARTS, NB, P, T), BF16, kind="Internal").ap() for n in "qk"]
        scratch3 = [scratch[0], nc.dram_tensor("scratch_k3", (Split.PARTS, NB, 4 * HD, T), BF16, kind="Internal").ap()]

        def part(tile, cols):
            def of(name, rows=P):
                a, n = cols[name]
                return tile[0:rows, a:a + n]
            return of

        w3_, w5_ = part(w3, L1_COLS), part(w5, L3_COLS)
        BLOCKS = N // P + 6
        sorted_x = nc.dram_tensor("sorted_x", ((BLOCKS + 1) * P, D), F32, kind="Internal").ap()
        sorted_y = nc.dram_tensor("sorted_y", (BLOCKS * P, D), F32, kind="Internal").ap()
        load_stage(core, dram, loads, sorted_x)
        coupling_stage(core, w0, w0_in, "c1_")
        scan_stage(core, w0, "s_")
        coupling_stage(core, w0, w0_in, "c2_")
        top1_stage(core, w1, w1_in, dram["experts1"], sorted_x, sorted_y, scattered, gathered, 0, "m1_")
        with ExitStack() as actx:
            v_all = core.sb(actx, "a1_v_all", [P, NT, D])
            rope_project_stage(core, w3, w3_in, v_all, scratch, "p1_")
            attend_stage(core, masks, masks_in, v_all, scratch, HEADS, True, w3_("o"), w3_in, (w3_("ones", 1), w3_("o_b", 1)), core.x, "a1_")
        top1_stage(core, w1, w1_in, dram["experts1"], sorted_x, sorted_y, scattered, gathered, 1, "m2_")
        mlp_stage(core, w2, w2_in, "f1_")
        norm_stage(core, "n1_")
        channels_stage(core, w4, w4_in, "h_")
        mlp_stage(core, w2, w2_in, "f2_")
        top4_stage(core, w5, w5_in, select, select_in, dram["experts3"], "t1_")
        norm_stage(core, "n2_")
        for kind in "gl":
            with ExitStack() as actx:
                v_all = core.sb(actx, kind + "_v_all", [P, NT, 32])
                gqa_project_stage(core, w5, w5_in, v_all, scratch3, kind, kind + "p_")
                if kind == "g":
                    attend_stage(core, masks, masks_in, v_all, scratch3, 4, False, w5_("g_o"), w5_in, None, core.xn, "ga_")
                else:
                    attend_window_stage(core, masks, masks_in, v_all, scratch3, 4, False, 32, w5_("l_o"), w5_in, None, [core.x, core.xn], "la_")
        top4_stage(core, w5, w5_in, select, select_in, dram["experts3"], "t2_")
        store_stage(core, dram_out, loads)



def packed(cols, width, parts):
    out = np.zeros((P, width), np.float32)
    for name, a in parts.items():
        at, w = cols[name]
        a = np.asarray(a)
        if a.ndim == 1:
            a = a[:, None] if w == 1 else np.broadcast_to(a[None, :], (P, w))
        out[:a.shape[0], at:at + a.shape[1]] = a
    return out


def bfloat16_bits(constants):
    return np.ascontiguousarray(constants, dtype=np.float32).view(np.uint16)[:, 1::2]


def laid_out(i):
    eye = np.eye(P, dtype=np.float32)
    q = P // 4
    twist = np.zeros((P, P), np.float32)
    for dst, src, sign in ((0, 2, 1), (1, 3, -1), (2, 0, -1), (3, 1, 1)):
        twist[src * q:(src + 1) * q, dst * q:(dst + 1) * q] = sign * np.eye(q)
    i = {k: np.asarray(v) for k, v in i.items()}

    def rep(v, n=P):
        return np.broadcast_to(v.reshape(1, -1), (n, v.size))

    a = {"x": i["L0_attn_x"].reshape(N, D)}
    a["const"] = packed(CONST_COLS, CONST_W, {
        "ident": eye, "twist": twist, "first8": np.broadcast_to(np.arange(8, 0, -1, dtype=np.float32), (P, 8)),
        "earlier": np.triu(np.ones((P, P)), 1), "ones": np.ones((P, P)), "block_start": P * np.broadcast_to(np.arange(NT + 8), (P, NT + 8))})
    a["w0"] = packed(L0_COLS, L0_W, {
        "cn_w1": i["L0_ffn_cn_w1"], "cn_w2": i["L0_ffn_cn_w2"], "cn_w3": i["L0_ffn_cn_w3"],
        "cn_w4": np.broadcast_to(i["L0_ffn_cn_w4"], (32, P)),
        "gc_w1": i["L0_ffn_gc_w1"], "gc_w2": i["L0_ffn_gc_w2"], "gc_w3": np.broadcast_to(i["L0_ffn_gc_w3"], (32, P)),
        "cn_b1": i["L0_ffn_cn_b1"], "cn_b2": i["L0_ffn_cn_b2"], "cn_b3": i["L0_ffn_cn_b3"], "cn_b4": rep(i["L0_ffn_cn_b4"]),
        "gc_b1": i["L0_ffn_gc_b1"], "gc_b2": i["L0_ffn_gc_b2"], "gc_b3": rep(i["L0_ffn_gc_b3"]),
        "range": rep(i["L0_ffn_adaptive_range"]), "B_wT": i["L0_attn_B_w"].T, "C_wT": i["L0_attn_C_w"].T,
        "C_b": rep(i["L0_attn_C_b"]), "log_A": i["L0_attn_log_A"], "B_b": i["L0_attn_B_b"]})
    def hidden(w, shared):
        both = np.concatenate([w, shared[None]])
        return both.reshape(8, P, 4, P)

    down = np.concatenate([i["L1_ffn_down_w"], i["L1_ffn_shared_down_w"][None]]).reshape(8, 4, P, P).transpose(0, 2, 1, 3)
    a["experts1"] = np.concatenate([hidden(i["L1_ffn_gate_w"], i["L1_ffn_shared_gate_w"]),
                                    hidden(i["L1_ffn_up_w"], i["L1_ffn_shared_up_w"]), down], axis=2)
    a["w1"] = i["L1_ffn_router_w"]

    def half_turned(wT):
        return np.roll(wT.reshape(-1, HEADS, HD), HD // 2, axis=2).reshape(wT.shape)

    def rope_tables(base, interleaved):
        f32 = np.float32
        inv = f32(1.0) / np.power(f32(base), np.arange(0, HD, 2, dtype=f32) / f32(HD))
        angle = np.arange(T, dtype=f32)[:, None] * inv[None, :].astype(f32)
        cos, sin = np.cos(angle), np.sin(angle)
        if interleaved:
            both = [np.stack(z, axis=-1).reshape(T, HD) for z in ((cos, cos), (-sin, sin))]
        else:
            both = [np.concatenate(z, axis=-1) for z in ((cos, cos), (-sin, sin))]
        return [z.reshape(T // P, P, HD).transpose(1, 0, 2).reshape(P, -1) for z in both]

    cos, sin = rope_tables(10000.0, False)
    wq, wk, wv, wo = (i[f"L1_attn_W{n}"].T for n in "qkvo")
    bq, bk = i["L1_attn_bq"], i["L1_attn_bk"]
    a["w3"] = packed(L1_COLS, L1_W, {
        "qk": np.concatenate([wq, half_turned(wq), wk, half_turned(wk)], axis=1),
        "qk_b": np.concatenate([bq, half_turned(bq[None])[0], bk, half_turned(bk[None])[0]])[None],
        "v": wv, "v_b": i["L1_attn_bv"][None], "o": wo, "o_b": i["L1_attn_bo"][None], "ones": np.ones((1, P), np.float32), "cos": cos, "sin": sin})
    p, f = np.arange(P)[:, None], np.arange(P + 32)[None, :]
    NEVER = -1e30
    a["masks"] = bfloat16_bits(packed(MASK_COLS, MASK_W, {
        "ident": eye, "future_key": np.where(f[:, :P] > p, NEVER, 0), "past_query": np.where(f[:, :P] < p, NEVER, 0),
        "band": np.where((f >= p) & (f - p < 32), 0, NEVER)}))

    def tiles(wT):
        return wT.reshape(-1, P, wT.shape[1]).transpose(1, 0, 2).reshape(P, -1)

    E3 = 32
    cols = lambda z: z.reshape(E3 // 2, 2, P, 64).transpose(0, 2, 1, 3).reshape(E3 // 2, P, P)
    pairs = np.stack([cols(i["L3_ffn_W1"]), cols(i["L3_ffn_W3"]), i["L3_ffn_W2"].reshape(E3 // 2, P, D)], axis=2)
    shared = np.stack([i["L3_ffn_Ws1"], i["L3_ffn_Ws3"], i["L3_ffn_Ws2"]], axis=1)[None]
    a["experts3"] = np.concatenate([pairs, shared])
    e, col = np.arange(3 * E3)[:, None] % E3, np.arange(E3 // 2 * P)[None, :]
    a["select"] = bfloat16_bits(e == 2 * (col // P) + col % P // 64)

    def turned(z):
        return z.reshape(z.shape[0], -1, 2)[:, :, ::-1].reshape(z.shape)

    gk, gv, lq, lk = i["L3_attn_g_k_up"], i["L3_attn_g_v_up"], i["L3_attn_l_wq"], i["L3_attn_l_wk"]
    (gcos, gsin), (lcos, lsin) = rope_tables(1000000.0, True), rope_tables(10000.0, True)
    a["w5"] = packed(L3_COLS, L3_W, {
        "router": i["L3_ffn_Wg"], "g_q": i["L3_attn_g_wq"], "g_qr": turned(i["L3_attn_g_wq"]), "g_down": i["L3_attn_g_kv_down"],
        "g_k": gk, "g_krv": np.concatenate([turned(gk), gv], axis=1), "g_o": i["L3_attn_g_wo"],
        "l_qkv": np.concatenate([lq, lk, turned(lq), turned(lk), i["L3_attn_l_wv"]], axis=1), "l_o": i["L3_attn_l_wo"],
        "gcos": gcos, "gsin": gsin, "lcos": lcos, "lsin": lsin, "norm1": i["L3_attn_norm1_w"], "norm2": i["L3_attn_norm2_w"]})
    qkvT, qkv_b = i["L2_attn_qkv_w"].T, i["L2_attn_qkv_b"]
    a["w4"] = packed(L2A_COLS, L2A_W, {
        "qkT": qkvT[:, :256], "vT": qkvT[:, 256:], "projT": i["L2_attn_proj_w"].T, "qk_b": qkv_b[None, :256], "proj_b": i["L2_attn_proj_b"][None],
        "ones": np.ones((1, P), np.float32), "v_b": qkv_b[256:], "norm_w": i["L2_attn_norm_w"], "norm_b": i["L2_attn_norm_b"]})

    def per_tile(s):
        return s.reshape(-1, P).T

    a["w2"] = packed(L2_COLS, L2_W, {
        "w1T": i["L2_ffn_w1_w"].T, "w2T": i["L2_ffn_w2_w"].T, "h1T": tiles(i["L2_ffn_h1_w"].T), "h2T": tiles(i["L2_ffn_h2_w"].T),
        "w3T": tiles(i["L2_ffn_w3_w"].T), "s3": rep(i["L2_ffn_w3_s"]), "s1": per_tile(i["L2_ffn_w1_s"]), "s2": per_tile(i["L2_ffn_w2_s"]),
        "sh1": per_tile(i["L2_ffn_h1_s"]), "sh2": per_tile(i["L2_ffn_h2_s"])})
    return {k: np.ascontiguousarray(v) for k, v in a.items()}


def kernel(**inputs):
    import concourse.bacc as bacc
    from concourse.bass_utils import run_bass_kernel_spmd

    arrays = {f"{k}_dram": v for k, v in laid_out(inputs).items()}
    nc = bacc.Bacc("TRN2", target_bir_lowering=False, num_devices=1)
    dram = {k[:-5]: nc.dram_tensor(k, v.shape, mybir.dt.from_np(v.dtype), kind="ExternalInput").ap() for k, v in arrays.items()}
    out = nc.dram_tensor("out_dram", (NB, T, D), F32, kind="ExternalOutput").ap()
    build(nc, dram, out.rearrange("b t d -> (b t) d"))
    r = run_bass_kernel_spmd(nc, [arrays], core_ids=[0])
    return r.results[0]["out_dram"]
```

```python
from contextlib import ExitStack

import numpy as np

import concourse.bass as bass
from concourse import mybir

ALU = mybir.AluOpType
ACT = mybir.ActivationFunctionType
AX = mybir.AxisListType
F32 = mybir.dt.float32
BF16 = mybir.dt.bfloat16
U16 = mybir.dt.uint16
I32 = mybir.dt.int32

P = 128
D = 128
NB, T = 2, 1024
N = NB * T
NT = N // P
CH = 512
NC = N // CH
TPC = CH // P
LN_EPS = 1e-5


def columns(widths):
    at, out = 0, {}
    for name, w in widths:
        out[name] = (at, w)
        at += w
    return out, at


L0_COLS, L0_W = columns([
    ("cn_w1", 128), ("cn_w2", 64), ("cn_w3", 128), ("cn_w4", 128), ("gc_w1", 64), ("gc_w2", 32), ("gc_w3", 128),
    ("cn_b1", 1), ("cn_b2", 1), ("cn_b3", 1), ("cn_b4", 1), ("gc_b1", 1), ("gc_b2", 1), ("gc_b3", 1),
    ("range", 1), ("B_wT", 128), ("C_wT", 128), ("C_b", 128), ("log_A", 1), ("B_b", 1)])
L1_COLS, L1_W = columns([
    ("qk", 512), ("v", 128), ("qk_b", 512), ("v_b", 128), ("o", 128), ("o_b", 128), ("ones", 128), ("cos", 64), ("sin", 64)])
MASK_COLS, MASK_W = columns([("ident", 128), ("future_key", 128), ("past_query", 128), ("band", 160)])
L2A_COLS, L2A_W = columns([
    ("qkT", 256), ("vT", 128), ("projT", 128), ("qk_b", 256), ("proj_b", 128), ("v_b", 1), ("norm_w", 1), ("norm_b", 1)])
L3_COLS, L3_W = columns([
    ("router", 32), ("g_q", 128), ("g_qr", 128), ("g_down", 32), ("g_k", 32), ("g_krv", 64), ("g_o", 128), ("l_qkv", 352), ("l_o", 128),
    ("gcos", 64), ("gsin", 64), ("lcos", 64), ("lsin", 64), ("norm1", 1), ("norm2", 1)])
L2_COLS, L2_W = columns([
    ("w1T", 512), ("w2T", 512), ("h1T", 2048), ("h2T", 2048), ("w3T", 512), ("s3", 128), ("s1", 4), ("s2", 4), ("sh1", 4), ("sh2", 4)])
CONST_COLS, CONST_W = columns([("ident", 128), ("twist", 128), ("first8", 8), ("earlier", 128), ("ones", 128), ("block_start", NT + 8)])


class Steps:

    def __init__(self, eng, sem):
        self.eng, self.sem, self.n = eng, sem, 0

    def did(self, ins):
        ins.then_inc(self.sem, 1)
        self.n += 1
        return self.n

    def after(self, n):
        self.eng.wait_ge(self.sem, n)

    def chain(self, ins):
        self.after(self.did(ins))


class Core:

    def __init__(self, nc, ctx):
        self.nc, self.ctx = nc, ctx
        self.stage_sems = []
        self.x = self.sb(ctx, "x", [P, NT, D])
        self.xn = self.sb(ctx, "xn", [P, NT, D])
        self.xnT = self.sb(ctx, "xnT", [P, N])
        self.stats = self.sb(ctx, "stats", [P, NT, 6])
        self.meanvar = self.sb(ctx, "meanvar", [P, NT, 2])
        self.rstd = self.sb(ctx, "rstd", [P, NT])
        self.zero = self.sb(ctx, "zero", [P, D])
        self.mhalf = self.sb(ctx, "mhalf", [P, NT])
        self.const = self.sb(ctx, "const", [P, CONST_W])
        self.psum = ctx.enter_context(nc.psum_tensor("psum", [P, 8, CH], F32))

    def sb(self, ctx, name, shape, dt=F32):
        return ctx.enter_context(self.nc.sbuf_tensor(name, shape, dt))

    def weight_sem(self, ctx, name):
        s = ctx.enter_context(self.nc.semaphore(name))
        self.first_stage_sem = s.num + 1
        return s

    def sem(self, ctx, name):
        s = self.nc.alloc_semaphore(name, num=self.first_stage_sem + len(self.stage_sems))
        self.stage_sems.append(s)
        return s

    def block(self, ctx):
        sems, self.stage_sems = self.stage_sems, []

        def close():
            self.nc.all_engine_barrier(sems_to_clear=range(sems[0].num, sems[-1].num + 1))
            for s in sems:
                self.nc.release_semaphore(s)

        ctx.callback(close)
        return ctx.enter_context(self.nc.Block())

    def c(self, name):
        a, w = CONST_COLS[name]
        return self.const[:, a:a + w]


class LayerNorm:

    BANKS = (6, 7)

    def __init__(self, core, ctx, tag):
        self.k = core
        self.var_ready = core.sem(ctx, tag + "var_ready")
        self.eps_added = core.sem(ctx, tag + "eps_added")
        self.rstd_ready = core.sem(ctx, tag + "rstd_ready")
        self.stat_step = core.sem(ctx, tag + "stat_step")
        self.xn_ready = core.sem(ctx, tag + "xn_ready")
        self.turned = core.sem(ctx, tag + "turned")
        self.xnT_ready = core.sem(ctx, tag + "xnT_ready")

    def vector(self, v):
        k = self.k

        def statistics(c):
            tiles = range(TPC * c, TPC * (c + 1))
            for t in tiles:
                v.bn_stats(k.stats[:, t, :], k.x[:, t, :]).then_inc(self.stat_step, 1)
            for t in tiles:
                v.wait_ge(self.stat_step, t + 1)
                ins = v.bn_aggr(k.meanvar[:, t, :], k.stats[:, t, :])
                ins.then_inc(self.var_ready, 1)

        def normalise(c):
            v.wait_ge(self.var_ready, TPC * (c + 1))
            v.wait_ge(self.rstd_ready, c + 1)
            for t in range(TPC * c, TPC * (c + 1)):
                v.tensor_scalar(k.xn[:, t, :], k.x[:, t, :], k.meanvar[:, t, 0:1], k.rstd[:, t:t + 1],
                                ALU.subtract, ALU.mult).then_inc(self.xn_ready, 1)

        statistics(0)
        for c in range(NC):
            if c + 1 < NC:
                statistics(c + 1)
            normalise(c)

    def pool(self, g):
        k = self.k
        for c in range(NC):
            a, b = TPC * c, TPC * (c + 1)
            g.wait_ge(self.var_ready, b)
            g.tensor_scalar(k.rstd[:, a:b], k.meanvar[:, a:b, 1], LN_EPS, None, ALU.add).then_inc(self.eps_added, 1)
            g.wait_ge(self.eps_added, c + 1)
            g.tensor_tensor(k.rstd[:, a:b], k.rstd[:, a:b], k.mhalf[:, a:b], ALU.pow).then_inc(self.rstd_ready, 1)

    def tensor(self, pe, c):
        k = self.k
        if c >= 2:
            pe.wait_ge(self.xnT_ready, c - 1)
        for t in range(TPC):
            pe.wait_ge(self.xn_ready, TPC * c + t + 1)
            ins = pe.transpose(k.psum[:, self.BANKS[c % 2], t * P:(t + 1) * P], k.xn[:, TPC * c + t, :], k.c("ident"))
        ins.then_inc(self.turned, 1)

    def scalar(self, act, c):
        k = self.k
        act.wait_ge(self.turned, c + 1)
        act.activation(k.xnT[:, c * CH:(c + 1) * CH], k.psum[:, self.BANKS[c % 2], :], ACT.Copy).then_inc(self.xnT_ready, 1)


def load_stage(core, dram, loads, sorted_x, cleared):
    nc = core.nc
    with ExitStack() as ctx:
        K = sorted_x.shape[0] // P
        x_in = core.sem(ctx, "x_in")
        mhalf_set = core.sem(ctx, "mhalf_set")
        zero_set = core.sem(ctx, "zero_set")
        block = core.block(ctx)

        @block.sync
        def _(sp):
            sp.dma_start(core.x[:, :, :], dram["x"].rearrange("(t p) d -> p t d", p=P)).then_inc(x_in, 16)
            sp.dma_start(core.const[:, :], dram["const"]).then_inc(x_in, 16)
            sp.wait_ge(zero_set, 1)
            sp.dma_start(sorted_x.rearrange("(k p) d -> p k d", p=P), core.zero[:, :].unsqueeze(1).broadcast_to([P, K, D])).then_inc(cleared, 16)
            sp.wait_ge(x_in, 32)

        @block.scalar
        def _(act):
            for tile, name, sem in loads:
                act.dma_start(tile, dram[name]).then_inc(sem, 16)

        @block.vector
        def _(v):
            v.memset(core.zero[:, :], 0.0).then_inc(zero_set, 1)

        @block.gpsimd
        def _(g):
            g.memset(core.mhalf[:, :], -0.5).then_inc(mhalf_set, 1)
            g.wait_ge(mhalf_set, 1)


def coupling_stage(core, w0, w0_in, tag):
    nc = core.nc
    CYCLES, LAYERS = 3, 5
    SUMS = 1.0 / T
    TANHS = [1] + [2 * c for c in range(1, NC)]
    GATES = [2 * c + 3 for c in range(NC - 1)] + [2 * NC]

    def w(name, rows=P):
        a, n = L0_COLS[name]
        return w0[0:rows, a:a + n]

    with ExitStack() as ctx:
        ln = LayerNorm(core, ctx, tag)
        hid = [core.sb(ctx, f"{tag}hid{i}", [r, NC, CH]) for i, r in enumerate((128, 64, 128))]
        gate = core.sb(ctx, tag + "gate", [P, NC, CH])
        prod = core.sb(ctx, tag + "prod", [P, NC, CH])
        ctx_sum = core.sb(ctx, tag + "ctx_sum", [P, NB])
        g1 = core.sb(ctx, tag + "g1", [64, NB])
        g2 = core.sb(ctx, tag + "g2", [32, NB])
        gth = core.sb(ctx, tag + "gth", [P, NB])
        half_b = core.sb(ctx, tag + "half_b", [P, 2])
        slope = core.sb(ctx, tag + "slope", [P, 2])
        shift = core.sb(ctx, tag + "shift", [P, NB])
        sum_ready = core.sem(ctx, tag + "sum_ready")
        ctx_pe = core.sem(ctx, tag + "ctx_pe")
        ctx_act = core.sem(ctx, tag + "ctx_act")
        dve_step = core.sem(ctx, tag + "dve_step")
        half_ready = core.sem(ctx, tag + "half_ready")
        shift_ready = core.sem(ctx, tag + "shift_ready")
        pe_out = core.sem(ctx, tag + "pe_out")
        hid_ready = core.sem(ctx, tag + "hid_ready")
        gate_ready = core.sem(ctx, tag + "gate_ready")
        prod_ready = core.sem(ctx, tag + "prod_ready")
        out_ready = core.sem(ctx, tag + "out_ready")
        back = core.sem(ctx, tag + "back")
        block = core.block(ctx)

        def out(c):
            return core.xnT[:, c * CH:(c + 1) * CH]

        def bank(layer, c, odd):
            return core.psum[:, 4 * ((layer + odd) % 2) + c, :]

        @block.gpsimd
        def _(g):
            ln.pool(g)

        @block.vector
        def _(v):
            s = Steps(v, dve_step)
            v.wait_ge(w0_in, 16)
            v.tensor_scalar(half_b[:, 0:1], w("cn_b4"), 0.5, None, ALU.mult).then_inc(half_ready, 1)
            v.tensor_scalar(half_b[:, 1:2], w("gc_b3"), 0.5, None, ALU.mult).then_inc(half_ready, 1)
            s.did(v.tensor_scalar(slope[:, 0:1], w("range"), 0.3, None, ALU.mult))
            s.did(v.tensor_scalar(slope[:, 1:2], w("range"), 0.7, None, ALU.mult))
            v.sem_inc(out_ready, NC)
            ln.vector(v)
            for b in range(NB):
                v.wait_ge(ln.xnT_ready, NC // NB * (b + 1))
                v.tensor_reduce(ctx_sum[:, b:b + 1], core.xnT[:, b * T:(b + 1) * T], AX.X, ALU.add).then_inc(sum_ready, 1)
            v.wait_ge(ctx_act, 3)
            s.after(2)
            s.chain(v.tensor_scalar(shift[:, :], gth[:, :], slope[:, 1:2], None, ALU.mult))
            v.tensor_scalar(shift[:, :], shift[:, :], 0.1, None, ALU.add).then_inc(shift_ready, 1)
            with v.Fori(0, CYCLES) as cyc:
                for c in range(NC):
                    v.wait_ge(gate_ready, cyc * (2 * NC) + GATES[c])
                    v.wait_ge(pe_out, cyc * (LAYERS * NC) + 4 * NC + c + 1)
                    v.wait_ge(out_ready, cyc * NC + c + 1)
                    v.tensor_tensor(prod[:, c, :], gate[:, c, :], core.psum[:, c, :], ALU.mult).then_inc(prod_ready, 1)
                    v.wait_ge(prod_ready, cyc * NC + c + 1)
                    v.tensor_tensor(out(c), out(c), prod[:, c, :], ALU.add).then_inc(out_ready, 1)
            for c in range(NC):
                v.wait_ge(back, c + 1)
                xs = core.x[:, TPC * c:TPC * (c + 1), :].rearrange("p t d -> p (t d)")
                s.did(v.scalar_tensor_tensor(xs, core.psum[:, 4 + c, :], 0.5, xs, ALU.mult, ALU.add))

        @block.tensor
        def _(pe):
            pe.wait_ge(w0_in, 16)
            for c in range(NC):
                ln.tensor(pe, c)
            def cycle(cyc, first):
                for c in range(NC):
                    pe.wait_ge(ln.xnT_ready, c + 1)
                    pe.wait_ge(out_ready, cyc * NC + c + 1)
                    pe.matmul(core.psum[:, 4 + c, :], w("cn_w1"), out(c), start=True, stop=True).then_inc(pe_out, 1)
                for layer, name, rows, cols, ctx_name, ctx_rows, ctx_cols, ctx_in in (
                        (1, "cn_w2", 128, 64, "gc_w1", 128, 64, ctx_sum), (2, "cn_w3", 64, 128, "gc_w2", 64, 32, g1), (3, "cn_w4", 128, 128, "gc_w3", 32, 128, g2)):
                    if first:
                        if layer == 1:
                            pe.wait_ge(sum_ready, NB)
                        else:
                            pe.wait_ge(ctx_act, layer - 1)
                            pe.wait_ge(hid_ready, (layer - 2) * NC + 1)
                        pe.matmul(core.psum[0:ctx_cols, 4 * ((layer + 1) % 2), 0:NB], w(ctx_name, ctx_rows), ctx_in[:, :], start=True, stop=True).then_inc(ctx_pe, 1)
                        pe.wait_ge(ctx_act, layer)
                    for c in range(NC):
                        pe.wait_ge(hid_ready, cyc * (3 * NC) + (layer - 1) * NC + c + 1)
                        pe.matmul(core.psum[0:cols, 4 * ((layer + 1) % 2) + c, :], w(name, rows), hid[layer - 1][:, c, :],
                                  start=True, stop=True).then_inc(pe_out, 1)
                for c in range(NC):
                    pe.wait_ge(gate_ready, cyc * (2 * NC) + TANHS[c])
                    pe.matmul(core.psum[:, c, :], core.c("twist"), out(c), start=True, stop=True).then_inc(pe_out, 1)

            cycle(0, True)
            with pe.Fori(1, CYCLES) as cyc:
                cycle(cyc, False)
            for c in range(NC):
                pe.wait_ge(out_ready, CYCLES * NC + c + 1)
                for t in range(TPC):
                    ins = pe.transpose(core.psum[:, 4 + c, t * P:(t + 1) * P], core.xnT[:, c * CH + t * P:c * CH + (t + 1) * P],
                                       core.c("ident"))
                ins.then_inc(back, 1)

        @block.scalar
        def _(act):
            act.wait_ge(w0_in, 16)
            for c in range(NC):
                ln.scalar(act, c)
            def global_net(layer):
                act.wait_ge(ctx_pe, layer + 1)
                if layer == 0:
                    ins = act.activation(g1[:, :], core.psum[0:64, 0, 0:NB], ACT.Gelu, bias=w("gc_b1", 64), scale=SUMS)
                elif layer == 1:
                    ins = act.activation(g2[:, :], core.psum[0:32, 4, 0:NB], ACT.Gelu, bias=w("gc_b2", 32))
                else:
                    act.wait_ge(half_ready, 2)
                    ins = act.activation(gth[:, :], core.psum[:, 0, 0:NB], ACT.Tanh, bias=half_b[:, 1:2], scale=0.5)
                ins.then_inc(ctx_act, 1)

            def cycle(cyc, first):
                for layer, rows, bias in ((0, 128, "cn_b1"), (1, 64, "cn_b2"), (2, 128, "cn_b3")):
                    for c in range(NC):
                        act.wait_ge(pe_out, cyc * (LAYERS * NC) + layer * NC + c + 1)
                        act.activation(hid[layer][:, c, :], core.psum[0:rows, 4 * ((layer + 1) % 2) + c, :], ACT.Gelu,
                                       bias=w(bias, rows)).then_inc(hid_ready, 1)
                        if first and c == NC - 2:
                            global_net(layer)
                if first:
                    act.wait_ge(shift_ready, 1)
                def scale(c):
                    act.wait_ge(gate_ready, cyc * (2 * NC) + TANHS[c])
                    b = c // (NC // NB)
                    act.activation(gate[:, c, :], gate[:, c, :], ACT.Identity, bias=shift[:, b:b + 1], scale=slope[:, 0:1]).then_inc(gate_ready, 1)

                for c in range(NC):
                    act.wait_ge(out_ready, cyc * NC + c + 1)
                    act.wait_ge(pe_out, cyc * (LAYERS * NC) + 3 * NC + c + 1)
                    act.activation(gate[:, c, :], core.psum[:, c, :], ACT.Tanh, bias=half_b[:, 0:1], scale=0.5).then_inc(gate_ready, 1)
                    if c:
                        scale(c - 1)
                scale(NC - 1)

            cycle(0, True)
            with act.Fori(1, CYCLES) as cyc:
                cycle(cyc, False)


def scan_stage(core, w0, tag):
    nc = core.nc
    CPB = T // CH

    def w(name, rows=P):
        a, n = L0_COLS[name]
        return w0[0:rows, a:a + n]

    with ExitStack() as ctx:
        ln = LayerNorm(core, ctx, tag)
        decay = core.sb(ctx, tag + "decay", [P, 1])
        decays = core.sb(ctx, tag + "decays", [P, CH])
        bx = core.sb(ctx, tag + "bx", [P, NC, CH])
        h = core.sb(ctx, tag + "h", [P, N])
        yb = core.sb(ctx, tag + "yb", [P, NC, TPC, D])
        decay_ready = core.sem(ctx, tag + "decay_ready")
        dve_step = core.sem(ctx, tag + "dve_step")
        bx_pe = core.sem(ctx, tag + "bx_pe")
        bx_ready = core.sem(ctx, tag + "bx_ready")
        h_ready = core.sem(ctx, tag + "h_ready")
        y_pe = core.sem(ctx, tag + "y_pe")
        block = core.block(ctx)

        @block.gpsimd
        def _(g):
            ln.pool(g)

        @block.scalar
        def _(act):
            act.activation(decay[:, :], w("log_A"), ACT.Sigmoid).then_inc(decay_ready, 1)
            for c in range(NC):
                ln.scalar(act, c)
                act.wait_ge(bx_pe, c + 1)
                act.activation(bx[:, c, :], core.psum[:, c, :], ACT.Identity, bias=w("B_b")).then_inc(bx_ready, 1)

        @block.tensor
        def _(pe):
            def outputs(c):
                pe.wait_ge(h_ready, c + 1)
                for t in range(TPC):
                    ins = pe.matmul(core.psum[:, 4 + c % 2, t * P:(t + 1) * P], h[:, c * CH + t * P:c * CH + (t + 1) * P],
                                    w("C_wT"), start=True, stop=True)
                ins.then_inc(y_pe, 1)

            for c in range(NC):
                ln.tensor(pe, c)
                pe.wait_ge(ln.xnT_ready, c + 1)
                pe.matmul(core.psum[:, c, :], w("B_wT"), core.xnT[:, c * CH:(c + 1) * CH], start=True, stop=True).then_inc(bx_pe, 1)
            for c in range(NC):
                if c >= 2:
                    pe.wait_ge(dve_step, 2 + 2 * (c - 1))
                outputs(c)

        @block.vector
        def _(v):
            s = Steps(v, dve_step)
            ln.vector(v)
            s.chain(v.memset(decays[:, :], 1.0))
            v.wait_ge(decay_ready, 1)
            s.chain(v.tensor_scalar(decays[:, :], decays[:, :], decay[:, 0:1], None, ALU.mult))
            for c in range(NC):
                v.wait_ge(bx_ready, c + 1)
                if c % CPB:
                    v.wait_ge(h_ready, c)
                first = h[:, c * CH - 1:c * CH] if c % CPB else 0.0
                v.tensor_tensor_scan(h[:, c * CH:(c + 1) * CH], decays[:, :], bx[:, c, :], first, ALU.mult, ALU.add).then_inc(h_ready, 1)
            cb = w("C_b").unsqueeze(1).broadcast_to([P, TPC, D])
            for c in range(NC):
                v.wait_ge(y_pe, c + 1)
                s.chain(v.tensor_tensor(yb[:, c, :, :], core.psum[:, 4 + c % 2, :].rearrange("p (t d) -> p t d", d=D), cb, ALU.add))
                xs = core.x[:, TPC * c:TPC * (c + 1), :]
                s.did(v.tensor_tensor(xs, xs, yb[:, c, :, :], ALU.add))


def top1_stage(core, w1, w1_in, dram_experts, sorted_x, sorted_y, cleared, scattered, gathered, call, tag):
    nc = core.nc
    E, HT = 8, 4
    H = HT * P
    GATE_AT, UP_AT, DOWN_AT = 0, H, 2 * H
    BLOCKS = (N + (E - 1) * (P - 1)) // P
    HALF = NC // 2
    HID0, DOWN0 = HALF * HT, HALF
    HID1, DOWN1 = HID0 + BLOCKS, DOWN0 + BLOCKS
    GATE, UP, DOWN, TURN, HIDT = (0, 1), (2, 3), (4, 5), 6, 7
    LOGITS, RANKS = 5, 7
    ROUND = float(2 ** 23)

    with ExitStack() as ctx:
        ln = LayerNorm(core, ctx, tag)
        logit = core.sb(ctx, tag + "logit", [P, NT, E])
        prob = core.sb(ctx, tag + "prob", [P, NT, E])
        first = core.sb(ctx, tag + "first", [P, NT, E])
        chosen = core.sb(ctx, tag + "chosen", [P, E, NT])
        most = core.sb(ctx, tag + "most", [P, NT])
        total = core.sb(ctx, tag + "total", [P, NT])
        coef = core.sb(ctx, tag + "coef", [P, NT])
        count = core.sb(ctx, tag + "count", [P, E])
        whole = core.sb(ctx, tag + "whole", [P, E])
        taken = core.sb(ctx, tag + "taken", [P, E, NT])
        ends = core.sb(ctx, tag + "ends", [P, E, NT])
        place = core.sb(ctx, tag + "place", [P, NT])
        place_in = core.sb(ctx, tag + "place_in", [P, NT], I32)
        place_out = core.sb(ctx, tag + "place_out", [P, NT], I32)
        passed = core.sb(ctx, tag + "passed", [P, E - 1, BLOCKS])
        owner = core.sb(ctx, tag + "owner", [P, BLOCKS])
        table = core.sb(ctx, tag + "table", [P, BLOCKS], I32)
        experts = core.sb(ctx, tag + "experts", [P, E - 1, 3 * H])
        shared = core.sb(ctx, tag + "shared", [P, 3 * H])
        rows = [core.sb(ctx, f"{tag}rows{odd}", [P, D]) for odd in range(2)]
        routed = core.sb(ctx, tag + "routed", [P, NT, D])
        rowsT = core.sb(ctx, tag + "rowsT", [P, 2, P])
        silu = core.sb(ctx, tag + "silu", [P, 2, CH])
        hid = core.sb(ctx, tag + "hid", [P, 2, HT, CH])
        block_hid = core.sb(ctx, tag + "block_hid", [P, 2, H])
        block_hidT = core.sb(ctx, tag + "block_hidT", [P, 2, H])
        outs = core.sb(ctx, tag + "outs", [P, BLOCKS, D])
        logits_pe = core.sem(ctx, tag + "logits_pe")
        dve_step = core.sem(ctx, tag + "dve_step")
        shifted = core.sem(ctx, tag + "shifted")
        exps = core.sem(ctx, tag + "exps")
        chosen_ready = core.sem(ctx, tag + "chosen_ready")
        ranks_pe = core.sem(ctx, tag + "ranks_pe")
        place_ready = core.sem(ctx, tag + "place_ready")
        table_ready = core.sem(ctx, tag + "table_ready")
        rows_in = [core.sem(ctx, f"{tag}rows_in{odd}") for odd in range(2)]
        shared_in = core.sem(ctx, tag + "shared_in")
        experts_in = core.sem(ctx, tag + "experts_in")
        turn_pe = core.sem(ctx, tag + "turn_pe")
        rowsT_ready = core.sem(ctx, tag + "rowsT_ready")
        gate_pe = core.sem(ctx, tag + "gate_pe")
        up_pe = core.sem(ctx, tag + "up_pe")
        silu_ready = core.sem(ctx, tag + "silu_ready")
        hid_ready = core.sem(ctx, tag + "hid_ready")
        hidT_pe = core.sem(ctx, tag + "hidT_pe")
        hidT_ready = core.sem(ctx, tag + "hidT_ready")
        down_pe = core.sem(ctx, tag + "down_pe")
        out_read = core.sem(ctx, tag + "out_read")
        spilled = core.sem(ctx, tag + "spilled")
        block = core.block(ctx)

        def reach(eng, sem, count):
            if not isinstance(count, int) or count > 0:
                eng.wait_ge(sem, count)

        def blocks(eng, step):
            for odd in (0, 1):
                step(0, odd, range(0, odd + 1))
            with eng.Fori(1, BLOCKS // 2) as pair:
                for odd in (0, 1):
                    step(pair, odd, range(0, 3))
            for odd in (0, 1):
                step(BLOCKS // 2, odd, range(1 + odd, 3))

        @block.sync
        def _(sp):
            sp.dma_start(shared[:, :], dram_experts[E - 1].rearrange("p j d -> p (j d)")).then_inc(shared_in, 16)
            for e in range(E - 1):
                sp.dma_start(experts[:, e, :], dram_experts[e].rearrange("p j d -> p (j d)")).then_inc(experts_in, 16)
            sp.wait_ge(scattered, 16 * NT * (call + 1))
            blocks_x, blocks_y = (z.rearrange("(k p) d -> p k d", p=P) for z in (sorted_x, sorted_y))

            def load(pair, odd):
                reach(sp, turn_pe, pair * 2 + odd - 1)
                src = blocks_x[:, bass.ds(pair * 2 + odd, 1), :].rearrange("p o d -> p (o d)")
                sp.dma_start(rows[odd][:, :], src).then_inc(rows_in[odd], 16)

            def spill(pair):
                sp.wait_ge(out_read, pair * 2 + DOWN0 + 2)
                sp.dma_start(blocks_y[:, bass.ds(pair * 2, 2), :], outs[:, bass.ds(pair * 2, 2), :]).then_inc(spilled, 16)

            for pair in (0, 1):
                for odd in (0, 1):
                    load(pair, odd)
            with sp.Fori(2, BLOCKS // 2) as pair:
                for odd in (0, 1):
                    load(pair, odd)
                spill(pair - 2)
            load(BLOCKS // 2, 0)
            for pair in (BLOCKS // 2 - 2, BLOCKS // 2 - 1):
                spill(pair)

        @block.gpsimd
        def _(g):
            ln.pool(g)
            g.wait_ge(cleared, 16)
            g.wait_ge(place_ready, 2)
            g.wait_ge(ln.xn_ready, NT)
            for t in range(NT):
                to = bass.IndirectOffsetOnAxis(ap=place_in[:, t:t + 1], axis=0)
                g.indirect_dma_start(sorted_x, to, core.xn[:, t, :], None).then_inc(scattered, 16)
            g.wait_ge(spilled, 16 * (BLOCKS // 2))
            for t in range(NT):
                at = bass.IndirectOffsetOnAxis(ap=place_out[:, t:t + 1], axis=0)
                g.indirect_dma_start(routed[:, t, :], None, sorted_y, at).then_inc(gathered[t], 16)

        @block.scalar
        def _(act):
            for c in range(NC):
                ln.scalar(act, c)
            act.wait_ge(shifted, 1)
            act.activation(prob[:, :, :], logit[:, :, :], ACT.Exp).then_inc(exps, 1)

            def gate(n, odd):
                reach(act, hid_ready, n - 1)
                act.wait_ge(gate_pe, n + 1)
                act.activation(silu[:, odd, :], core.psum[:, GATE[odd], :], ACT.Silu).then_inc(silu_ready, 1)

            def step(pair, odd, parts):
                k = pair * 2 + odd
                if 0 in parts:
                    gate(k + HID0, odd)
                if 1 in parts:
                    reach(act, down_pe, k + DOWN0 - 2)
                    act.wait_ge(hidT_pe, k)
                    act.activation(block_hidT[:, 1 - odd, :], core.psum[:, HIDT, :], ACT.Copy).then_inc(hidT_ready, 1)

            for n in range(HID0):
                gate(n, n % 2)
            blocks(act, step)
            for n in range(HID0):
                gate(HID1 + n, n % 2)

        @block.tensor
        def _(pe):
            pe.wait_ge(w1_in, 16)

            def logits(c):
                pe.wait_ge(ln.xnT_ready, c + 1)
                for t in range(TPC * c, TPC * (c + 1)):
                    ins = pe.matmul(core.psum[:, LOGITS, t * E:(t + 1) * E], core.xnT[:, t * P:(t + 1) * P], w1[:, 0:E], start=True, stop=True)
                if c == NC - 1:
                    ins.then_inc(logits_pe, 1)

            for c in range(NC):
                ln.tensor(pe, c)
                if c:
                    logits(c - 1)
            logits(NC - 1)

            def shared_up(n0, c, j):
                n = n0 + j
                xc = core.xnT[:, c * CH:(c + 1) * CH]
                reach(pe, silu_ready, n - 1)
                pe.matmul(core.psum[:, GATE[n % 2], :], shared[:, GATE_AT + j * P:GATE_AT + (j + 1) * P], xc, start=True, stop=True).then_inc(gate_pe, 1)
                reach(pe, hid_ready, n - 1)
                pe.matmul(core.psum[:, UP[n % 2], :], shared[:, UP_AT + j * P:UP_AT + (j + 1) * P], xc, start=True, stop=True).then_inc(up_pe, 1)

            def shared_down(n0, d, c):
                pe.wait_ge(hid_ready, n0 + HT)
                reach(pe, out_read, d - 1)
                for t in range(TPC):
                    for j in range(HT):
                        ins = pe.matmul(core.psum[:, DOWN[d % 2], t * P:(t + 1) * P], hid[:, c % 2, j, t * P:(t + 1) * P],
                                        shared[:, DOWN_AT + j * P:DOWN_AT + (j + 1) * P], start=(j == 0), stop=(j == HT - 1))
                ins.then_inc(down_pe, 1)

            def turn(pair, odd):
                pe.wait_ge(rows_in[odd], pair * 16 + 16)
                reach(pe, rowsT_ready, pair * 2 + odd)
                pe.transpose(core.psum[:, TURN, 0:P], rows[odd][:, :], core.c("ident")).then_inc(turn_pe, 1)

            def expert(k):
                return pe.value_load(table[0:1, bass.ds(k, 1)], min_val=0, max_val=E - 2)

            def weights(e, at, n):
                return experts[:, bass.ds(e, 1), at:at + n].rearrange("p o c -> p (o c)")

            def step(pair, odd, parts):
                k = pair * 2 + odd
                if 0 in parts:
                    e = expert(k)
                    turn(pair + odd, 1 - odd)
                    pe.wait_ge(rowsT_ready, k + 1)
                    pe.wait_ge(silu_ready, k + HID0 - 1)
                    pe.matmul(core.psum[:, GATE[odd], :], rowsT[:, odd, :], weights(e, GATE_AT, H), start=True, stop=True).then_inc(gate_pe, 1)
                    pe.wait_ge(hid_ready, k + HID0 - 1)
                    pe.matmul(core.psum[:, UP[odd], :], rowsT[:, odd, :], weights(e, UP_AT, H), start=True, stop=True).then_inc(up_pe, 1)
                if 1 in parts:
                    pe.wait_ge(hid_ready, k + HID0)
                    reach(pe, hidT_ready, k - 1)
                    for j in range(HT):
                        ins = pe.transpose(core.psum[:, HIDT, j * P:(j + 1) * P], block_hid[:, 1 - odd, j * P:(j + 1) * P], core.c("ident"))
                    ins.then_inc(hidT_pe, 1)
                if 2 in parts:
                    e = expert(k - 2)
                    pe.wait_ge(hidT_ready, k - 1)
                    pe.wait_ge(out_read, k + DOWN0 - 3)
                    for j in range(HT):
                        ins = pe.matmul(core.psum[:, DOWN[odd], 0:D], block_hidT[:, odd, j * P:(j + 1) * P], weights(e, DOWN_AT + j * P, D),
                                        start=(j == 0), stop=(j == HT - 1))
                    ins.then_inc(down_pe, 1)

            def shared_chunks(n0, d0, c0):
                for c in range(HALF):
                    for j in range(HT):
                        shared_up(n0 + c * HT, c0 + c, j)
                        if n0 == 0 and c == 0 and j == 1:
                            pe.wait_ge(chosen_ready, 1)
                            picks = chosen[:, :, :].rearrange("p e t -> p (e t)")
                            pe.matmul(core.psum[:, RANKS, 0:P], core.c("earlier"), picks, start=True, stop=True)
                            pe.matmul(core.psum[:, RANKS, P:2 * P], core.c("ones"), picks, start=True, stop=True).then_inc(ranks_pe, 1)
                    if c:
                        shared_down(n0 + (c - 1) * HT, d0 + c - 1, c0 + c - 1)
                shared_down(n0 + (HALF - 1) * HT, d0 + HALF - 1, c0 + HALF - 1)

            pe.wait_ge(shared_in, 16)
            shared_chunks(0, 0, 0)
            pe.wait_ge(table_ready, 1)
            pe.wait_ge(experts_in, 16 * (E - 1))
            turn(0, 0)
            blocks(pe, step)
            shared_chunks(HID1, DOWN1, HALF)

        @block.vector
        def _(v):
            s = Steps(v, dve_step)
            ln.vector(v)
            v.wait_ge(logits_pe, 1)
            lp = core.psum[:, LOGITS, 0:NT * E].rearrange("p (t e) -> p t e", e=E)

            def wide(a):
                return a.unsqueeze(2).broadcast_to([P, NT, E])

            s.chain(v.tensor_reduce(most[:, :], lp, AX.X, ALU.max))
            v.tensor_tensor(logit[:, :, :], lp, wide(most[:, :]), ALU.subtract).then_inc(shifted, 1)
            v.wait_ge(shifted, 1)
            order = core.c("first8").unsqueeze(1).broadcast_to([P, NT, E])
            s.chain(v.scalar_tensor_tensor(first[:, :, :], logit[:, :, :], 0.0, order, ALU.is_equal, ALU.mult))
            s.chain(v.tensor_reduce(most[:, :], first[:, :, :], AX.X, ALU.max))
            v.tensor_tensor(chosen[:, :, :].rearrange("p e t -> p t e"), first[:, :, :], wide(most[:, :]), ALU.is_equal).then_inc(chosen_ready, 1)
            v.wait_ge(exps, 1)
            s.chain(v.tensor_reduce(total[:, :], prob[:, :, :], AX.X, ALU.add))
            v.wait_ge(chosen_ready, 1)
            s.did(v.tensor_scalar(coef[:, :], chosen[:, E - 1, :], -1.0, 1.0, ALU.mult, ALU.add))
            s.chain(v.reciprocal(total[:, :], total[:, :]))
            s.did(v.tensor_tensor(coef[:, :], coef[:, :], total[:, :], ALU.mult))
            v.wait_ge(ranks_pe, 1)
            within = core.psum[:, RANKS, 0:P].rearrange("p (e t) -> p e t", e=E)
            in_tile = core.psum[:, RANKS, P:2 * P].rearrange("p (e t) -> p e t", e=E)
            s.did(v.tensor_reduce(count[:, :], in_tile, AX.X, ALU.add))
            s.chain(v.tensor_copy(taken[:, :, :], in_tile))
            s.chain(v.tensor_scalar(whole[:, :], count[:, :], 1.0 / P, (P - 1) / P - 0.498, ALU.mult, ALU.add))
            s.chain(v.tensor_scalar(whole[:, :], whole[:, :], ROUND, None, ALU.add))
            s.chain(v.tensor_scalar(whole[:, :], whole[:, :], ROUND, None, ALU.subtract))
            s.chain(v.scalar_tensor_tensor(count[:, :], whole[:, :], float(P), count[:, :], ALU.mult, ALU.subtract))
            s.chain(v.tensor_tensor(taken[:, :, NT - 1], taken[:, :, NT - 1], count[:, :], ALU.add))

            def flat(a):
                return a[:, :, :].rearrange("p e t -> p (e t)")

            s.chain(v.tensor_tensor_scan(flat(ends), core.c("ones"), flat(taken), 0.0, ALU.mult, ALU.add))
            s.chain(v.tensor_tensor(taken[:, :, :], ends[:, :, :], taken[:, :, :], ALU.subtract))
            s.chain(v.tensor_tensor(taken[:, :, :], within, taken[:, :, :], ALU.add))
            s.chain(v.tensor_tensor(taken[:, :, :], taken[:, :, :], chosen[:, :, :], ALU.mult))
            s.chain(v.tensor_reduce(place[:, :], taken[:, :, :].rearrange("p e t -> p t e"), AX.X, ALU.add))
            v.tensor_copy(place_in[:, :], place[:, :]).then_inc(place_ready, 1)
            v.tensor_scalar(place_out[:, :], place[:, :], float(BLOCKS * P - 1), None, ALU.min).then_inc(place_ready, 1)
            start = core.c("block_start")[:, 0:BLOCKS].unsqueeze(1).broadcast_to([P, E - 1, BLOCKS])
            s.chain(v.tensor_tensor(passed[:, :, :], start, ends[:, 0:E - 1, NT - 1].unsqueeze(2).broadcast_to([P, E - 1, BLOCKS]), ALU.is_ge))
            s.chain(v.tensor_reduce(owner[:, :], passed[:, :, :].rearrange("p e b -> p b e"), AX.X, ALU.add))
            v.tensor_scalar(table[:, :], owner[:, :], float(E - 2), None, ALU.min).then_inc(table_ready, 1)

            def multiply(n, odd, dst):
                v.wait_ge(silu_ready, n + 1)
                v.wait_ge(up_pe, n + 1)
                v.tensor_tensor(dst, silu[:, odd, :], core.psum[:, UP[odd], :], ALU.mult).then_inc(hid_ready, 1)

            def shared_add(d, c):
                v.wait_ge(down_pe, d + 1)
                xs = core.x[:, TPC * c:TPC * (c + 1), :].rearrange("p t d -> p (t d)")
                v.scalar_tensor_tensor(xs, core.psum[:, DOWN[d % 2], :], 0.5, xs, ALU.mult, ALU.add).then_inc(out_read, 1)

            def add_routed(t):
                v.wait_ge(gathered[t], 16 * (call + 1))
                xs = core.x[:, t, :]
                s.did(v.scalar_tensor_tensor(xs, routed[:, t, :], coef[:, t:t + 1], xs, ALU.mult, ALU.add))

            def shared_chunks(n0, d0, c0):
                for c in range(HALF):
                    for j in range(HT):
                        multiply(n0 + c * HT + j, j % 2, hid[:, c, j, :])
                        if c0 and c * HT + j:
                            add_routed(c * HT + j - 1)
                    if c:
                        shared_add(d0 + c - 1, c0 + c - 1)
                shared_add(d0 + HALF - 1, c0 + HALF - 1)

            def turned(k, odd):
                v.wait_ge(turn_pe, k + 1)
                v.wait_ge(up_pe, k + HID0 - 1)
                v.tensor_copy(rowsT[:, odd, :], core.psum[:, TURN, 0:P]).then_inc(rowsT_ready, 1)

            def step(pair, odd, parts):
                k = pair * 2 + odd
                if 0 in parts:
                    turned(k + 1, 1 - odd)
                    reach(v, hidT_pe, k - 1)
                    multiply(k + HID0, odd, block_hid[:, odd, :])
                if 2 in parts:
                    v.wait_ge(down_pe, k + DOWN0 - 1)
                    dst = outs[:, bass.ds(k - 2, 1), :].rearrange("p o d -> p (o d)")
                    v.tensor_copy(dst, core.psum[:, DOWN[odd], 0:D]).then_inc(out_read, 1)

            shared_chunks(0, 0, 0)
            turned(0, 0)
            blocks(v, step)
            shared_chunks(HID1, DOWN1, HALF)
            v.wait_ge(out_read, DOWN1 + HALF)
            for t in range(HALF * HT - 1, NT):
                add_routed(t)


def mlp_stage(core, w2, w2_in, tag):
    nc = core.nc
    HT = 4

    def w(name, j=0):
        a, n = L2_COLS[name]
        return w2[:, a + j * P:a + (j + 1) * P] if n > HT else w2[:, a + j:a + j + 1]

    with ExitStack() as ctx:
        ln = LayerNorm(core, ctx, tag)
        gate = core.sb(ctx, tag + "gate", [P, 2, CH])
        h0 = core.sb(ctx, tag + "h0", [P, HT, N])
        h1 = core.sb(ctx, tag + "h1", [P, HT, CH])
        h2 = core.sb(ctx, tag + "h2", [P, HT, CH])
        y = core.sb(ctx, tag + "y", [P, TPC, D])
        gate_pe = core.sem(ctx, tag + "gate_pe")
        up_pe = core.sem(ctx, tag + "up_pe")
        silu_ready = core.sem(ctx, tag + "silu_ready")
        h0_ready = core.sem(ctx, tag + "h0_ready")
        hid_pe = core.sem(ctx, tag + "hid_pe")
        gelu_ready = core.sem(ctx, tag + "gelu_ready")
        y_pe = core.sem(ctx, tag + "y_pe")
        scaled = core.sem(ctx, tag + "scaled")
        added = core.sem(ctx, tag + "added")
        block = core.block(ctx)
        GATE, UP, HID, Y = (0, 1), (2, 3), (0, 1), 4
        GELUS = 2 * HT

        @block.gpsimd
        def _(g):
            ln.pool(g)

        @block.scalar
        def _(act):
            act.wait_ge(w2_in, 16)
            for c in range(NC):
                ln.scalar(act, c)
                for j in range(HT):
                    n = c * HT + j
                    if n >= 2:
                        act.wait_ge(h0_ready, n - 1)
                    act.wait_ge(gate_pe, n + 1)
                    act.activation(gate[:, n % 2, :], core.psum[:, GATE[n % 2], :], ACT.Silu, scale=w("s1", j)).then_inc(silu_ready, 1)
            act.sem_inc(gelu_ready, 1)
            with act.Fori(0, NC) as c:
                for layer, dst, scale in ((0, h1, "sh1"), (1, h2, "sh2")):
                    for j in range(HT):
                        n = layer * HT + j
                        act.wait_ge(hid_pe, c * GELUS + n + 1)
                        act.activation(dst[:, j, :], core.psum[:, HID[n % 2], :], ACT.Gelu, scale=w(scale, j)).then_inc(gelu_ready, 1)

        @block.tensor
        def _(pe):
            pe.wait_ge(w2_in, 16)
            ln.tensor(pe, 0)
            for c in range(NC):
                if c + 1 < NC:
                    ln.tensor(pe, c + 1)
                pe.wait_ge(ln.xnT_ready, c + 1)
                xc = core.xnT[:, c * CH:(c + 1) * CH]
                for j in range(HT):
                    n = c * HT + j
                    if n >= 2:
                        pe.wait_ge(silu_ready, n - 1)
                    pe.matmul(core.psum[:, GATE[n % 2], :], w("w1T", j), xc, start=True, stop=True).then_inc(gate_pe, 1)
                    if n >= 2:
                        pe.wait_ge(h0_ready, n - 1)
                    pe.matmul(core.psum[:, UP[n % 2], :], w("w2T", j), xc, start=True, stop=True).then_inc(up_pe, 1)
            pe.wait_ge(h0_ready, NC * HT)
            with pe.Fori(0, NC) as c:
                for layer, name in ((0, "h1T"), (1, "h2T")):
                    for j in range(HT):
                        n = layer * HT + j
                        pe.wait_ge(gelu_ready, c * GELUS + 1 + (n - 1 if n >= 2 else 0))
                        if layer == 1 and j == 0:
                            pe.wait_ge(gelu_ready, c * GELUS + 1 + HT)
                        for i in range(HT):
                            src = h0[:, i, bass.ds(c * CH, CH)] if layer == 0 else h1[:, i, :]
                            ins = pe.matmul(core.psum[:, HID[n % 2], :], w(name, i * HT + j), src, start=(i == 0), stop=(i == HT - 1))
                        ins.then_inc(hid_pe, 1)
                pe.wait_ge(gelu_ready, c * GELUS + 1 + GELUS)
                pe.wait_ge(added, c + 1)
                for t in range(TPC):
                    for i in range(HT):
                        ins = pe.matmul(core.psum[:, Y, t * P:(t + 1) * P], h2[:, i, t * P:(t + 1) * P], w("w3T", i), start=(i == 0), stop=(i == HT - 1))
                ins.then_inc(y_pe, 1)

        @block.vector
        def _(v):
            v.wait_ge(w2_in, 16)
            ln.vector(v)
            for c in range(NC):
                for j in range(HT):
                    n = c * HT + j
                    v.wait_ge(silu_ready, n + 1)
                    v.wait_ge(up_pe, n + 1)
                    v.scalar_tensor_tensor(h0[:, j, c * CH:(c + 1) * CH], core.psum[:, UP[n % 2], :], w("s2", j), gate[:, n % 2, :],
                                           ALU.mult, ALU.mult).then_inc(h0_ready, 1)
            v.sem_inc(added, 1)
            a, n = L2_COLS["s3"]
            s3 = w2[:, a:a + n].unsqueeze(1).broadcast_to([P, TPC, D])
            with v.Fori(0, NC) as c:
                v.wait_ge(y_pe, c + 1)
                v.wait_ge(added, c + 1)
                v.tensor_tensor(y[:, :, :], core.psum[:, Y, :].rearrange("p (t d) -> p t d", d=D), s3, ALU.mult).then_inc(scaled, 1)
                v.wait_ge(scaled, c + 1)
                xs = core.x[:, bass.ds(c * TPC, TPC), :]
                v.scalar_tensor_tensor(xs, y[:, :, :], 0.5, xs, ALU.mult, ALU.add).then_inc(added, 1)


class Norm:

    BANKS = (6, 7)

    def __init__(self, core, ctx, tag, src, dst, rms=False, eps=LN_EPS):
        self.k, self.src, self.dst, self.rms, self.eps = core, src, dst, rms, eps
        self.square = core.sb(ctx, tag + "square", [P, NT])
        self.stat_step = core.sem(ctx, tag + "stat_step")
        self.var_ready = core.sem(ctx, tag + "var_ready")
        self.pool_step = core.sem(ctx, tag + "pool_step")
        self.rstd_ready = core.sem(ctx, tag + "rstd_ready")
        self.xn_ready = core.sem(ctx, tag + "xn_ready")
        self.turned = core.sem(ctx, tag + "turned")
        self.xnT_ready = core.sem(ctx, tag + "xnT_ready")

    def vector(self, v):
        k = self.k

        def statistics(c):
            tiles = range(TPC * c, TPC * (c + 1))
            for t in tiles:
                v.bn_stats(k.stats[:, t, :], self.src[:, t, :]).then_inc(self.stat_step, 1)
            for t in tiles:
                v.wait_ge(self.stat_step, t + 1)
                v.bn_aggr(k.meanvar[:, t, :], k.stats[:, t, :]).then_inc(self.var_ready, 1)

        def normalise(c):
            v.wait_ge(self.var_ready, TPC * (c + 1))
            v.wait_ge(self.rstd_ready, c + 1)
            for t in range(TPC * c, TPC * (c + 1)):
                if self.rms:
                    ins = v.tensor_scalar(self.dst[:, t, :], self.src[:, t, :], k.rstd[:, t:t + 1], None, ALU.mult)
                else:
                    ins = v.tensor_scalar(self.dst[:, t, :], self.src[:, t, :], k.meanvar[:, t, 0:1], k.rstd[:, t:t + 1],
                                          ALU.subtract, ALU.mult)
                ins.then_inc(self.xn_ready, 1)

        statistics(0)
        for c in range(NC):
            if c + 1 < NC:
                statistics(c + 1)
            normalise(c)

    def pool(self, g):
        k = self.k
        s = Steps(g, self.pool_step)
        for c in range(NC):
            a, b = TPC * c, TPC * (c + 1)
            g.wait_ge(self.var_ready, b)
            var, mean, r = k.meanvar[:, a:b, 1], k.meanvar[:, a:b, 0], k.rstd[:, a:b]
            if self.rms:
                s.chain(g.tensor_tensor(self.square[:, a:b], mean, mean, ALU.mult))
                s.chain(g.tensor_tensor(self.square[:, a:b], self.square[:, a:b], var, ALU.add))
                var = self.square[:, a:b]
            s.chain(g.tensor_scalar(r, var, self.eps, None, ALU.add))
            g.tensor_tensor(r, r, k.mhalf[:, a:b], ALU.pow).then_inc(self.rstd_ready, 1)

    def tensor(self, pe, c):
        k = self.k
        if c >= 2:
            pe.wait_ge(self.xnT_ready, c - 1)
        for t in range(TPC):
            pe.wait_ge(self.xn_ready, TPC * c + t + 1)
            ins = pe.transpose(k.psum[:, self.BANKS[c % 2], t * P:(t + 1) * P], self.dst[:, TPC * c + t, :], k.c("ident"))
        ins.then_inc(self.turned, 1)

    def scalar(self, act, c, gain=1.0, bias=0.0):
        k = self.k
        act.wait_ge(self.turned, c + 1)
        act.activation(k.xnT[:, c * CH:(c + 1) * CH], k.psum[:, self.BANKS[c % 2], :], ACT.Identity, bias=bias, scale=gain).then_inc(self.xnT_ready, 1)


def norm_stage(core, tag):
    with ExitStack() as ctx:
        ln = Norm(core, ctx, tag, core.x, core.xn)
        block = core.block(ctx)

        @block.gpsimd
        def _(g):
            ln.pool(g)

        @block.vector
        def _(v):
            ln.vector(v)


class Split:

    PARTS = 3

    def __init__(self, core, ctx, tag, rows, scratch):
        self.k, self.rows, self.scratch = core, rows, scratch
        self.parts = [core.sb(ctx, f"{tag}parts{i}", [r, self.PARTS, 2, CH], BF16) for i, r in enumerate(rows)]
        self.rest = [core.sb(ctx, f"{tag}rest{i}", [r, CH]) for i, r in enumerate(rows)]
        self.heads_pe = core.sem(ctx, tag + "heads_pe")
        self.part_ready = core.sem(ctx, tag + "part_ready")
        self.rest_ready = core.sem(ctx, tag + "rest_ready")
        self.spilled = [[core.sem(ctx, f"{tag}spilled{i}{odd}") for odd in range(2)] for i in range(2)]

    def parted(self, c, p, i):
        return 2 * (self.PARTS * c + p) + i + 1

    def left(self, c, p, i):
        return 2 * ((self.PARTS - 1) * c + p - 1) + i + 1

    def scalar(self, act, c, sources):
        for p in range(self.PARTS):
            for i, source in enumerate(sources):
                if p == 0:
                    act.wait_ge(self.heads_pe, 2 * c + i + 1)
                    if c >= 2:
                        act.wait_ge(self.spilled[i][c % 2], 16 * (c // 2))
                else:
                    act.wait_ge(self.rest_ready, self.left(c, p, i))
                    source = self.rest[i][:, :]
                act.activation(self.parts[i][:, p, c % 2, :], source, ACT.Copy).then_inc(self.part_ready, 1)

    def vector(self, v, c, sources):
        for p in range(1, self.PARTS):
            for i, source in enumerate(sources):
                v.wait_ge(self.part_ready, self.parted(c, p - 1, i))
                if p > 1:
                    v.wait_ge(self.rest_ready, self.left(c, p - 1, i))
                elif c:
                    v.wait_ge(self.rest_ready, self.left(c - 1, self.PARTS - 1, i))
                v.tensor_tensor(self.rest[i][:, :], source if p == 1 else self.rest[i][:, :], self.parts[i][:, p - 1, c % 2, :],
                                ALU.subtract).then_inc(self.rest_ready, 1)

    def read(self, pe, c):
        pe.wait_ge(self.rest_ready, self.left(c, 1, 1))
        pe.wait_ge(self.part_ready, self.parted(c, 0, 1))

    def sync(self, sp, c, i):
        b, at = divmod(c * CH, T)
        sp.wait_ge(self.part_ready, self.parted(c, self.PARTS - 1, i))
        dst = self.scratch[i][:, b, :, at:at + CH].rearrange("p r t -> r p t")
        sp.dma_start(dst, self.parts[i][:, :, c % 2, :]).then_inc(self.spilled[i][c % 2], 16)

    def landed(self, sp):
        for i in range(2):
            for odd in range(2):
                sp.wait_ge(self.spilled[i][odd], 16 * NC // 2)


HEADS, HD = 16, 8
GROUP = 4


def rope_project_stage(core, w3, w3_in, v_all, scratch, tag):
    nc = core.nc
    QK = 2 * 2 * D

    def w(name, rows=P):
        a, n = L1_COLS[name]
        return w3[0:rows, a:a + n]

    with ExitStack() as ctx:
        ln = LayerNorm(core, ctx, tag)
        sp_ = Split(core, ctx, tag, (P, P), scratch)
        cosed = core.sb(ctx, tag + "cosed", [P, 2 * D])
        sined = core.sb(ctx, tag + "sined", [P, 2 * D])
        heads = core.sb(ctx, tag + "heads", [P, 2, 2, D])
        qk_pe = core.sem(ctx, tag + "qk_pe")
        qk = core.sb(ctx, tag + "qk", [P, QK])
        biased = core.sem(ctx, tag + "biased")
        cos_step = core.sem(ctx, tag + "cos_step")
        heads_ready = core.sem(ctx, tag + "heads_ready")
        turned = core.sem(ctx, tag + "turned_qk")
        block = core.block(ctx)
        QK_BANK, V_BANK, T_BANK = (0, 1), (2, 3), (4, 5, 6, 7)

        def turned_bank(c, i):
            return core.psum[:, T_BANK[2 * (c % 2) + i], :]

        @block.gpsimd
        def _(g):
            ln.pool(g)

        @block.sync
        def _(sp):
            for c in range(NC):
                for i in range(2):
                    sp_.sync(sp, c, i)
            sp_.landed(sp)

        @block.tensor
        def _(pe):
            pe.wait_ge(w3_in, 16)
            for c in range(NC):
                ln.tensor(pe, c)

            def turn(t):
                c = t // TPC
                if t % TPC == 0 and c >= 2:
                    sp_.read(pe, c - 2)
                elif t == TPC:
                    pe.wait_ge(ln.xnT_ready, NC)
                pe.wait_ge(heads_ready, t + 1)
                for i in range(2):
                    ins = pe.transpose(turned_bank(c, i)[:, (t % TPC) * P:(t % TPC + 1) * P], heads[:, t % 2, i, :], core.c("ident"))
                    if t % TPC == TPC - 1:
                        ins.then_inc(sp_.heads_pe, 1)
                    elif i == 1:
                        ins.then_inc(turned, 1)

            for t in range(NT):
                pe.wait_ge(ln.xnT_ready, t // TPC + 1)
                if t >= 2:
                    pe.wait_ge(biased, 2 * (t - 1))
                xt = core.xnT[:, t * P:(t + 1) * P]
                for bank, name, n in ((QK_BANK, "qk", QK), (V_BANK, "v", D)):
                    ins = pe.matmul(core.psum[:, bank[t % 2], 0:n], xt, w(name), start=True, stop=True)
                ins.then_inc(qk_pe, 1)
                if t:
                    turn(t - 1)
            turn(NT - 1)

        @block.scalar
        def _(act):
            act.wait_ge(w3_in, 16)
            for c in range(NC):
                ln.scalar(act, c)
            for c in range(NC):
                sp_.scalar(act, c, [turned_bank(c, i) for i in range(2)])

        @block.vector
        def _(v):
            v.wait_ge(w3_in, 16)
            ln.vector(v)

            def table(name, t):
                a, n = L1_COLS[name]
                tab = w3[:, a + (t % (T // P)) * HD:a + (t % (T // P)) * HD + HD]
                return tab.unsqueeze(1).unsqueeze(3).broadcast_to([P, 2 * HEADS // GROUP, HD, GROUP])

            def grouped(a):
                return a.rearrange("p (g d h) -> p g d h", d=HD, h=GROUP)

            for t in range(NT):
                v.wait_ge(qk_pe, t + 1)
                if t:
                    v.wait_ge(cos_step, 2 * t)
                v.tensor_tensor(qk[:, :], core.psum[:, QK_BANK[t % 2], :], w("qk_b"), ALU.add).then_inc(biased, 1)
                v.tensor_tensor(v_all[:, t, :], core.psum[:, V_BANK[t % 2], 0:D], w("v_b"), ALU.add).then_inc(biased, 1)
                ps = qk[:, :].rearrange("p (r f) -> p r f", r=2)
                v.wait_ge(biased, 2 * t + 1)
                if t:
                    v.wait_ge(heads_ready, t)
                v.tensor_tensor(grouped(cosed[:, :]), grouped(ps[:, 0, :]), table("cos", t), ALU.mult).then_inc(cos_step, 1)
                v.tensor_tensor(grouped(sined[:, :]), grouped(ps[:, 1, :]), table("sin", t), ALU.mult).then_inc(cos_step, 1)
                v.wait_ge(cos_step, 2 * t + 2)
                if t >= 2:
                    u = t - 2
                    v.wait_ge(turned, u // TPC * (TPC - 1) + min(u % TPC + 1, TPC - 1))
                    if u // TPC * TPC + TPC - 1 == u:
                        v.wait_ge(sp_.heads_pe, 2 * (u // TPC + 1))
                v.tensor_tensor(heads[:, t % 2, :, :].rearrange("p i f -> p (i f)"), cosed[:, :], sined[:, :], ALU.add).then_inc(heads_ready, 1)
                if t % TPC == 1 and t > TPC:
                    sp_.vector(v, t // TPC - 1, [turned_bank(t // TPC - 1, i) for i in range(2)])
            sp_.vector(v, NC - 1, [turned_bank(NC - 1, i) for i in range(2)])


def attend_stage(core, masks, masks_in, v_all, scratch, kv_heads, ones, window, w_out, w_out_in, b_out, out, also, tag):
    nc = core.nc
    guard = ones is not None
    PARTS = Split.PARTS
    PAIRS = PARTS ** 2
    ROWS = PAIRS * HD
    KROWS = ROWS + (PARTS if guard else 0)
    SCALE = HD ** -0.5
    KT = T // P
    G = GROUP
    GPB = HEADS // G
    GROUPS = NB * GPB
    VH = 1 if kv_heads < HEADS else G
    RING = 4
    STACK = 2 * PARTS * 16
    SUBS = 1 if window else G
    EXPS = KT * SUBS
    WIDE = P + window if window else T
    PROBS = 4 if window else 2
    TURN_SLOT = 3 if window else 2 if guard else 3
    COPIES = 1 if guard else 2
    LEAD = 2
    O_BANK, MAX_BANK = 4, 6
    T_BANK = O_BANK if guard else 6
    assert not (guard and window) and (not window or 2 * WIDE <= CH)

    units = [(hh, qt, lo, min(lo + CH, (qt + 1) * P)) for hh in range(G) for qt in range(KT) for lo in range(0, (qt + 1) * P, CH)] if guard else []
    UNITS = len(units)
    MAXES = 2 * KT
    MAX_STEPS = 2 * PARTS + 1
    FIRST = G - 1
    upto = [max(0, slot + 1 - FIRST) * UNITS // (EXPS - FIRST) for slot in range(EXPS)]
    AHEAD_BANKS = (6, 7, 0, 1, 2, 3)
    TURN_AT = len(AHEAD_BANKS) - 1

    def max_bank(n, u):
        if isinstance(n, int) and n < LEAD:
            return AHEAD_BANKS[(LEAD * UNITS - 1 - (n * UNITS + u)) % len(AHEAD_BANKS)], len(AHEAD_BANKS)
        return MAX_BANK + (u + 1) % 2, 2

    def score_banks(m):
        kt = m // SUBS
        if window or guard or kt == 0:
            return (2 * (m % 2), 2 * (m % 2) + 1)
        if kt * P < CH:
            first = (0, 2, T_BANK)[(m - SUBS) % 3]
            return (first, first + 1)
        ring = (0, 1, 2, 3, T_BANK, T_BANK + 1)
        return (ring[m % len(ring)],)

    def freed(m):
        earlier = max(e for e in range(m - EXPS, m) if set(score_banks(e % EXPS)) & set(score_banks(m)))
        return earlier + 1

    T_FIRST = min((m for m in range(EXPS) if T_BANK in score_banks(m)), default=None)

    def unit_range(slot):
        return range(upto[slot - 1] if slot else 0, upto[slot])

    def spans(lo, hi):
        return [(a, b) for a, b in ((lo, min(hi, CH)), (max(lo, CH), hi)) if a < b]

    def reach(eng, sem, count):
        if not isinstance(count, int) or count > 0:
            eng.wait_ge(sem, count)

    def groups(eng, step):
        lead = LEAD if guard else 0
        step(0, True)
        with eng.Fori(1, GROUPS - lead) as n:
            step(n, True)
        for n in range(GROUPS - lead, GROUPS):
            step(n, False)

    with ExitStack() as ctx:
        qs = core.sb(ctx, tag + "qs", [KROWS, RING, G, T], BF16)
        ks = core.sb(ctx, tag + "ks", [KROWS, RING, VH, T], BF16)
        vslot = core.sb(ctx, tag + "vslot", [P, KT, VH, 32])
        probs = core.sb(ctx, tag + "probs", [P, PROBS, G, WIDE])
        o = core.sb(ctx, tag + "o", [P, T])
        otok = core.sb(ctx, tag + "otok", [P, NT, D])
        sums = core.sb(ctx, tag + "sums", [P, KT, G])
        most = core.sb(ctx, tag + "most", [P, G, MAXES])
        least = core.sb(ctx, tag + "least", [P, G, KT])
        rest = core.sb(ctx, tag + "rest", [G * KT, 2, P])
        most_parts = core.sb(ctx, tag + "most_parts", [G * KT, PARTS, P], BF16)
        stack_in = core.sem(ctx, tag + "stack_in")
        started = core.sem(ctx, tag + "started")
        set_up = core.sem(ctx, tag + "set_up")
        ones_in = core.sem(ctx, tag + "ones_in")
        max_pe = core.sem(ctx, tag + "max_pe")
        max_read = core.sem(ctx, tag + "max_read")
        max_turned = core.sem(ctx, tag + "max_turned")
        max_step = core.sem(ctx, tag + "max_step")
        max_in = core.sem(ctx, tag + "max_in")
        vslot_ready = core.sem(ctx, tag + "vslot_ready")
        score_pe = core.sem(ctx, tag + "score_pe")
        probs_ready = core.sem(ctx, tag + "probs_ready")
        pv_pe = core.sem(ctx, tag + "pv_pe")
        o_copied = core.sem(ctx, tag + "o_copied")
        o_turned = core.sem(ctx, tag + "o_turned")
        sums_ready = core.sem(ctx, tag + "sums_ready")
        o_ready = core.sem(ctx, tag + "o_ready")
        oT_pe = core.sem(ctx, tag + "oT_pe")
        oT_ready = core.sem(ctx, tag + "oT_ready")
        y_pe = core.sem(ctx, tag + "y_pe")
        also_added = core.sem(ctx, tag + "also_added")
        y_added = core.sem(ctx, tag + "y_added")
        block = core.block(ctx)

        def flat(bank):
            return core.psum[:, bank:bank + 2, :].rearrange("p b c -> p (b c)")

        def scored(m):
            banks = score_banks(m)
            return (flat(banks[0]), 0) if len(banks) == 2 else (core.psum[:, banks[0], :], CH)

        def mask(name):
            a, n = MASK_COLS[name]
            return masks[:, a:a + n]

        def stack(tile, rows, n, head, lo, hi):
            return tile[0:rows, bass.ds(n % RING, 1), head, lo:hi].rearrange("r o t -> r (o t)")

        def copy_o(eng, n, half=None):
            eng.wait_ge(pv_pe, n * KT + (KT // 2 if half == 0 else KT))
            reach(eng, o_turned, n)
            if guard:
                ins = eng.activation(o[:, :], flat(O_BANK), ACT.Copy)
            else:
                ins = eng.tensor_copy(o[:, half * CH:(half + 1) * CH], flat(O_BANK)[:, half * CH:(half + 1) * CH])
            ins.then_inc(o_copied, 1)

        @block.sync
        def _(sp):
            def place(n):
                return n % RING if isinstance(n, int) else sp.snap(n % RING)

            def load(n, slot):
                batch, head = n // GPB, n % GPB
                def at(tile, i):
                    return tile[i * PARTS * HD:(i + 1) * PARTS * HD, bass.ds(slot, 1), :, :].rearrange("r o h t -> r (o h t)")

                for i in range(PARTS):
                    q = scratch[0][i].rearrange("b r t -> (b r) t")[bass.ds(n * (G * HD), G * HD), :].rearrange("(d h) t -> d (h t)", h=G)
                    sp.dma_start(at(qs, i), q.unsqueeze(0).broadcast_to([PARTS, HD, G * T])).then_inc(stack_in, 16)
                    k = scratch[1].rearrange("p b (g d h) t -> p d (b g) (h t)", d=HD, h=G)
                    if VH > 1:
                        k = k[:, :, bass.ds(n, 1), :].rearrange("p d o f -> p d (o f)")
                    else:
                        k = k[:, :, bass.ds(batch, 1), bass.ds(head * T, T)].rearrange("p d o f -> p d (o f)")
                    sp.dma_start(at(ks, i), k).then_inc(stack_in, 16)

            def maximum(n, slot):
                sp.wait_ge(max_step, n * MAX_STEPS + MAX_STEPS)
                for p in range(PARTS):
                    dst = qs[ROWS + p:ROWS + p + 1, bass.ds(slot, 1), :, :].rearrange("r o h (k q) -> r (o h k) q", q=P)
                    sp.dma_start(dst, most_parts[:, p:p + 1, :]).then_inc(max_in, 16)

            load(0, 0)
            if guard:
                sp.wait_ge(started, 1)
                load(1, 1)
                maximum(0, 0)
                sp.wait_ge(started, 2)
                load(2, 2)
                maximum(1, 1)
                sp.wait_ge(started, 3)
                load(3, 3)
                with sp.Fori(1, GROUPS - RING + 1) as n:
                    max_slot, slot = place(n + 1), place(n + 3)
                    maximum(n + 1, max_slot)
                    sp.wait_ge(started, n + 3)
                    load(n + 3, slot)
                for n in range(GROUPS - RING + 2, GROUPS):
                    maximum(n, n % RING)
            else:
                with sp.Fori(1, GROUPS) as n:
                    slot = place(n)
                    sp.wait_ge(started, n)
                    load(n, slot)

        @block.gpsimd
        def _(g):
            s = Steps(g, set_up)
            s.chain(g.memset(vslot[:, :, :, :], 0.0))
            s.chain(g.memset(vslot[:, :, :, HD:HD + 1], 1.0))

            def values_of(n, half):
                at = half * (KT // 2)
                src = v_all[:, bass.ds(n // GPB * KT + at, KT // 2), bass.ds(n % GPB * (VH * HD), VH * HD)].rearrange("p k (h d) -> p k h d", d=HD)
                g.tensor_copy(vslot[:, at:at + KT // 2, :, 0:HD], src).then_inc(vslot_ready, 1)

            for half in range(2):
                values_of(0, half)
            with g.Fori(1, GROUPS) as n:
                for half in range(2):
                    g.wait_ge(pv_pe, n * KT - (0 if half else KT // 2))
                    values_of(n, half)

        @block.tensor
        def _(pe):
            pe.wait_ge(masks_in, 16)

            def max_unit(n, u):
                hh, qt, lo, hi = units[u]
                if u == 0:
                    pe.wait_ge(stack_in, n * STACK + STACK)
                bank, again = max_bank(n, u)
                reach(pe, max_read, n * UNITS + u + 1 - again)
                if u == (TURN_AT if again > 2 else 1):
                    reach(pe, max_step, n * MAX_STEPS - 3)
                s = core.psum[:, bank, :]
                last = hi == (qt + 1) * P
                ins = pe.matmul(s[:, 0:hi - lo], stack(qs, ROWS, n, hh, qt * P, (qt + 1) * P), stack(ks, ROWS, n, hh if VH == G else 0, lo, hi),
                                start=True, stop=not last)
                if u == 0:
                    ins.then_inc(started, 1)
                if last:
                    ins = pe.matmul(s[:, hi - lo - P:hi - lo], mask("ident"), mask("future_key"), start=False, stop=True)
                ins.then_inc(max_pe, 1)

            def max_turn(n):
                pe.wait_ge(max_step, n * MAX_STEPS + 2)
                pe.transpose(core.psum[0:G * KT, MAX_BANK, 0:P], least[:, :, :].rearrange("p h k -> p (h k)"), core.c("ident")).then_inc(max_turned, 1)

            def scores(n, kt, hh):
                m = kt * SUBS + hh
                if m == 0:
                    if guard:
                        pe.wait_ge(max_in, n * (PARTS * 16) + PARTS * 16)
                        if isinstance(n, int) and n == 0:
                            pe.wait_ge(max_read, LEAD * UNITS)
                            pe.wait_ge(ones_in, 16)
                    else:
                        pe.wait_ge(stack_in, n * STACK + STACK)
                reach(pe, probs_ready, n * EXPS + freed(m))
                if window:
                    return band_scores(n, kt)
                if m == T_FIRST and not guard:
                    reach(pe, o_ready, n)
                s, start = scored(m)
                for lo, hi in spans(kt * P, T):
                    ins = pe.matmul(s[:, lo - start:hi - start], stack(ks, KROWS, n, hh if VH == G else 0, kt * P, (kt + 1) * P), stack(qs, KROWS, n, hh, lo, hi),
                                    start=True, stop=lo != kt * P)
                if m == 0 and not guard:
                    ins.then_inc(started, 1)
                pe.matmul(s[:, kt * P - start:(kt + 1) * P - start], mask("ident"), mask("past_query"), start=False, stop=True).then_inc(score_pe, 1)

            def band_scores(n, kt):
                wide = min(T, kt * P + WIDE) - kt * P
                for hh in range(G):
                    bank = core.psum[:, 2 * (kt % 2) + hh // 2, hh % 2 * WIDE:hh % 2 * WIDE + wide]
                    for lo, hi in spans(kt * P, kt * P + wide):
                        ins = pe.matmul(bank[:, lo - kt * P:hi - kt * P], stack(ks, KROWS, n, 0, kt * P, (kt + 1) * P), stack(qs, KROWS, n, hh, lo, hi),
                                        start=hh % 2 == 0 and lo == kt * P, stop=False, skip_group_check=True)
                    if kt == 0 and hh == 0:
                        ins.then_inc(started, 1)
                    ins = pe.matmul(bank, mask("ident"), mask("band")[:, 0:wide], start=False, stop=hh % 2 == 1, skip_group_check=True)
                ins.then_inc(score_pe, 1)

            def values(n, kt, part, parts):
                if part == 0:
                    pe.wait_ge(probs_ready, n * EXPS + (kt + 1) * SUBS)
                    if kt % (KT // 2) == 0:
                        pe.wait_ge(vslot_ready, 2 * n + 1 + kt // (KT // 2))
                    if guard and kt == 0:
                        reach(pe, o_ready, n)
                    elif not guard:
                        last_query = min(T, kt * P + WIDE) - 1
                        if window and kt == 0:
                            reach(pe, o_copied, n * COPIES - 1)
                        elif kt == 0 or window and last_query >= CH > last_query - P:
                            reach(pe, o_copied, n * COPIES)
                first = kt * P if window else 0
                width = (min(T, kt * P + WIDE) - kt * P) // parts
                for lo, hi in spans(kt * P + part * width, kt * P + (part + 1) * width):
                    for hh in range(G):
                        ins = pe.matmul(flat(O_BANK)[32 * hh:32 * hh + 32, lo:hi], vslot[:, kt, hh if VH == G else 0, :],
                                        probs[:, kt % PROBS, hh, lo - first:hi - first],
                                        start=lo % CH == 0 and (kt == 0 or bool(window) and kt * P < lo), stop=kt == KT - 1,
                                        tile_position=(0, 32 * hh), skip_group_check=True)
                if part == parts - 1:
                    ins.then_inc(pv_pe, 1)

            def turn(n):
                pe.wait_ge(o_copied, (n + 1) * COPIES)
                reach(pe, o_ready, n)
                for t in range(KT):
                    ins = pe.transpose(flat(T_BANK)[:, t * P:(t + 1) * P], o[:, t * P:(t + 1) * P], core.c("ident"))
                ins.then_inc(o_turned, 1)

            def step(n, ahead):
                later = not (isinstance(n, int) and n == 0)
                last = isinstance(n, int) and n == GROUPS - 1
                for kt in range(KT):
                    for hh in range(SUBS):
                        slot = kt * SUBS + hh
                        scores(n, kt, hh)
                        mine = list(unit_range(slot)) if ahead and guard else []
                        if window:
                            if kt >= 2:
                                values(n, kt - 2, 0, 1)
                            elif later:
                                values(n - 1, KT - 2 + kt, 0, 1)
                        elif kt:
                            for u in mine[:1]:
                                max_unit(n + LEAD, u)
                            mine = mine[1:]
                            if guard:
                                values(n, kt - 1, hh, SUBS)
                            elif hh:
                                values(n, kt - 1, hh - 1, SUBS)
                            elif kt > 1:
                                values(n, kt - 2, SUBS - 1, SUBS)
                        elif hh == 0 and later:
                            if not guard:
                                values(n - 1, KT - 2, SUBS - 1, SUBS)
                            values(n - 1, KT - 1, 0, 1)
                        if slot == TURN_SLOT and later:
                            turn(n - 1)
                        if slot == 2 and guard and not last:
                            max_turn(n + 1)
                        for u in mine:
                            max_unit(n + LEAD, u)

            if guard:
                for n in range(LEAD):
                    for u in range(UNITS):
                        if n and u == TURN_AT:
                            max_turn(n - 1)
                        max_unit(n, u)
            groups(pe, step)
            if not guard:
                values(GROUPS - 1, KT - 2, SUBS - 1, SUBS)
            values(GROUPS - 1, KT - 1, 0, 1)
            turn(GROUPS - 1)
            pe.wait_ge(w_out_in, 16)
            pe.wait_ge(o_ready, GROUPS)
            for c in range(NC):
                if c >= 2:
                    pe.wait_ge(oT_ready, c - 1)
                for t in range(TPC):
                    ins = pe.transpose(core.psum[:, c % 2, t * P:(t + 1) * P], otok[:, TPC * c + t, :], core.c("ident"))
                ins.then_inc(oT_pe, 1)
            for c in range(NC):
                pe.wait_ge(oT_ready, c + 1)
                if c >= 2:
                    pe.wait_ge(y_added, c - 1)
                for t in range(TPC):
                    dst = core.psum[:, 2 + c % 2, t * P:(t + 1) * P]
                    if b_out is not None:
                        pe.matmul(dst, b_out[0], b_out[1], start=True, stop=False)
                    ins = pe.matmul(dst, core.xnT[:, c * CH + t * P:c * CH + (t + 1) * P], w_out, start=b_out is None, stop=True)
                ins.then_inc(y_pe, 1)

        @block.scalar
        def _(act):
            def step(n, ahead):
                later = not (isinstance(n, int) and n == 0)
                for kt in range(KT):
                    for hh in range(SUBS):
                        m = kt * SUBS + hh
                        if hh == 0:
                            reach(act, pv_pe, n * KT + kt - PROBS + 1)
                        act.wait_ge(score_pe, n * EXPS + m + 1)
                        if window:
                            wide = min(T, kt * P + WIDE) - kt * P
                            src = core.psum[:, 2 * (m % 2):2 * (m % 2) + 2, 0:2 * WIDE].rearrange("p b (h q) -> p b h q", q=WIDE)[:, :, :, 0:wide]
                            dst = probs[:, kt % PROBS, :, 0:wide].rearrange("p (b h) q -> p b h q", b=2)
                        else:
                            s, start = scored(m)
                            src, dst = s[:, kt * P - start:T - start], probs[:, kt % PROBS, hh, kt * P:T]
                        act.activation(dst, src, ACT.Exp, scale=SCALE).then_inc(probs_ready, 1)
                        if m == 0 and later and guard:
                            copy_o(act, n - 1)

            if guard:
                dst = ks[ROWS:KROWS, :, :, :].rearrange("r s h t -> r (s h) t").bitcast(U16)
                act.dma_start(dst, ones.unsqueeze(1).broadcast_to([PARTS, RING * VH, T])).then_inc(ones_in, 16)
            groups(act, step)
            if guard:
                copy_o(act, GROUPS - 1)
            for c in range(NC):
                act.wait_ge(oT_pe, c + 1)
                act.activation(core.xnT[:, c * CH:(c + 1) * CH], core.psum[:, c % 2, :], ACT.Copy).then_inc(oT_ready, 1)

        @block.vector
        def _(v):
            def max_unit(n, u):
                hh, qt, lo, hi = units[u]
                v.wait_ge(max_pe, n * UNITS + u + 1)
                at = qt if lo == 0 else KT + qt
                if u == 0:
                    reach(v, max_step, n * MAX_STEPS - MAX_STEPS + 2)
                v.tensor_reduce(most[:, hh:hh + 1, at], core.psum[:, max_bank(n, u)[0], 0:hi - lo], AX.X, ALU.max).then_inc(max_read, 1)

            def negate(n):
                v.wait_ge(max_read, n * UNITS + UNITS)
                both = KT // 2
                v.tensor_tensor(most[:, :, both:KT], most[:, :, both:KT], most[:, :, KT + both:2 * KT], ALU.max).then_inc(max_step, 1)
                v.wait_ge(max_step, n * MAX_STEPS + 1)
                v.tensor_scalar(least[:, :, :], most[:, :, 0:KT], -1.0, None, ALU.mult).then_inc(max_step, 1)

            def split(n):
                v.wait_ge(max_turned, n + 1)
                reach(v, max_in, n * (PARTS * 16))
                left = core.psum[0:G * KT, MAX_BANK, 0:P]
                for p in range(PARTS):
                    v.tensor_copy(most_parts[:, p, :], left).then_inc(max_step, 1)
                    if p < PARTS - 1:
                        v.wait_ge(max_step, n * MAX_STEPS + 3 + 2 * p)
                        v.tensor_tensor(rest[:, p, :], left, most_parts[:, p, :], ALU.subtract).then_inc(max_step, 1)
                        v.wait_ge(max_step, n * MAX_STEPS + 4 + 2 * p)
                        left = rest[:, p, :]

            def normalise(n):
                v.wait_ge(o_turned, n + 1)
                turned = flat(T_BANK).rearrange("p (t h f) -> p t h f", h=G, f=32)
                v.reciprocal(sums[:, :, :], turned[:, :, :, HD]).then_inc(sums_ready, 1)
                v.wait_ge(sums_ready, n + 1)
                dst = otok[:, bass.ds(n // GPB * KT, KT), bass.ds(n % GPB * (G * HD), G * HD)].rearrange("p t (h d) -> p t h d", d=HD)
                v.tensor_tensor(dst, turned[:, :, :, 0:HD], sums[:, :, :].unsqueeze(3).broadcast_to([P, KT, G, HD]), ALU.mult).then_inc(o_ready, 1)

            def step(n, ahead):
                later = not (isinstance(n, int) and n == 0)
                last = isinstance(n, int) and n == GROUPS - 1
                if later:
                    if not guard:
                        copy_o(v, n - 1, 1)
                    normalise(n - 1)
                if not guard:
                    copy_o(v, n, 0)
                if guard and not last:
                    split(n + 1)
                if guard and ahead:
                    for u in range(UNITS):
                        max_unit(n + LEAD, u)
                    negate(n + LEAD)

            if guard:
                for n in range(LEAD):
                    for u in range(UNITS):
                        if n and u == TURN_AT:
                            split(n - 1)
                        max_unit(n, u)
                    negate(n)
            if also is not None:
                for c in range(NC):
                    tiles = slice(TPC * c, TPC * (c + 1))
                    v.tensor_tensor(out[:, tiles, :], out[:, tiles, :], also[:, tiles, :], ALU.add).then_inc(also_added, 1)
            groups(v, step)
            if not guard:
                copy_o(v, GROUPS - 1, 1)
            normalise(GROUPS - 1)
            if also is not None:
                v.wait_ge(also_added, NC)
            for c in range(NC):
                v.wait_ge(y_pe, c + 1)
                tiles = slice(TPC * c, TPC * (c + 1))
                y = core.psum[:, 2 + c % 2, :].rearrange("p (t d) -> p t d", d=D)
                v.tensor_tensor(out[:, tiles, :], out[:, tiles, :], y, ALU.add).then_inc(y_added, 1)


def channels_stage(core, w4, w4_in, tag):
    nc = core.nc
    SCALE = 1.0 / T ** 0.5
    KT = T // P
    S_BANK, M_BANK = (4, 5), (6, 7)

    def w(name, rows=P):
        a, n = L2A_COLS[name]
        return w4[0:rows, a:a + n]

    with ExitStack() as ctx:
        xr = core.sb(ctx, tag + "xr", [P, NT, D])
        ln = Norm(core, ctx, tag, core.xn, xr)
        qk = core.sb(ctx, tag + "qk", [P, NT, 2, D])
        vT = core.sb(ctx, tag + "vT", [P, N])
        prob = core.sb(ctx, tag + "prob", [P, NB, D])
        mixed = core.sb(ctx, tag + "mixed", [P, NB, D])
        most = core.sb(ctx, tag + "most", [P, NB])
        total = core.sb(ctx, tag + "total", [P, NB])
        qk_pe = core.sem(ctx, tag + "qk_pe")
        qk_ready = core.sem(ctx, tag + "qk_ready")
        v_pe = core.sem(ctx, tag + "v_pe")
        v_ready = core.sem(ctx, tag + "v_ready")
        score_pe = core.sem(ctx, tag + "score_pe")
        dve_step = core.sem(ctx, tag + "dve_step")
        most_ready = core.sem(ctx, tag + "most_ready")
        exps = core.sem(ctx, tag + "exps")
        prob_ready = core.sem(ctx, tag + "prob_ready")
        mixed_pe = core.sem(ctx, tag + "mixed_pe")
        mixed_ready = core.sem(ctx, tag + "mixed_ready")
        y_pe = core.sem(ctx, tag + "y_pe")
        y_added = core.sem(ctx, tag + "y_added")
        block = core.block(ctx)

        @block.gpsimd
        def _(g):
            ln.pool(g)

        @block.tensor
        def _(pe):
            pe.wait_ge(w4_in, 16)

            def score(t):
                pe.wait_ge(qk_ready, t + 1)
                ins = pe.matmul(core.psum[:, S_BANK[t // KT], 0:D], qk[:, t, 0, :], qk[:, t, 1, :], start=t % KT == 0, stop=t % KT == KT - 1)
                if t % KT == KT - 1:
                    ins.then_inc(score_pe, 1)

            ln.tensor(pe, 0)
            for c in range(NC):
                if c + 1 < NC:
                    ln.tensor(pe, c + 1)
                pe.wait_ge(ln.xnT_ready, c + 1)
                if c >= 2:
                    pe.wait_ge(v_ready, c - 1)
                pe.matmul(core.psum[:, 2 + c % 2, :], w("vT"), core.xnT[:, c * CH:(c + 1) * CH], start=True, stop=True).then_inc(v_pe, 1)
                for t in range(TPC * c, TPC * (c + 1)):
                    if t >= 2:
                        pe.wait_ge(qk_ready, t - 1)
                    dst = core.psum[:, t % 2, 0:2 * D]
                    pe.matmul(dst, core.xnT[:, t * P:(t + 1) * P], w("qkT"), start=True, stop=True).then_inc(qk_pe, 1)
                    if t:
                        score(t - 1)
            score(NT - 1)
            for b in range(NB):
                pe.wait_ge(prob_ready, b + 1)
                pe.matmul(core.psum[:, M_BANK[b], 0:D], prob[:, b, :], w("projT"), start=True, stop=True).then_inc(mixed_pe, 1)
            for c in range(NC):
                b = c // (NC // NB)
                pe.wait_ge(mixed_ready, b + 1)
                pe.wait_ge(v_ready, c + 1)
                if c >= 2:
                    pe.wait_ge(y_added, c - 1)
                for t in range(TPC):
                    dst = core.psum[:, c % 2, t * P:(t + 1) * P]
                    ins = pe.matmul(dst, vT[:, c * CH + t * P:c * CH + (t + 1) * P], mixed[:, b, :], start=True, stop=True)
                ins.then_inc(y_pe, 1)

        @block.scalar
        def _(act):
            act.wait_ge(w4_in, 16)
            for c in range(NC):
                ln.scalar(act, c, gain=w("norm_w"), bias=w("norm_b"))
                act.wait_ge(v_pe, c + 1)
                act.activation(vT[:, c * CH:(c + 1) * CH], core.psum[:, 2 + c % 2, :], ACT.Identity, bias=w("v_b")).then_inc(v_ready, 1)
            for b in range(NB):
                act.wait_ge(most_ready, b + 1)
                act.activation(prob[:, b, :], core.psum[:, S_BANK[b], 0:D], ACT.Exp, bias=most[:, b:b + 1], scale=SCALE,
                               accum_out=total[:, b:b + 1]).then_inc(exps, 1)
            for b in range(NB):
                act.wait_ge(mixed_pe, b + 1)
                act.activation(mixed[:, b, :], core.psum[:, M_BANK[b], 0:D], ACT.Copy).then_inc(mixed_ready, 1)

        @block.vector
        def _(v):
            v.wait_ge(w4_in, 16)
            s = Steps(v, dve_step)
            ln.vector(v)
            for t in range(NT):
                v.wait_ge(qk_pe, t + 1)
                v.tensor_tensor(qk[:, t, :, :].rearrange("p i d -> p (i d)"), core.psum[:, t % 2, 0:2 * D], w("qk_b"), ALU.add).then_inc(qk_ready, 1)
            for b in range(NB):
                v.wait_ge(score_pe, b + 1)
                s.chain(v.tensor_reduce(most[:, b:b + 1], core.psum[:, S_BANK[b], 0:D], AX.X, ALU.max))
                v.tensor_scalar(most[:, b:b + 1], most[:, b:b + 1], -SCALE, None, ALU.mult).then_inc(most_ready, 1)
            added = []
            for c in range(NC):
                tiles = slice(TPC * c, TPC * (c + 1))
                s.chain(v.tensor_tensor(core.x[:, tiles, :], core.x[:, tiles, :], core.xn[:, tiles, :], ALU.add))
                proj_b = w("proj_b").unsqueeze(1).broadcast_to([P, TPC, D])
                added.append(s.did(v.tensor_tensor(core.x[:, tiles, :], core.x[:, tiles, :], proj_b, ALU.add)))
            for b in range(NB):
                v.wait_ge(exps, b + 1)
                s.chain(v.reciprocal(total[:, b:b + 1], total[:, b:b + 1]))
                v.tensor_scalar(prob[:, b, :], prob[:, b, :], total[:, b:b + 1], None, ALU.mult).then_inc(prob_ready, 1)
            for c in range(NC):
                tiles = slice(TPC * c, TPC * (c + 1))
                v.wait_ge(y_pe, c + 1)
                s.after(added[c])
                v.tensor_tensor(core.x[:, tiles, :], core.x[:, tiles, :], core.psum[:, c % 2, :].rearrange("p (t d) -> p t d", d=D), ALU.add).then_inc(y_added, 1)


def top4_stage(core, w5, w5_in, masks, select, select_in, dram_experts, tag):
    nc = core.nc
    E, TOP, CAPACITY = 32, 4, 4 * N * 4 // 32
    PAIRS = E // 2
    SLOTS = 2
    STEPS = SLOTS * NC
    PARTS = 3
    G_BANK, U_BANK, C_BANK = 4, 5, 6
    SHARED_G, SHARED_U = (4, 6), (5, 7)
    LOGITS, WITHIN, TOTALS = 3, 3, 2
    TURN = (6, 7)

    with ExitStack() as ctx:
        ln = LayerNorm(core, ctx, tag)
        logit = core.sb(ctx, tag + "logit", [P, NT, E])
        prob = core.sb(ctx, tag + "prob", [P, NT, E])
        above = core.sb(ctx, tag + "above", [P, NT, E])
        equal = core.sb(ctx, tag + "equal", [P, NT, E])
        inside = core.sb(ctx, tag + "inside", [P, NT, E])
        inside_t = core.sb(ctx, tag + "inside_t", [P, E, NT])
        order = core.sb(ctx, tag + "order", [P, NT, E])
        served = core.sb(ctx, tag + "served", [P, E, NT])
        top = core.sb(ctx, tag + "top", [P, NT, 8])
        total = core.sb(ctx, tag + "total", [P, NT])
        places = core.sb(ctx, tag + "places", [P, NT])
        factor = core.sb(ctx, tag + "factor", [P, NT, E])
        split = core.sb(ctx, tag + "split", [P, NT, P // E, E], BF16)
        parts = core.sb(ctx, tag + "parts", [PARTS * E, N], BF16)
        slot = [core.sb(ctx, f"{tag}slot{s}", [P, 3, P]) for s in range(SLOTS + 1)]
        silu = core.sb(ctx, tag + "silu", [P, 2, CH])
        prod = core.sb(ctx, tag + "prod", [P, 2, CH])
        hid = core.sb(ctx, tag + "hid", [P, 2, CH])
        logits_pe = core.sem(ctx, tag + "logits_pe")
        set_up = core.sem(ctx, tag + "set_up")
        dve_step = core.sem(ctx, tag + "dve_step")
        shifted = core.sem(ctx, tag + "shifted")
        exps = core.sem(ctx, tag + "exps")
        chosen = core.sem(ctx, tag + "chosen")
        ranks_pe = core.sem(ctx, tag + "ranks_pe")
        ranks_read = core.sem(ctx, tag + "ranks_read")
        split_ready = core.sem(ctx, tag + "split_ready")
        turn_pe = core.sem(ctx, tag + "turn_pe")
        part_ready = core.sem(ctx, tag + "part_ready")
        slot_in = [core.sem(ctx, f"{tag}slot_in{s}") for s in range(SLOTS + 1)]
        slot_free = [core.sem(ctx, f"{tag}slot_free{s}") for s in range(SLOTS)]
        gate_pe = core.sem(ctx, tag + "gate_pe")
        up_pe = core.sem(ctx, tag + "up_pe")
        factor_pe = core.sem(ctx, tag + "factor_pe")
        silu_ready = core.sem(ctx, tag + "silu_ready")
        prod_ready = core.sem(ctx, tag + "prod_ready")
        hid_ready = core.sem(ctx, tag + "hid_ready")
        down_pe = core.sem(ctx, tag + "down_pe")
        block = core.block(ctx)

        @block.gpsimd
        def _(g):
            g.memset(inside[:, :, :], 1.0).then_inc(set_up, 1)
            g.memset(inside_t[:, :, :], 1.0).then_inc(set_up, 1)
            g.wait_ge(set_up, 2)
            g.memset(inside[:, :, 0:1], 0.0).then_inc(set_up, 1)
            g.memset(inside_t[:, :, 0:1], 0.0).then_inc(set_up, 1)
            g.memset(split[:, :, PARTS:P // E, :], 0.0).then_inc(set_up, 1)
            ln.pool(g)

        @block.sync
        def _(sp):
            for s in range(SLOTS):
                sp.sem_inc(slot_free[s], 1)
            sp.dma_start(slot[SLOTS][:, :, :], dram_experts[PAIRS]).then_inc(slot_in[SLOTS], 16)
            with sp.Fori(0, PAIRS // SLOTS) as i:
                for s in range(SLOTS):
                    sp.wait_ge(slot_free[s], i + 1)
                    sp.dma_start(slot[s][:, :, :], dram_experts[bass.ds(i * SLOTS + s, 1), :, :, :].rearrange("e p j d -> (e p) j d")).then_inc(slot_in[s], 16)

        @block.scalar
        def _(act):
            for c in range(NC):
                ln.scalar(act, c)
            act.wait_ge(shifted, 1)
            act.activation(prob[:, :, :], logit[:, :, :], ACT.Exp).then_inc(exps, 1)

            def silus(n, buf, bank):
                act.wait_ge(gate_pe, n + 1)
                act.activation(silu[:, buf, :], core.psum[:, bank, :], ACT.Silu).then_inc(silu_ready, 1)

            for c in range(NC):
                if c >= 2:
                    act.wait_ge(hid_ready, c - 1)
                silus(c, c % 2, SHARED_G[c % 2])
            for c in range(NC):
                act.wait_ge(turn_pe, c + 1)
                act.activation(parts[:, c * CH:(c + 1) * CH], core.psum[0:PARTS * E, TURN[c % 2], :], ACT.Copy).then_inc(part_ready, 1)
            with act.Fori(0, PAIRS // SLOTS) as i:
                for k in range(STEPS):
                    n = i * STEPS + NC + k
                    act.wait_ge(prod_ready, i * STEPS + NC + k - 1)
                    silus(n, k % 2, G_BANK)

        @block.tensor
        def _(pe):
            pe.wait_ge(w5_in, 16)
            pe.wait_ge(select_in, 16)
            wa, wn = L3_COLS["router"]

            def logits(c):
                pe.wait_ge(ln.xnT_ready, c + 1)
                for t in range(TPC * c, TPC * (c + 1)):
                    ins = pe.matmul(core.psum[:, LOGITS, t * E:(t + 1) * E], core.xnT[:, t * P:(t + 1) * P], w5[:, wa:wa + wn], start=True, stop=True)
                if c == NC - 1:
                    ins.then_inc(logits_pe, 1)

            for c in range(NC):
                ln.tensor(pe, c)
                if c:
                    logits(c - 1)
            logits(NC - 1)

            def shared_up(c):
                xc = core.xnT[:, c * CH:(c + 1) * CH]
                if c >= 2:
                    pe.wait_ge(silu_ready, c - 1)
                pe.matmul(core.psum[:, SHARED_G[c % 2], :], shared[:, 0, :], xc, start=True, stop=True).then_inc(gate_pe, 1)
                if c >= 2:
                    pe.wait_ge(hid_ready, c - 1)
                pe.matmul(core.psum[:, SHARED_U[c % 2], :], shared[:, 1, :], xc, start=True, stop=True).then_inc(up_pe, 1)

            def ranks():
                pe.wait_ge(chosen, 1)
                picks = above[:, :, :].rearrange("p t e -> p e t")
                pe.matmul(core.psum[:, WITHIN, :], core.c("earlier"), picks, start=True, stop=True)
                pe.matmul(core.psum[:, TOTALS, :], core.c("ones"), picks, start=True, stop=True).then_inc(ranks_pe, 1)

            def turn():
                pe.wait_ge(split_ready, 1)
                pe.wait_ge(hid_ready, NC)
                a, n = MASK_COLS["ident"]
                for c in range(NC):
                    if c >= 2:
                        pe.wait_ge(part_ready, c - 1)
                    for t in range(TPC):
                        ins = pe.matmul(core.psum[:, TURN[c % 2], t * P:(t + 1) * P],
                                        split[:, c * TPC + t, :, :].rearrange("p s e -> p (s e)"), masks[:, a:a + n], start=True, stop=True)
                    ins.then_inc(turn_pe, 1)

            def up(n, sl, c, pair):
                xc = core.xnT[:, c * CH:(c + 1) * CH]
                pe.wait_ge(silu_ready, n)
                pe.matmul(core.psum[:, G_BANK, :], sl[:, 0, :], xc, start=True, stop=True).then_inc(gate_pe, 1)
                pe.wait_ge(prod_ready, n)
                pe.matmul(core.psum[:, U_BANK, :], sl[:, 1, :], xc, start=True, stop=True).then_inc(up_pe, 1)
                pe.wait_ge(hid_ready, n)
                pe.matmul(core.psum[:, C_BANK, :], select[:, bass.ds(pair * P, P)], parts[:, c * CH:(c + 1) * CH],
                          start=True, stop=True).then_inc(factor_pe, 1)

            def down(n, buf, sl, c, first=False):
                pe.wait_ge(hid_ready, n + 1)
                for t in range(TPC):
                    ins = pe.matmul(core.psum[:, c, t * P:(t + 1) * P], hid[:, buf, t * P:(t + 1) * P], sl[:, 2, :],
                                    start=first and t == 0, stop=False, skip_group_check=True)
                ins.then_inc(down_pe, 1)

            shared = slot[SLOTS]
            def shared_down(c):
                down(c, c % 2, shared, c, True)

            pe.wait_ge(slot_in[SLOTS], 16)
            shared_up(0)
            shared_up(1)
            shared_down(0)
            shared_up(2)
            ranks()
            shared_down(1)
            shared_up(3)
            turn()
            pe.wait_ge(ranks_read, 1)
            shared_down(2)
            shared_down(3)
            pe.wait_ge(part_ready, NC)
            with pe.Fori(0, PAIRS // SLOTS) as i:
                def at(k):
                    s, c = divmod(k, NC)
                    return i * STEPS + NC + k, s, c

                def drop(k):
                    n, s, c = at(k)
                    down(n, k % 2, slot[s], c)
                    if c == NC - 1:
                        pe.wait_ge(down_pe, n + 1)
                        pe.sem_inc(slot_free[s], 1)

                for k in range(STEPS):
                    n, s, c = at(k)
                    if c == 0:
                        pe.wait_ge(slot_in[s], i * 16 + 16)
                    up(n, slot[s], c, i * SLOTS + s)
                    if k:
                        drop(k - 1)
                drop(STEPS - 1)

        @block.vector
        def _(v):
            s = Steps(v, dve_step)
            ln.vector(v)
            v.wait_ge(logits_pe, 1)
            lp = core.psum[:, LOGITS, :].rearrange("p (t e) -> p t e", e=E)

            def wide(a):
                return a.unsqueeze(2).broadcast_to([P, NT, E])

            for t in range(NT):
                last = s.did(v.max(top[:, t, :], lp[:, t, :]))
            s.after(last)
            v.tensor_tensor(logit[:, :, :], lp, wide(top[:, :, 0]), ALU.subtract).then_inc(shifted, 1)

            def shared_multiply(c):
                v.wait_ge(silu_ready, c + 1)
                v.wait_ge(up_pe, c + 1)
                if c >= 2:
                    v.wait_ge(down_pe, c - 1)
                v.tensor_tensor(hid[:, c % 2, :], silu[:, c % 2, :], core.psum[:, SHARED_U[c % 2], :], ALU.mult).then_inc(hid_ready, 1)

            fourth = wide(top[:, :, TOP - 1])
            s.did(v.tensor_tensor(equal[:, :, :], lp, fourth, ALU.is_equal))
            s.chain(v.tensor_tensor(above[:, :, :], lp, fourth, ALU.is_gt))
            s.chain(v.tensor_reduce(places[:, :], above[:, :, :], AX.X, ALU.add))
            s.chain(v.tensor_scalar(places[:, :], places[:, :], -1.0, float(TOP), ALU.mult, ALU.add))
            v.wait_ge(set_up, 5)

            def flat(a):
                return a[:, :, :].rearrange("p a b -> p (a b)")

            s.chain(v.tensor_tensor_scan(flat(order), flat(inside), flat(equal), 0.0, ALU.mult, ALU.add))
            s.chain(v.tensor_tensor(order[:, :, :], order[:, :, :], wide(places[:, :]), ALU.is_le))
            s.chain(v.tensor_tensor(equal[:, :, :], equal[:, :, :], order[:, :, :], ALU.mult))
            v.tensor_tensor(above[:, :, :], above[:, :, :], equal[:, :, :], ALU.add).then_inc(chosen, 1)
            shared_multiply(0)
            v.wait_ge(exps, 1)
            s.chain(v.tensor_reduce(total[:, :], prob[:, :, :], AX.X, ALU.add))
            s.chain(v.reciprocal(total[:, :], total[:, :]))
            s.chain(v.tensor_tensor(prob[:, :, :], prob[:, :, :], wide(total[:, :]), ALU.mult))
            v.wait_ge(chosen, 1)
            s.chain(v.tensor_tensor(prob[:, :, :], prob[:, :, :], above[:, :, :], ALU.mult))
            shared_multiply(1)
            v.wait_ge(ranks_pe, 1)
            in_tile = core.psum[:, TOTALS, :]
            s.chain(v.tensor_tensor_scan(flat(served), flat(inside_t), in_tile, 0.0, ALU.mult, ALU.add))
            s.chain(v.tensor_tensor(flat(served), flat(served), in_tile, ALU.subtract))
            v.tensor_tensor(flat(served), flat(served), core.psum[:, WITHIN, :], ALU.add).then_inc(ranks_read, 1)
            v.wait_ge(ranks_read, 1)
            s.chain(v.scalar_tensor_tensor(factor[:, :, :], served[:, :, :].rearrange("p e t -> p t e"), float(CAPACITY), prob[:, :, :], ALU.is_lt, ALU.mult))
            shared_multiply(2)
            for p in range(PARTS):
                ins = v.tensor_copy(split[:, :, p, :], factor[:, :, :])
                if p < PARTS - 1:
                    s.chain(ins)
                    s.chain(v.tensor_tensor(factor[:, :, :], factor[:, :, :], split[:, :, p, :], ALU.subtract))
                else:
                    ins.then_inc(split_ready, 1)
            shared_multiply(3)
            v.wait_ge(hid_ready, NC)
            v.sem_inc(prod_ready, NC)

            def multiply(n, k):
                v.wait_ge(silu_ready, n + 1)
                v.wait_ge(up_pe, n + 1)
                v.tensor_tensor(prod[:, k % 2, :], silu[:, k % 2, :], core.psum[:, U_BANK, :], ALU.mult).then_inc(prod_ready, 1)
                v.wait_ge(prod_ready, n + 1)
                v.wait_ge(down_pe, n - 1)
                v.wait_ge(factor_pe, n - NC + 1)
                v.tensor_tensor(hid[:, k % 2, :], prod[:, k % 2, :], core.psum[:, C_BANK, :], ALU.mult).then_inc(hid_ready, 1)

            with v.Fori(0, PAIRS // SLOTS) as i:
                for k in range(STEPS):
                    multiply(i * STEPS + NC + k, k)
            for c in range(NC):
                v.wait_ge(down_pe, NC + PAIRS * NC - (NC - 1 - c))
                xs = core.x[:, TPC * c:TPC * (c + 1), :].rearrange("p t d -> p (t d)")
                s.did(v.scalar_tensor_tensor(xs, core.psum[:, c, :], 0.5, xs, ALU.mult, ALU.add))


def gqa_project_stage(core, w5, w5_in, v_all, scratch, kind, tag):
    nc = core.nc
    EPS = 1e-6
    KV = 4
    QK = D + KV * HD
    VW = KV * HD
    LATENT = 32

    def w(name, rows=P):
        a, n = L3_COLS[name]
        return w5[0:rows, a:a + n]

    with ExitStack() as ctx:
        xr = core.sb(ctx, tag + "xr", [P, NT, D])
        ln = Norm(core, ctx, tag, core.xn, xr, rms=True, eps=EPS)
        sp_ = Split(core, ctx, tag, (P, VW), scratch)
        latent = core.sb(ctx, tag + "latent", [LATENT, N])
        cosed = core.sb(ctx, tag + "cosed", [P, TPC, QK])
        sined = core.sb(ctx, tag + "sined", [P, TPC, QK])
        heads = core.sb(ctx, tag + "heads", [P, 2, TPC, QK])
        square = core.sb(ctx, tag + "squares", [P, TPC, QK])
        HN = QK // HD
        mean = core.sb(ctx, tag + "mean", [P, TPC, HN])
        root = core.sb(ctx, tag + "root", [P, TPC, HN])
        slope = core.sb(ctx, tag + "slope", [P, TPC, HN])
        latent_pe = core.sem(ctx, tag + "latent_pe")
        latent_ready = core.sem(ctx, tag + "latent_ready")
        qkv_pe = core.sem(ctx, tag + "qkv_pe")
        v_ready = core.sem(ctx, tag + "v_ready")
        cos_step = core.sem(ctx, tag + "cos_step")
        dve_step = core.sem(ctx, tag + "dve_step")
        mean_ready = core.sem(ctx, tag + "mean_ready")
        root_ready = core.sem(ctx, tag + "root_ready")
        heads_ready = core.sem(ctx, tag + "heads_ready")
        block = core.block(ctx)
        QKV_BANK, T_BANK = (0, 1, 2, 3), (4, 5)
        LAT_BANK = T_BANK
        turned = [core.psum[0:n, bank, :] for n, bank in zip((D, VW), T_BANK)]

        @block.gpsimd
        def _(g):
            ln.pool(g)

        @block.sync
        def _(sp):
            for c in range(NC):
                for i in range(2):
                    sp_.sync(sp, c, i)
            sp_.landed(sp)

        @block.tensor
        def _(pe):
            pe.wait_ge(w5_in, 16)
            for c in range(NC):
                ln.tensor(pe, c)
            if kind == "g":
                for c in range(NC):
                    pe.wait_ge(ln.xnT_ready, c + 1)
                    if c >= 2:
                        pe.wait_ge(latent_ready, c - 1)
                    pe.matmul(core.psum[0:LATENT, LAT_BANK[c % 2], :], w("g_down"), core.xnT[:, c * CH:(c + 1) * CH],
                              start=True, stop=True).then_inc(latent_pe, 1)

            def turn(c):
                pe.wait_ge(heads_ready, c + 1)
                if c:
                    sp_.read(pe, c - 1)
                for i, (a, n) in enumerate(((0, D), (D, VW))):
                    for t in range(TPC):
                        ins = pe.transpose(core.psum[0:n, T_BANK[i], t * P:(t + 1) * P], heads[:, c % 2, t, a:a + n], core.c("ident"))
                    ins.then_inc(sp_.heads_pe, 1)

            for t in range(NT):
                if t >= TPC:
                    pe.wait_ge(cos_step, 2 * (t - TPC + 1))
                    pe.wait_ge(v_ready, t - TPC + 1)
                pe.wait_ge(ln.xnT_ready, t // TPC + 1)
                xt = core.xnT[:, t * P:(t + 1) * P]
                bank = core.psum[:, QKV_BANK[t % TPC], :]
                if kind == "l":
                    ins = pe.matmul(bank[:, 0:2 * QK + VW], xt, w("l_qkv"), start=True, stop=True)
                else:
                    pe.wait_ge(latent_ready, t // TPC + 1)
                    lt = latent[:, t * P:(t + 1) * P]
                    pe.matmul(bank[:, 0:D], xt, w("g_q"), start=True, stop=True)
                    pe.matmul(bank[:, QK:QK + D], xt, w("g_qr"), start=True, stop=True)
                    pe.matmul(bank[:, D:QK], lt, w("g_k", LATENT), start=True, stop=True)
                    ins = pe.matmul(bank[:, QK + D:2 * QK + VW], lt, w("g_krv", LATENT), start=True, stop=True)
                ins.then_inc(qkv_pe, 1)
                if t % TPC == TPC - 1 and t > TPC:
                    turn(t // TPC - 1)
            turn(NC - 1)

        @block.scalar
        def _(act):
            act.wait_ge(w5_in, 16)
            for c in range(NC):
                ln.scalar(act, c, gain=w("norm1" if kind == "g" else "norm2"))
            if kind == "g":
                for c in range(NC):
                    act.wait_ge(latent_pe, c + 1)
                    act.activation(latent[:, c * CH:(c + 1) * CH], core.psum[0:LATENT, LAT_BANK[c % 2], :], ACT.Copy).then_inc(latent_ready, 1)
            for t in range(NT):
                act.wait_ge(cos_step, 2 * (t + 1))
                act.activation(v_all[:, t, :], core.psum[:, QKV_BANK[t % TPC], 2 * QK:2 * QK + VW], ACT.Copy).then_inc(v_ready, 1)
                if t % TPC == TPC - 1:
                    act.wait_ge(mean_ready, t // TPC + 1)
                    act.activation(root[:, :, :], mean[:, :, :], ACT.Sqrt).then_inc(root_ready, 1)
                if t % TPC == 2 and t > TPC:
                    sp_.scalar(act, t // TPC - 1, turned)
            sp_.scalar(act, NC - 1, turned)

        @block.vector
        def _(v):
            v.wait_ge(w5_in, 16)
            s = Steps(v, dve_step)
            ln.vector(v)

            def table(name, t):
                a, n = L3_COLS[kind + name]
                tab = w5[:, a + (t % (T // P)) * HD:a + (t % (T // P)) * HD + HD]
                return tab.unsqueeze(1).unsqueeze(3).broadcast_to([P, HN // GROUP, HD, GROUP])

            def grouped(a):
                return a.rearrange("p (g d h) -> p g d h", d=HD, h=GROUP)

            def by_head(a):
                return a.rearrange("p t (g d h) -> p (t g) h d", d=HD, h=GROUP)

            def per_head(a):
                return a.rearrange("p t (g h) -> p (t g) h", h=GROUP)

            def split(c):
                v.wait_ge(sp_.heads_pe, 2 * c + 2)
                sp_.vector(v, c, turned)

            for c in range(NC):
                for k in range(TPC):
                    t = c * TPC + k
                    ps = core.psum[:, QKV_BANK[t % TPC], :]
                    v.wait_ge(qkv_pe, t + 1)
                    if c:
                        v.wait_ge(dve_step, 8 * c)
                    for dst, a, name in ((cosed, 0, "cos"), (sined, QK, "sin")):
                        v.tensor_tensor(grouped(dst[:, k, :]), grouped(ps[:, a:a + QK]), table(name, t), ALU.mult).then_inc(cos_step, 1)
                    if k == TPC - 1 and c:
                        split(c - 1)
                hc = heads[:, c % 2, :, :]
                v.wait_ge(cos_step, 2 * TPC * (c + 1))
                s.chain(v.tensor_tensor(hc, cosed[:, :, :], sined[:, :, :], ALU.add))
                s.chain(v.tensor_tensor(square[:, :, :], hc, hc, ALU.mult))
                s.chain(v.tensor_reduce(per_head(mean[:, :, :]), by_head(square[:, :, :]), AX.X, ALU.add))
                v.tensor_scalar(mean[:, :, :], mean[:, :, :], 1.0 / HD, EPS, ALU.mult, ALU.add).then_inc(mean_ready, 1)
                v.wait_ge(root_ready, c + 1)
                s.chain(v.reciprocal(root[:, :, :], root[:, :, :]))
                s.chain(v.tensor_tensor(slope[:, :, :], root[:, :, :], root[:, :, :], ALU.mult))
                s.chain(v.tensor_tensor(slope[:, :, :], slope[:, :, :], mean[:, :, :], ALU.mult))
                s.chain(v.tensor_scalar(slope[:, :, :], slope[:, :, :], -0.5, 1.5, ALU.mult, ALU.add))
                s.chain(v.tensor_tensor(root[:, :, :], root[:, :, :], slope[:, :, :], ALU.mult))
                h4 = hc.rearrange("p t (g d h) -> p (t g) d h", d=HD, h=GROUP)
                v.tensor_tensor(h4, h4, per_head(root[:, :, :]).unsqueeze(2).broadcast_to([P, TPC * HN // GROUP, HD, GROUP]), ALU.mult).then_inc(heads_ready, 1)
            split(NC - 1)


def store_stage(core, dram_out, loads):
    nc = core.nc
    with ExitStack() as ctx:
        stored = core.sem(ctx, "stored")
        block = core.block(ctx)

        @block.sync
        def _(sp):
            sp.dma_start(dram_out.rearrange("(t p) d -> p t d", p=P), core.x[:, :, :]).then_inc(stored, 16)
            sp.wait_ge(stored, 16)
            for _, _, sem in loads:
                sp.wait_ge(sem, 16)


def build(nc, dram, dram_out):
    with ExitStack() as ctx:
        core = Core(nc, ctx)
        w0 = core.sb(ctx, "w0", [P, L0_W])
        w1 = core.sb(ctx, "w1", [P, 8])
        w2 = core.sb(ctx, "w2", [P, L2_W])
        w3 = core.sb(ctx, "w3", [P, L1_W])
        w4 = core.sb(ctx, "w4", [P, L2A_W])
        w5 = core.sb(ctx, "w5", [P, L3_W])
        select = core.sb(ctx, "select", [96, 16 * P], BF16)
        masks = core.sb(ctx, "masks", [P, MASK_W], BF16)
        w0_in, w1_in, w2_in, w3_in, w4_in, w5_in, masks_in, select_in = (
            core.weight_sem(ctx, f"{n}_in") for n in ("w0", "w1", "w2", "w3", "w4", "w5", "masks", "select"))
        scattered = core.weight_sem(ctx, "scattered")
        gathered = [core.weight_sem(ctx, f"gathered{t}") for t in range(NT)]
        loads = [(w0[:, :], "w0", w0_in), (w1[:, :], "w1", w1_in), (w3[:, :], "w3", w3_in), (masks[:, :].bitcast(U16), "masks", masks_in),
                 (w2[:, :], "w2", w2_in), (w4[:, :], "w4", w4_in), (w5[:, :], "w5", w5_in), (select[:, :].bitcast(U16), "select", select_in)]
        scratch = [nc.dram_tensor(f"scratch_{n}", (Split.PARTS, NB, P, T), BF16, kind="Internal").ap() for n in "qk"]
        scratch3 = [scratch[0], nc.dram_tensor("scratch_k3", (Split.PARTS, NB, 4 * HD, T), BF16, kind="Internal").ap()]

        def part(tile, cols):
            def of(name, rows=P):
                a, n = cols[name]
                return tile[0:rows, a:a + n]
            return of

        w3_, w5_ = part(w3, L1_COLS), part(w5, L3_COLS)
        BLOCKS = N // P + 6
        sorted_x = nc.dram_tensor("sorted_x", ((BLOCKS + 1) * P, D), F32, kind="Internal").ap()
        sorted_y = nc.dram_tensor("sorted_y", (BLOCKS * P, D), F32, kind="Internal").ap()
        cleared = core.weight_sem(ctx, "cleared")
        load_stage(core, dram, loads, sorted_x, cleared)
        coupling_stage(core, w0, w0_in, "c1_")
        scan_stage(core, w0, "s_")
        coupling_stage(core, w0, w0_in, "c2_")
        top1_stage(core, w1, w1_in, dram["experts1"], sorted_x, sorted_y, cleared, scattered, gathered, 0, "m1_")
        with ExitStack() as actx:
            v_all = core.sb(actx, "a1_v_all", [P, NT, D])
            rope_project_stage(core, w3, w3_in, v_all, scratch, "p1_")
            attend_stage(core, masks, masks_in, v_all, scratch, HEADS, dram["ones"], 0, w3_("o"), w3_in, (w3_("ones", 1), w3_("o_b", 1)), core.x, None, "a1_")
        top1_stage(core, w1, w1_in, dram["experts1"], sorted_x, sorted_y, cleared, scattered, gathered, 1, "m2_")
        mlp_stage(core, w2, w2_in, "f1_")
        norm_stage(core, "n1_")
        channels_stage(core, w4, w4_in, "h_")
        mlp_stage(core, w2, w2_in, "f2_")
        top4_stage(core, w5, w5_in, masks, select, select_in, dram["experts3"], "t1_")
        norm_stage(core, "n2_")
        for kind in "gl":
            with ExitStack() as actx:
                v_all = core.sb(actx, kind + "_v_all", [P, NT, 32])
                gqa_project_stage(core, w5, w5_in, v_all, scratch3, kind, kind + "p_")
                if kind == "g":
                    attend_stage(core, masks, masks_in, v_all, scratch3, 4, None, 0, w5_("g_o"), w5_in, None, core.xn, None, "ga_")
                else:
                    attend_stage(core, masks, masks_in, v_all, scratch3, 4, None, 32, w5_("l_o"), w5_in, None, core.x, core.xn, "la_")
        top4_stage(core, w5, w5_in, masks, select, select_in, dram["experts3"], "t2_")
        store_stage(core, dram_out, loads)



def packed(cols, width, parts):
    out = np.zeros((P, width), np.float32)
    for name, a in parts.items():
        at, w = cols[name]
        a = np.asarray(a)
        if a.ndim == 1:
            a = a[:, None] if w == 1 else np.broadcast_to(a[None, :], (P, w))
        out[:a.shape[0], at:at + a.shape[1]] = a
    return out


def bfloat16_bits(constants):
    return np.ascontiguousarray(constants, dtype=np.float32).view(np.uint16)[:, 1::2]


def laid_out(i):
    eye = np.eye(P, dtype=np.float32)
    q = P // 4
    twist = np.zeros((P, P), np.float32)
    for dst, src, sign in ((0, 2, 1), (1, 3, -1), (2, 0, -1), (3, 1, 1)):
        twist[src * q:(src + 1) * q, dst * q:(dst + 1) * q] = sign * np.eye(q)
    i = {k: np.asarray(v) for k, v in i.items()}

    def rep(v, n=P):
        return np.broadcast_to(v.reshape(1, -1), (n, v.size))

    a = {"x": i["L0_attn_x"].reshape(N, D)}
    a["const"] = packed(CONST_COLS, CONST_W, {
        "ident": eye, "twist": twist, "first8": np.broadcast_to(np.arange(8, 0, -1, dtype=np.float32), (P, 8)),
        "earlier": np.triu(np.ones((P, P)), 1), "ones": np.ones((P, P)), "block_start": P * np.broadcast_to(np.arange(NT + 8), (P, NT + 8))})
    a["w0"] = packed(L0_COLS, L0_W, {
        "cn_w1": i["L0_ffn_cn_w1"], "cn_w2": i["L0_ffn_cn_w2"], "cn_w3": i["L0_ffn_cn_w3"],
        "cn_w4": np.broadcast_to(i["L0_ffn_cn_w4"], (32, P)),
        "gc_w1": i["L0_ffn_gc_w1"], "gc_w2": i["L0_ffn_gc_w2"], "gc_w3": np.broadcast_to(i["L0_ffn_gc_w3"], (32, P)),
        "cn_b1": i["L0_ffn_cn_b1"], "cn_b2": i["L0_ffn_cn_b2"], "cn_b3": i["L0_ffn_cn_b3"], "cn_b4": rep(i["L0_ffn_cn_b4"]),
        "gc_b1": i["L0_ffn_gc_b1"], "gc_b2": i["L0_ffn_gc_b2"], "gc_b3": rep(i["L0_ffn_gc_b3"]),
        "range": rep(i["L0_ffn_adaptive_range"]), "B_wT": i["L0_attn_B_w"].T, "C_wT": i["L0_attn_C_w"].T,
        "C_b": rep(i["L0_attn_C_b"]), "log_A": i["L0_attn_log_A"], "B_b": i["L0_attn_B_b"]})
    def hidden(w, shared):
        both = np.concatenate([w, shared[None]])
        return both.reshape(8, P, 4, P)

    down = np.concatenate([i["L1_ffn_down_w"], i["L1_ffn_shared_down_w"][None]]).reshape(8, 4, P, P).transpose(0, 2, 1, 3)
    a["experts1"] = np.concatenate([hidden(i["L1_ffn_gate_w"], i["L1_ffn_shared_gate_w"]),
                                    hidden(i["L1_ffn_up_w"], i["L1_ffn_shared_up_w"]), down], axis=2)
    a["w1"] = i["L1_ffn_router_w"]

    def half_turned(wT):
        return np.roll(wT.reshape(-1, HEADS, HD), HD // 2, axis=2).reshape(wT.shape)

    def rope_tables(base, interleaved):
        f32 = np.float32
        inv = f32(1.0) / np.power(f32(base), np.arange(0, HD, 2, dtype=f32) / f32(HD))
        angle = np.arange(T, dtype=f32)[:, None] * inv[None, :].astype(f32)
        cos, sin = np.cos(angle), np.sin(angle)
        if interleaved:
            both = [np.stack(z, axis=-1).reshape(T, HD) for z in ((cos, cos), (-sin, sin))]
        else:
            both = [np.concatenate(z, axis=-1) for z in ((cos, cos), (-sin, sin))]
        return [z.reshape(T // P, P, HD).transpose(1, 0, 2).reshape(P, -1) for z in both]

    cos, sin = rope_tables(10000.0, False)
    def grouped(w):
        return w.reshape(w.shape[0], -1, GROUP, HD).swapaxes(2, 3).reshape(w.shape)

    wq, wk, wv, wo = (i[f"L1_attn_W{n}"].T for n in "qkvo")
    bq, bk = i["L1_attn_bq"][None], i["L1_attn_bk"][None]
    a["w3"] = packed(L1_COLS, L1_W, {
        "qk": np.concatenate([grouped(z) for z in (wq, wk, half_turned(wq), half_turned(wk))], axis=1),
        "qk_b": np.concatenate([grouped(z)[0] for z in (bq, bk, half_turned(bq), half_turned(bk))]),
        "v": wv, "v_b": i["L1_attn_bv"], "o": wo, "o_b": i["L1_attn_bo"][None], "ones": np.ones((1, P), np.float32), "cos": cos, "sin": sin})
    p, f = np.arange(P)[:, None], np.arange(P + 32)[None, :]
    NEVER = -1e30
    a["masks"] = bfloat16_bits(packed(MASK_COLS, MASK_W, {
        "ident": eye, "future_key": np.where(f[:, :P] > p, NEVER, 0), "past_query": np.where(f[:, :P] < p, NEVER, 0),
        "band": np.where((f >= p) & (f - p < 32), 0, NEVER)}))

    a["ones"] = bfloat16_bits(np.ones((Split.PARTS, T)))

    def tiles(wT):
        return wT.reshape(-1, P, wT.shape[1]).transpose(1, 0, 2).reshape(P, -1)

    E3 = 32
    cols = lambda z: z.reshape(E3 // 2, 2, P, 64).transpose(0, 2, 1, 3).reshape(E3 // 2, P, P)
    pairs = np.stack([cols(i["L3_ffn_W1"]), cols(i["L3_ffn_W3"]), i["L3_ffn_W2"].reshape(E3 // 2, P, D)], axis=2)
    shared = np.stack([i["L3_ffn_Ws1"], i["L3_ffn_Ws3"], i["L3_ffn_Ws2"]], axis=1)[None]
    a["experts3"] = np.concatenate([pairs, shared])
    e, col = np.arange(3 * E3)[:, None] % E3, np.arange(E3 // 2 * P)[None, :]
    a["select"] = bfloat16_bits(e == 2 * (col // P) + col % P // 64)

    def turned(z):
        return z.reshape(z.shape[0], -1, 2)[:, :, ::-1].reshape(z.shape)

    gk, gv, gq, lq, lk = i["L3_attn_g_k_up"], i["L3_attn_g_v_up"], i["L3_attn_g_wq"], i["L3_attn_l_wq"], i["L3_attn_l_wk"]
    (gcos, gsin), (lcos, lsin) = rope_tables(1000000.0, True), rope_tables(10000.0, True)
    a["w5"] = packed(L3_COLS, L3_W, {
        "router": i["L3_ffn_Wg"], "g_q": grouped(gq), "g_qr": grouped(turned(gq)), "g_down": i["L3_attn_g_kv_down"],
        "g_k": grouped(gk), "g_krv": np.concatenate([grouped(turned(gk)), gv], axis=1), "g_o": i["L3_attn_g_wo"],
        "l_qkv": np.concatenate([grouped(lq), grouped(lk), grouped(turned(lq)), grouped(turned(lk)), i["L3_attn_l_wv"]], axis=1), "l_o": i["L3_attn_l_wo"],
        "gcos": gcos, "gsin": gsin, "lcos": lcos, "lsin": lsin, "norm1": i["L3_attn_norm1_w"], "norm2": i["L3_attn_norm2_w"]})
    qkvT, qkv_b = i["L2_attn_qkv_w"].T, i["L2_attn_qkv_b"]
    a["w4"] = packed(L2A_COLS, L2A_W, {
        "qkT": qkvT[:, :256], "vT": qkvT[:, 256:], "projT": i["L2_attn_proj_w"].T, "qk_b": qkv_b[:256], "proj_b": i["L2_attn_proj_b"],
        "v_b": qkv_b[256:], "norm_w": i["L2_attn_norm_w"], "norm_b": i["L2_attn_norm_b"]})

    def per_tile(s):
        return s.reshape(-1, P).T

    a["w2"] = packed(L2_COLS, L2_W, {
        "w1T": i["L2_ffn_w1_w"].T, "w2T": i["L2_ffn_w2_w"].T, "h1T": tiles(i["L2_ffn_h1_w"].T), "h2T": tiles(i["L2_ffn_h2_w"].T),
        "w3T": tiles(i["L2_ffn_w3_w"].T), "s3": rep(i["L2_ffn_w3_s"]), "s1": per_tile(i["L2_ffn_w1_s"]), "s2": per_tile(i["L2_ffn_w2_s"]),
        "sh1": per_tile(i["L2_ffn_h1_s"]), "sh2": per_tile(i["L2_ffn_h2_s"])})
    return {k: np.ascontiguousarray(v) for k, v in a.items()}


def kernel(**inputs):
    import concourse.bacc as bacc
    from concourse.bass_utils import run_bass_kernel_spmd

    arrays = {f"{k}_dram": v for k, v in laid_out(inputs).items()}
    nc = bacc.Bacc("TRN2", target_bir_lowering=False, num_devices=1)
    dram = {k[:-5]: nc.dram_tensor(k, v.shape, mybir.dt.from_np(v.dtype), kind="ExternalInput").ap() for k, v in arrays.items()}
    out = nc.dram_tensor("out_dram", (NB, T, D), F32, kind="ExternalOutput").ap()
    build(nc, dram, out.rearrange("b t d -> (b t) d"))
    r = run_bass_kernel_spmd(nc, [arrays], core_ids=[0])
    return r.results[0]["out_dram"]
```
